# Optimizing a Trainium2 kernel written in Bass

```python
import numpy as np
import jax
import jax.numpy as jnp

def _softmax(x, axis=-1):
    return jax.nn.softmax(x, axis=axis)

def _gelu(x):
    return jax.nn.gelu(x, approximate=True)

def _silu(x):
    return jax.nn.silu(x)

def _sigmoid(x):
    return jax.nn.sigmoid(x)

def _layernorm(x, axis=-1, eps=1e-05):
    m = jnp.mean(x, axis=axis, keepdims=True)
    v = jnp.var(x, axis=axis, keepdims=True)
    return (x - m) / jnp.sqrt(v + eps)

def _scatter_add(tgt, idx, src, axis=0):
    return tgt.at[idx].add(src)

def _segment_sum(src, seg, n):
    return jax.ops.segment_sum(src, seg, n)
kernel_name = 'mk_vit_tower_cls_d4_tok_img256_r4_0cebb8'

def setup_inputs(seed: int=0):
    np.random.seed(seed)
    _w = jnp.asarray

    def _rec_inputs():
        import jax
        import jax.numpy as jnp
        _rk = jax.random.key(seed)
        x = -7.10856e-05 + 0.999911 * jax.random.normal(jax.random.fold_in(_rk, 1), (8, 64, 128, 64), jnp.float32)
        cls_tok = 0.02 * jax.random.normal(jax.random.fold_in(_rk, 5), (1, 1, 64), jnp.float32)
        return (x, cls_tok)
    x, cls_tok = _rec_inputs()

    def _L0_tok_setup():
        import jax, jax.numpy as jnp
        import numpy as np
        PATCH_LEN = 16
        STRIDE = 8
        PAD = 8
        key = jax.random.key(seed)
        k1, k2 = jax.random.split(key)
        x = jax.random.normal(k1, (32, 64, 128, 64), dtype=jnp.float32)
        in_feat = 64 * (PATCH_LEN // 2 + 1) * 2
        W = jax.random.normal(k2, (64, in_feat), dtype=jnp.float32) * 0.02
        return {'x': x, 'W': W}
    _L0_tok_all = _L0_tok_setup()
    _L0_tok_in = {k: v for k, v in _L0_tok_all.items() if k in ('W',)}
    del _L0_tok_all

    def _L0_attn_setup():
        import jax, jax.numpy as jnp
        import numpy as np
        B, L, D = (4, 256, 64)
        N_PER, N_HYP = (48, 16)
        K = N_PER + N_HYP

        def _mlp(x, w1, b1, w2, b2):
            h = jax.nn.gelu(x @ w1.T + b1, approximate=False)
            return h @ w2.T + b2
        key = jax.random.key(seed)
        ks = iter(jax.random.split(key, 32))

        def lin(o, i):
            return jax.random.normal(next(ks), (o, i), jnp.float32) * 0.02

        def bias(o):
            return jnp.zeros((o,), jnp.float32)
        inp = {'x': jax.random.normal(next(ks), (B, L, D), jnp.float32)}
        inp.update(kp_w1=lin(D, D), kp_b1=bias(D), kp_w2=lin(N_PER, D), kp_b2=bias(N_PER))
        inp.update(qp_w1=lin(D, D), qp_b1=bias(D), qp_w2=lin(N_PER, D), qp_b2=bias(N_PER))
        inp.update(kh_w1=lin(D, D), kh_b1=bias(D), kh_w2=lin(2 * N_HYP, D), kh_b2=bias(2 * N_HYP))
        inp.update(qh_w1=lin(D, D), qh_b1=bias(D), qh_w2=lin(2 * N_HYP, D), qh_b2=bias(2 * N_HYP))
        inp.update(v_w=lin(D, D), v_b=bias(D))
        inp.update(ln_g=jnp.ones((D,), jnp.float32), ln_b=jnp.zeros((D,), jnp.float32))
        inp.update(out_w=lin(D, D), out_b=bias(D))
        return inp
    _L0_attn_all = _L0_attn_setup()
    _L0_attn_in = {k: v for k, v in _L0_attn_all.items() if k in ('kp_w1', 'kp_b1', 'kp_w2', 'kp_b2', 'qp_w1', 'qp_b1', 'qp_w2', 'qp_b2', 'kh_w1', 'kh_b1', 'kh_w2', 'kh_b2', 'qh_w1', 'qh_b1', 'qh_w2', 'qh_b2', 'v_w', 'v_b', 'ln_g', 'ln_b', 'out_w', 'out_b')}
    del _L0_attn_all

    def _L0_ffn_setup():
        import jax, jax.numpy as jnp
        import numpy as np
        B, T, C = (64, 96, 64)
        NH, NKV = (4, 2)
        HD = C // NH
        NREP = NH // NKV
        NE, TOPK = (8, 2)
        HID = int(8 / 3 * C)
        EPS_RMS = 1e-06

        def _rope_tables(t_len):
            inv_freq = 1.0 / 10000.0 ** (np.arange(0, HD, 2, dtype=np.float32) / HD)
            t = np.arange(t_len, dtype=np.float32)
            freqs = np.outer(t, inv_freq)
            emb = np.concatenate([freqs, freqs], axis=-1)
            return (jnp.asarray(np.cos(emb)), jnp.asarray(np.sin(emb)))

        def _rotate_half(x):
            h = x.shape[-1] // 2
            return jnp.concatenate([-x[..., h:], x[..., :h]], axis=-1)

        def _rmsnorm(v, w):
            return v * jax.lax.rsqrt(jnp.mean(v * v, axis=-1, keepdims=True) + EPS_RMS) * w
        key = jax.random.key(seed)
        ks = jax.random.split(key, 10)
        s = lambda k, shape: jax.random.normal(k, shape, jnp.float32) * 0.02
        return {'x': jax.random.normal(ks[0], (B, T, C), jnp.float32), 'ln1_w': jnp.ones((C,), jnp.float32), 'ln2_w': jnp.ones((C,), jnp.float32), 'wq': s(ks[1], (NH * HD, C)), 'wk': s(ks[2], (NKV * HD, C)), 'wv': s(ks[3], (NKV * HD, C)), 'wo': s(ks[4], (C, C)), 'router_w': s(ks[5], (NE, C)), 'w1': s(ks[6], (NE, HID, C)), 'w2': s(ks[7], (NE, C, HID)), 'w3': s(ks[8], (NE, HID, C))}
    _L0_ffn_all = _L0_ffn_setup()
    _L0_ffn_in = {k: v for k, v in _L0_ffn_all.items() if k in ('ln1_w', 'ln2_w', 'wq', 'wk', 'wv', 'wo', 'router_w', 'w1', 'w2', 'w3')}
    del _L0_ffn_all

    def _L1_attn_setup():
        import jax, jax.numpy as jnp
        import numpy as np
        D_MODEL, D_INNER, D_STATE, K = (64, 128, 16, 4)

        def _depthwise_causal_conv(xp, conv_w, conv_b):
            xt = jnp.transpose(xp, (0, 2, 1))
            out = jax.lax.conv_general_dilated(xt, conv_w, window_strides=(1,), padding=[(K - 1, 0)], dimension_numbers=('NCH', 'OIH', 'NCH'), feature_group_count=D_INNER)
            out = out + conv_b[None, :, None]
            return jnp.transpose(out, (0, 2, 1))
        key = jax.random.key(seed)
        ks = jax.random.split(key, 10)
        s = 0.02
        x = jax.random.normal(ks[0], (8, 512, D_MODEL), dtype=jnp.float32)
        W_in = s * jax.random.normal(ks[1], (D_MODEL, 2 * D_INNER), dtype=jnp.float32)
        conv_w = s * jax.random.normal(ks[2], (D_INNER, 1, K), dtype=jnp.float32)
        conv_b = s * jax.random.normal(ks[3], (D_INNER,), dtype=jnp.float32)
        W_xproj = s * jax.random.normal(ks[4], (D_INNER, 1 + 2 * D_STATE), dtype=jnp.float32)
        w_dt = s * jax.random.normal(ks[5], (D_INNER,), dtype=jnp.float32)
        b_dt = s * jax.random.normal(ks[6], (D_INNER,), dtype=jnp.float32)
        A = -jax.random.uniform(ks[7], (D_INNER, D_STATE), dtype=jnp.float32, minval=0.5, maxval=2.0)
        D = s * jax.random.normal(ks[8], (D_INNER,), dtype=jnp.float32)
        W_out = s * jax.random.normal(ks[9], (D_INNER, D_MODEL), dtype=jnp.float32)
        return {'x': x, 'W_in': W_in, 'conv_w': conv_w, 'conv_b': conv_b, 'W_xproj': W_xproj, 'w_dt': w_dt, 'b_dt': b_dt, 'A': A, 'D': D, 'W_out': W_out}
    _L1_attn_all = _L1_attn_setup()
    _L1_attn_in = {k: v for k, v in _L1_attn_all.items() if k in ('W_in', 'conv_w', 'conv_b', 'W_xproj', 'w_dt', 'b_dt', 'A', 'D', 'W_out')}
    del _L1_attn_all

    def _L1_ffn_setup():
        import jax, jax.numpy as jnp
        import numpy as np
        DIM = 64
        HEADS = 8
        NUM_KEYS = 64
        NUM_KV = NUM_KEYS ** 2
        PK_TOPK = 16
        FINAL_TOPK = 16
        DIM_KEY = DIM // 2
        P = 2

        def _pk(x, Wq_pk, pk_keys):
            b, n, _ = x.shape
            q = (x @ Wq_pk).reshape(b, n, P, HEADS, DIM_KEY).transpose(2, 0, 1, 3, 4)
            sim = jnp.einsum('pbnhd,pkhd->pbnhk', q, pk_keys)
            scores, idx = jax.lax.top_k(sim, PK_TOPK)
            idx0 = idx[0]
            idx1 = idx[1] * NUM_KEYS
            index = (idx0[..., :, None] + idx1[..., None, :]).reshape(b, n, HEADS, PK_TOPK * PK_TOPK)
            score = (scores[0][..., :, None] + scores[1][..., None, :]).reshape(b, n, HEADS, PK_TOPK * PK_TOPK)
            final_scores, pk_idx = jax.lax.top_k(score, FINAL_TOPK)
            final_indices = jnp.take_along_axis(index, pk_idx, axis=-1)
            final_scores = jax.nn.softmax(final_scores, axis=-1)
            return (final_scores, final_indices)
        key = jax.random.key(seed)
        ks = jax.random.split(key, 7)
        b, n = (2, 256)
        std = 0.02
        x = jax.random.normal(ks[0], (b, n, DIM), dtype=jnp.float32)
        Wq_pk = jax.random.normal(ks[1], (DIM, P * HEADS * DIM_KEY), dtype=jnp.float32) * std
        pk_keys = jax.random.normal(ks[2], (P, NUM_KEYS, HEADS, DIM_KEY), dtype=jnp.float32) * std
        Wq = jax.random.normal(ks[3], (DIM, HEADS * DIM), dtype=jnp.float32) * std
        keys_table = jax.random.normal(ks[4], (NUM_KV * HEADS, DIM), dtype=jnp.float32) * std
        values_table = jax.random.normal(ks[5], (NUM_KV * HEADS, DIM), dtype=jnp.float32) * std
        Wo = jax.random.normal(ks[6], (DIM * HEADS, DIM), dtype=jnp.float32) * std
        return {'x': x, 'Wq_pk': Wq_pk, 'pk_keys': pk_keys, 'Wq': Wq, 'keys_table': keys_table, 'values_table': values_table, 'Wo': Wo}
    _L1_ffn_all = _L1_ffn_setup()
    _L1_ffn_in = {k: v for k, v in _L1_ffn_all.items() if k in ('Wq_pk', 'pk_keys', 'Wq', 'keys_table', 'values_table', 'Wo')}
    del _L1_ffn_all

    def _L2_attn_setup():
        import jax, jax.numpy as jnp
        import numpy as np
        B, T, C, H, G = (8, 2048, 64, 8, 64)
        D = C // H
        key = jax.random.key(seed)
        ks = jax.random.split(key, 16)
        s = 0.02
        return {'x_q': jax.random.normal(ks[0], (B, T, C), jnp.float32), 'x_r': jax.random.normal(ks[1], (B, T, C), jnp.float32), 'y': jax.random.normal(ks[2], (B, T, C), jnp.float32), 'W_in': jax.random.normal(ks[3], (C, C), jnp.float32) * s, 'b_in': jnp.zeros((C,), jnp.float32), 'W_slice': jax.random.normal(ks[4], (D, G), jnp.float32) * s, 'b_slice': jnp.zeros((G,), jnp.float32), 'temperature': jnp.ones((1, H, 1, 1), jnp.float32) / np.float32(np.sqrt(D)), 'W_q': jax.random.normal(ks[5], (D, D), jnp.float32) * s, 'b_q': jnp.zeros((D,), jnp.float32), 'W_k': jax.random.normal(ks[6], (D, D), jnp.float32) * s, 'b_k': jnp.zeros((D,), jnp.float32), 'W_v': jax.random.normal(ks[7], (D, D), jnp.float32) * s, 'b_v': jnp.zeros((D,), jnp.float32), 'W_out': jax.random.normal(ks[8], (C, C), jnp.float32) * s, 'b_out': jnp.zeros((C,), jnp.float32)}
    _L2_attn_all = _L2_attn_setup()
    _L2_attn_in = {k: v for k, v in _L2_attn_all.items() if k in ('x_r', 'y', 'W_in', 'b_in', 'W_slice', 'b_slice', 'temperature', 'W_q', 'b_q', 'W_k', 'b_k', 'W_v', 'b_v', 'W_out', 'b_out')}
    del _L2_attn_all

    def _L2_ffn_setup():
        import jax, jax.numpy as jnp
        import numpy as np
        NUM_EXPERTS = 8
        TOP_K = 2
        B, S, D = (8, 2048, 64)

        def _moe(tokens, router_w, w1, b1, w2, b2):
            N = tokens.shape[0]
            E = router_w.shape[0]
            logits = tokens.astype(jnp.float32) @ router_w.astype(jnp.float32).T
            probs = jax.nn.softmax(logits, axis=-1)
            rw, re = jax.lax.top_k(probs, TOP_K)
            if TOP_K > 1:
                rw = rw / jnp.maximum(rw.sum(-1, keepdims=True), 1e-12)
            rw = rw.astype(tokens.dtype)
            combine = jnp.zeros((N, E), tokens.dtype).at[jnp.arange(N)[:, None], re].set(rw)
            out = tokens
            for e in range(E):
                h = jax.nn.gelu(tokens @ w1[e] + b1[e], approximate=False)
                y = h @ w2[e] + b2[e]
                out = out + combine[:, e:e + 1] * y
            return out
        key = jax.random.key(seed)
        ks = jax.random.split(key, 4)
        scale = 1.0 / np.sqrt(D).astype(np.float32)
        return {'input_embeddings': jax.random.normal(ks[0], (B, S, D), jnp.float32), 'router_w': jax.random.normal(ks[1], (NUM_EXPERTS, D), jnp.float32) * scale, 'w1': jax.random.normal(ks[2], (NUM_EXPERTS, D, D), jnp.float32) * scale, 'b1': jnp.zeros((NUM_EXPERTS, D), jnp.float32), 'w2': jax.random.normal(ks[3], (NUM_EXPERTS, D, D), jnp.float32) * scale, 'b2': jnp.zeros((NUM_EXPERTS, D), jnp.float32)}
    _L2_ffn_all = _L2_ffn_setup()
    _L2_ffn_in = {k: v for k, v in _L2_ffn_all.items() if k in ('router_w', 'w1', 'b1', 'w2', 'b2')}
    del _L2_ffn_all

    def _L3_attn_setup():
        import jax, jax.numpy as jnp
        import numpy as np
        SEQ, BATCH, IN, HID = (512, 64, 64, 64)
        key = jax.random.key(seed)
        k1, k2, k3, k4, k5 = jax.random.split(key, 5)
        s = 1.0 / np.sqrt(HID)
        return {'x_in': jax.random.normal(k1, (SEQ, BATCH, IN), dtype=jnp.float32), 'W_ih': jax.random.uniform(k2, (HID, IN), jnp.float32, -s, s), 'W_hh': jax.random.uniform(k3, (HID, HID), jnp.float32, -s, s), 'b_ih': jax.random.uniform(k4, (HID,), jnp.float32, -s, s), 'b_hh': jax.random.uniform(k5, (HID,), jnp.float32, -s, s)}
    _L3_attn_all = _L3_attn_setup()
    _L3_attn_in = {k: v for k, v in _L3_attn_all.items() if k in ('W_ih', 'W_hh', 'b_ih', 'b_hh')}
    del _L3_attn_all

    def _L3_ffn_setup():
        import jax, jax.numpy as jnp
        import numpy as np
        C = 64
        HID = 256
        E = 8
        TEMP = 1.0
        key = jax.random.key(seed)
        ks = jax.random.split(key, 7)
        x = jax.random.normal(ks[0], (8, 4096, C), dtype=jnp.float32)
        W1 = jax.random.normal(ks[1], (C, HID), dtype=jnp.float32) * 0.02
        b1 = jnp.zeros((HID,), dtype=jnp.float32)
        Wg = jax.random.normal(ks[2], (HID, E), dtype=jnp.float32) * 0.02
        bg = jnp.zeros((E,), dtype=jnp.float32)
        Wd = jax.random.normal(ks[3], (E, HID, C), dtype=jnp.float32) * 0.02
        bd = jnp.zeros((E, C), dtype=jnp.float32)
        return {'x': x, 'W1': W1, 'b1': b1, 'Wg': Wg, 'bg': bg, 'Wd': Wd, 'bd': bd}
    _L3_ffn_all = _L3_ffn_setup()
    _L3_ffn_in = {k: v for k, v in _L3_ffn_all.items() if k in ('W1', 'b1', 'Wg', 'bg', 'Wd', 'bd')}
    del _L3_ffn_all
    return {'x': x, 'cls_tok': cls_tok, 'L0_tok_W': _L0_tok_in['W'], 'L0_attn_kp_w1': _L0_attn_in['kp_w1'], 'L0_attn_kp_b1': _L0_attn_in['kp_b1'], 'L0_attn_kp_w2': _L0_attn_in['kp_w2'], 'L0_attn_kp_b2': _L0_attn_in['kp_b2'], 'L0_attn_qp_w1': _L0_attn_in['qp_w1'], 'L0_attn_qp_b1': _L0_attn_in['qp_b1'], 'L0_attn_qp_w2': _L0_attn_in['qp_w2'], 'L0_attn_qp_b2': _L0_attn_in['qp_b2'], 'L0_attn_kh_w1': _L0_attn_in['kh_w1'], 'L0_attn_kh_b1': _L0_attn_in['kh_b1'], 'L0_attn_kh_w2': _L0_attn_in['kh_w2'], 'L0_attn_kh_b2': _L0_attn_in['kh_b2'], 'L0_attn_qh_w1': _L0_attn_in['qh_w1'], 'L0_attn_qh_b1': _L0_attn_in['qh_b1'], 'L0_attn_qh_w2': _L0_attn_in['qh_w2'], 'L0_attn_qh_b2': _L0_attn_in['qh_b2'], 'L0_attn_v_w': _L0_attn_in['v_w'], 'L0_attn_v_b': _L0_attn_in['v_b'], 'L0_attn_ln_g': _L0_attn_in['ln_g'], 'L0_attn_ln_b': _L0_attn_in['ln_b'], 'L0_attn_out_w': _L0_attn_in['out_w'], 'L0_attn_out_b': _L0_attn_in['out_b'], 'L0_ffn_ln1_w': _L0_ffn_in['ln1_w'], 'L0_ffn_ln2_w': _L0_ffn_in['ln2_w'], 'L0_ffn_wq': _L0_ffn_in['wq'], 'L0_ffn_wk': _L0_ffn_in['wk'], 'L0_ffn_wv': _L0_ffn_in['wv'], 'L0_ffn_wo': _L0_ffn_in['wo'], 'L0_ffn_router_w': _L0_ffn_in['router_w'], 'L0_ffn_w1': _L0_ffn_in['w1'], 'L0_ffn_w2': _L0_ffn_in['w2'], 'L0_ffn_w3': _L0_ffn_in['w3'], 'L1_attn_W_in': _L1_attn_in['W_in'], 'L1_attn_conv_w': _L1_attn_in['conv_w'], 'L1_attn_conv_b': _L1_attn_in['conv_b'], 'L1_attn_W_xproj': _L1_attn_in['W_xproj'], 'L1_attn_w_dt': _L1_attn_in['w_dt'], 'L1_attn_b_dt': _L1_attn_in['b_dt'], 'L1_attn_A': _L1_attn_in['A'], 'L1_attn_D': _L1_attn_in['D'], 'L1_attn_W_out': _L1_attn_in['W_out'], 'L1_ffn_Wq_pk': _L1_ffn_in['Wq_pk'], 'L1_ffn_pk_keys': _L1_ffn_in['pk_keys'], 'L1_ffn_Wq': _L1_ffn_in['Wq'], 'L1_ffn_keys_table': _L1_ffn_in['keys_table'], 'L1_ffn_values_table': _L1_ffn_in['values_table'], 'L1_ffn_Wo': _L1_ffn_in['Wo'], 'L2_attn_x_r': _L2_attn_in['x_r'], 'L2_attn_y': _L2_attn_in['y'], 'L2_attn_W_in': _L2_attn_in['W_in'], 'L2_attn_b_in': _L2_attn_in['b_in'], 'L2_attn_W_slice': _L2_attn_in['W_slice'], 'L2_attn_b_slice': _L2_attn_in['b_slice'], 'L2_attn_temperature': _L2_attn_in['temperature'], 'L2_attn_W_q': _L2_attn_in['W_q'], 'L2_attn_b_q': _L2_attn_in['b_q'], 'L2_attn_W_k': _L2_attn_in['W_k'], 'L2_attn_b_k': _L2_attn_in['b_k'], 'L2_attn_W_v': _L2_attn_in['W_v'], 'L2_attn_b_v': _L2_attn_in['b_v'], 'L2_attn_W_out': _L2_attn_in['W_out'], 'L2_attn_b_out': _L2_attn_in['b_out'], 'L2_ffn_router_w': _L2_ffn_in['router_w'], 'L2_ffn_w1': _L2_ffn_in['w1'], 'L2_ffn_b1': _L2_ffn_in['b1'], 'L2_ffn_w2': _L2_ffn_in['w2'], 'L2_ffn_b2': _L2_ffn_in['b2'], 'L3_attn_W_ih': _L3_attn_in['W_ih'], 'L3_attn_W_hh': _L3_attn_in['W_hh'], 'L3_attn_b_ih': _L3_attn_in['b_ih'], 'L3_attn_b_hh': _L3_attn_in['b_hh'], 'L3_ffn_W1': _L3_ffn_in['W1'], 'L3_ffn_b1': _L3_ffn_in['b1'], 'L3_ffn_Wg': _L3_ffn_in['Wg'], 'L3_ffn_bg': _L3_ffn_in['bg'], 'L3_ffn_Wd': _L3_ffn_in['Wd'], 'L3_ffn_bd': _L3_ffn_in['bd']}

def reference(x, cls_tok, L0_tok_W, L0_attn_kp_w1, L0_attn_kp_b1, L0_attn_kp_w2, L0_attn_kp_b2, L0_attn_qp_w1, L0_attn_qp_b1, L0_attn_qp_w2, L0_attn_qp_b2, L0_attn_kh_w1, L0_attn_kh_b1, L0_attn_kh_w2, L0_attn_kh_b2, L0_attn_qh_w1, L0_attn_qh_b1, L0_attn_qh_w2, L0_attn_qh_b2, L0_attn_v_w, L0_attn_v_b, L0_attn_ln_g, L0_attn_ln_b, L0_attn_out_w, L0_attn_out_b, L0_ffn_ln1_w, L0_ffn_ln2_w, L0_ffn_wq, L0_ffn_wk, L0_ffn_wv, L0_ffn_wo, L0_ffn_router_w, L0_ffn_w1, L0_ffn_w2, L0_ffn_w3, L1_attn_W_in, L1_attn_conv_w, L1_attn_conv_b, L1_attn_W_xproj, L1_attn_w_dt, L1_attn_b_dt, L1_attn_A, L1_attn_D, L1_attn_W_out, L1_ffn_Wq_pk, L1_ffn_pk_keys, L1_ffn_Wq, L1_ffn_keys_table, L1_ffn_values_table, L1_ffn_Wo, L2_attn_x_r, L2_attn_y, L2_attn_W_in, L2_attn_b_in, L2_attn_W_slice, L2_attn_b_slice, L2_attn_temperature, L2_attn_W_q, L2_attn_b_q, L2_attn_W_k, L2_attn_b_k, L2_attn_W_v, L2_attn_b_v, L2_attn_W_out, L2_attn_b_out, L2_ffn_router_w, L2_ffn_w1, L2_ffn_b1, L2_ffn_w2, L2_ffn_b2, L3_attn_W_ih, L3_attn_W_hh, L3_attn_b_ih, L3_attn_b_hh, L3_ffn_W1, L3_ffn_b1, L3_ffn_Wg, L3_ffn_bg, L3_ffn_Wd, L3_ffn_bd):
    import jax
    import jax.numpy as jnp

    def _L0_tok_ref(x, W):
        import jax, jax.numpy as jnp
        import numpy as np
        PATCH_LEN = 16
        STRIDE = 8
        PAD = 8
        B, C, T, V = x.shape
        xp = jnp.pad(x, ((0, 0), (0, 0), (0, PAD), (0, 0)), mode='edge')
        Tp = T + PAD
        N = (Tp - PATCH_LEN) // STRIDE + 1
        idx = jnp.arange(N)[:, None] * STRIDE + jnp.arange(PATCH_LEN)[None, :]
        patches = xp[:, :, idx, :]
        patches = jnp.transpose(patches, (0, 4, 2, 3, 1))
        xf = jnp.fft.rfft(patches, axis=-2, norm='ortho')
        F = xf.shape[-2]
        x_real = xf.real.reshape(B, V, N, F * C)
        x_imag = xf.imag.reshape(B, V, N, F * C)
        x_emb = jnp.concatenate([x_real, x_imag], axis=-1)
        x_emb = x_emb @ W.T
        return x_emb.reshape(B, V * N, -1)

    def _L0_attn_ref(x, kp_w1, kp_b1, kp_w2, kp_b2, qp_w1, qp_b1, qp_w2, qp_b2, kh_w1, kh_b1, kh_w2, kh_b2, qh_w1, qh_b1, qh_w2, qh_b2, v_w, v_b, ln_g, ln_b, out_w, out_b):
        import jax, jax.numpy as jnp
        import numpy as np
        B, L, D = (4, 256, 64)
        N_PER, N_HYP = (48, 16)
        K = N_PER + N_HYP

        def _mlp(x, w1, b1, w2, b2):
            h = jax.nn.gelu(x @ w1.T + b1, approximate=False)
            return h @ w2.T + b2
        Bx, Lx, Dx = x.shape
        key_p = jnp.tanh(_mlp(x, kp_w1, kp_b1, kp_w2, kp_b2)) * jnp.pi
        query_p = jnp.tanh(_mlp(x, qp_w1, qp_b1, qp_w2, qp_b2)) * jnp.pi
        key_phasor_p = jnp.exp(1j * key_p.astype(jnp.complex64))
        query_phasor_p = jnp.exp(1j * query_p.astype(jnp.complex64))
        key_h = jnp.tanh(_mlp(x, kh_w1, kh_b1, kh_w2, kh_b2)).reshape(Bx, Lx, N_HYP, 2) * 0.9
        query_h = jnp.tanh(_mlp(x, qh_w1, qh_b1, qh_w2, qh_b2)).reshape(Bx, Lx, N_HYP, 2) * 0.9
        key_ang = jnp.arctan2(key_h[..., 1], key_h[..., 0])
        query_ang = jnp.arctan2(query_h[..., 1], query_h[..., 0])
        key_amp = 1.0 - jnp.sqrt(jnp.sum(key_h * key_h, axis=-1))
        query_amp = 1.0 - jnp.sqrt(jnp.sum(query_h * query_h, axis=-1))
        key_phasor_h = key_amp * jnp.exp(1j * key_ang.astype(jnp.complex64))
        query_phasor_h = query_amp * jnp.exp(1j * query_ang.astype(jnp.complex64))
        key_phasor = jnp.concatenate([key_phasor_p, key_phasor_h], axis=-1)
        query_phasor = jnp.concatenate([query_phasor_p, query_phasor_h], axis=-1)
        V = (x @ v_w.T + v_b).astype(jnp.complex64)
        bound = key_phasor[..., :, None] * V[..., None, :]
        memory = jnp.cumsum(bound, axis=1)
        retrieved = jnp.real(jnp.sum(memory * jnp.conj(query_phasor)[..., None], axis=2))
        positions = jnp.arange(1, Lx + 1, dtype=jnp.float32)
        norm = jnp.sqrt(positions * float(K))[None, :, None]
        r = retrieved / norm
        mu = jnp.mean(r, axis=-1, keepdims=True)
        var = jnp.mean(jnp.square(r - mu), axis=-1, keepdims=True)
        r_ln = (r - mu) / jnp.sqrt(var + 1e-05) * ln_g + ln_b
        return x + (r_ln @ out_w.T + out_b)

    def _L0_ffn_ref(x, ln1_w, ln2_w, wq, wk, wv, wo, router_w, w1, w2, w3):
        import jax, jax.numpy as jnp
        import numpy as np
        B, T, C = (64, 96, 64)
        NH, NKV = (4, 2)
        HD = C // NH
        NREP = NH // NKV
        NE, TOPK = (8, 2)
        HID = int(8 / 3 * C)
        EPS_RMS = 1e-06

        def _rope_tables(t_len):
            inv_freq = 1.0 / 10000.0 ** (np.arange(0, HD, 2, dtype=np.float32) / HD)
            t = np.arange(t_len, dtype=np.float32)
            freqs = np.outer(t, inv_freq)
            emb = np.concatenate([freqs, freqs], axis=-1)
            return (jnp.asarray(np.cos(emb)), jnp.asarray(np.sin(emb)))

        def _rotate_half(x):
            h = x.shape[-1] // 2
            return jnp.concatenate([-x[..., h:], x[..., :h]], axis=-1)

        def _rmsnorm(v, w):
            return v * jax.lax.rsqrt(jnp.mean(v * v, axis=-1, keepdims=True) + EPS_RMS) * w
        Bx, Tx, Cx = x.shape
        h = _rmsnorm(x, ln1_w)
        q = (h @ wq.T).reshape(Bx, Tx, NH, HD).transpose(0, 2, 1, 3)
        k = (h @ wk.T).reshape(Bx, Tx, NKV, HD).transpose(0, 2, 1, 3)
        v = (h @ wv.T).reshape(Bx, Tx, NKV, HD).transpose(0, 2, 1, 3)
        cos, sin = _rope_tables(Tx)
        cos, sin = (cos[None, None], sin[None, None])
        q = q * cos + _rotate_half(q) * sin
        k = k * cos + _rotate_half(k) * sin
        k = jnp.repeat(k, NREP, axis=1)
        v = jnp.repeat(v, NREP, axis=1)
        scores = jnp.einsum('bhtd,bhsd->bhts', q, k) / jnp.sqrt(jnp.float32(HD))
        causal = jnp.tril(jnp.ones((Tx, Tx), dtype=bool))
        scores = jnp.where(causal[None, None], scores, jnp.float32(-1e+30))
        att = jax.nn.softmax(scores, axis=-1)
        y = jnp.einsum('bhts,bhsd->bhtd', att, v).transpose(0, 2, 1, 3).reshape(Bx, Tx, Cx)
        x = x + y @ wo.T
        flat = _rmsnorm(x, ln2_w).reshape(-1, Cx)
        probs = jax.nn.softmax(flat @ router_w.T, axis=-1)
        tp, ti = jax.lax.top_k(probs, TOPK)
        tp = tp / (jnp.sum(tp, axis=-1, keepdims=True) + 1e-09)
        weights = jnp.sum(tp[..., None] * jax.nn.one_hot(ti, NE, dtype=flat.dtype), axis=1)
        out = jnp.zeros_like(flat)
        for e in range(NE):
            hh = jax.nn.silu(flat @ w1[e].T) * (flat @ w3[e].T)
            out = out + weights[:, e:e + 1] * (hh @ w2[e].T)
        return x + out.reshape(Bx, Tx, Cx)

    def _L1_attn_ref(x, W_in, conv_w, conv_b, W_xproj, w_dt, b_dt, A, D, W_out):
        import jax, jax.numpy as jnp
        import numpy as np
        D_MODEL, D_INNER, D_STATE, K = (64, 128, 16, 4)

        def _depthwise_causal_conv(xp, conv_w, conv_b):
            xt = jnp.transpose(xp, (0, 2, 1))
            out = jax.lax.conv_general_dilated(xt, conv_w, window_strides=(1,), padding=[(K - 1, 0)], dimension_numbers=('NCH', 'OIH', 'NCH'), feature_group_count=D_INNER)
            out = out + conv_b[None, :, None]
            return jnp.transpose(out, (0, 2, 1))
        B, T, _ = x.shape
        xz = x @ W_in
        x_part, z_part = jnp.split(xz, 2, axis=-1)
        xc = _depthwise_causal_conv(x_part, conv_w, conv_b)
        u = xc * jax.nn.sigmoid(z_part)
        xp = u @ W_xproj
        dt_in = xp[..., :1]
        B_t = xp[..., 1:1 + D_STATE]
        C_t = xp[..., 1 + D_STATE:]
        dt = jax.nn.softplus(dt_in * w_dt + b_dt)
        xs = (jnp.moveaxis(dt, 1, 0), jnp.moveaxis(u, 1, 0), jnp.moveaxis(B_t, 1, 0), jnp.moveaxis(C_t, 1, 0))

        def step(state, inp):
            dt_t, u_t, Bv, Cv = inp
            dA = jnp.exp(dt_t[..., None] * A[None])
            state = state * dA + (dt_t * u_t)[..., None] * Bv[:, None, :]
            yt = jnp.sum(state * Cv[:, None, :], axis=-1) + D * u_t
            return (state, yt)
        state0 = jnp.zeros((B, D_INNER, D_STATE), dtype=x.dtype)
        _, y = jax.lax.scan(step, state0, xs)
        y = jnp.moveaxis(y, 1, 0)
        return y @ W_out

    def _L1_ffn_ref(x, Wq_pk, pk_keys, Wq, keys_table, values_table, Wo):
        import jax, jax.numpy as jnp
        import numpy as np
        DIM = 64
        HEADS = 8
        NUM_KEYS = 64
        NUM_KV = NUM_KEYS ** 2
        PK_TOPK = 16
        FINAL_TOPK = 16
        DIM_KEY = DIM // 2
        P = 2

        def _pk(x, Wq_pk, pk_keys):
            b, n, _ = x.shape
            q = (x @ Wq_pk).reshape(b, n, P, HEADS, DIM_KEY).transpose(2, 0, 1, 3, 4)
            sim = jnp.einsum('pbnhd,pkhd->pbnhk', q, pk_keys)
            scores, idx = jax.lax.top_k(sim, PK_TOPK)
            idx0 = idx[0]
            idx1 = idx[1] * NUM_KEYS
            index = (idx0[..., :, None] + idx1[..., None, :]).reshape(b, n, HEADS, PK_TOPK * PK_TOPK)
            score = (scores[0][..., :, None] + scores[1][..., None, :]).reshape(b, n, HEADS, PK_TOPK * PK_TOPK)
            final_scores, pk_idx = jax.lax.top_k(score, FINAL_TOPK)
            final_indices = jnp.take_along_axis(index, pk_idx, axis=-1)
            final_scores = jax.nn.softmax(final_scores, axis=-1)
            return (final_scores, final_indices)
        b, n, d = x.shape
        q = (x @ Wq).reshape(b, n, HEADS, DIM) * DIM ** (-0.5)
        kv_scores, indices = _pk(x, Wq_pk, pk_keys)
        offsets = jnp.arange(HEADS, dtype=indices.dtype) * NUM_KV
        ind = indices + offsets[None, None, :, None]
        k = jnp.einsum('bnhk,bnhkd->bnhd', kv_scores, keys_table[ind])
        v = jnp.einsum('bnhk,bnhkd->bnhd', kv_scores, values_table[ind])
        sim = jnp.einsum('bihd,bjhd->bhij', q, k)
        neg = -jnp.finfo(sim.dtype).max
        causal = jnp.tril(jnp.ones((n, n), dtype=bool))
        sim = jnp.where(causal, sim, neg)
        attn = jax.nn.softmax(sim, axis=-1)
        out = jnp.einsum('bhij,bjhd->bhid', attn, v)
        out = out.transpose(0, 2, 1, 3).reshape(b, n, HEADS * DIM)
        return out @ Wo

    def _L2_attn_ref(x_q, x_r, y, W_in, b_in, W_slice, b_slice, temperature, W_q, b_q, W_k, b_k, W_v, b_v, W_out, b_out):
        import jax, jax.numpy as jnp
        import numpy as np
        B, T, C, H, G = (8, 2048, 64, 8, 64)
        D = C // H
        Bs, Ts, Cs = x_q.shape
        Hh = temperature.shape[1]
        Dd = Cs // Hh
        tmp_x = (x_q @ W_in + b_in).reshape(Bs, Ts, Hh, Dd).transpose(0, 2, 1, 3)
        slice_weights = jax.nn.softmax((tmp_x @ W_slice + b_slice) / temperature, axis=-1)
        slice_norm = slice_weights.sum(axis=2)
        slice_ = jnp.einsum('bhnc,bhng->bhgc', tmp_x, slice_weights)
        token = slice_ / (slice_norm[:, :, :, None] + 1e-05)
        q = token @ W_q + b_q
        k = token @ W_k + b_k
        v = token @ W_v + b_v
        attn = jax.nn.softmax(q @ k.swapaxes(-2, -1) / float(np.sqrt(Dd)), axis=-1)
        out = attn @ v
        out = jnp.einsum('bhgc,bhng->bhnc', out, slice_weights)
        out = out.transpose(0, 2, 1, 3).reshape(Bs, Ts, Cs)
        return out @ W_out + b_out

    def _L2_ffn_ref(input_embeddings, router_w, w1, b1, w2, b2):
        import jax, jax.numpy as jnp
        import numpy as np
        NUM_EXPERTS = 8
        TOP_K = 2
        B, S, D = (8, 2048, 64)

        def _moe(tokens, router_w, w1, b1, w2, b2):
            N = tokens.shape[0]
            E = router_w.shape[0]
            logits = tokens.astype(jnp.float32) @ router_w.astype(jnp.float32).T
            probs = jax.nn.softmax(logits, axis=-1)
            rw, re = jax.lax.top_k(probs, TOP_K)
            if TOP_K > 1:
                rw = rw / jnp.maximum(rw.sum(-1, keepdims=True), 1e-12)
            rw = rw.astype(tokens.dtype)
            combine = jnp.zeros((N, E), tokens.dtype).at[jnp.arange(N)[:, None], re].set(rw)
            out = tokens
            for e in range(E):
                h = jax.nn.gelu(tokens @ w1[e] + b1[e], approximate=False)
                y = h @ w2[e] + b2[e]
                out = out + combine[:, e:e + 1] * y
            return out
        b, s, d = input_embeddings.shape
        tokens = input_embeddings.reshape(b * s, d)
        return _moe(tokens, router_w, w1, b1, w2, b2).reshape(b, s, d)

    def _L3_attn_ref(x_in, W_ih, W_hh, b_ih, b_hh):
        import jax, jax.numpy as jnp
        import numpy as np
        SEQ, BATCH, IN, HID = (512, 64, 64, 64)
        xp = jnp.einsum('tbi,hi->tbh', x_in, W_ih) + b_ih + b_hh
        h0 = jnp.zeros((x_in.shape[1], W_hh.shape[0]), dtype=x_in.dtype)

        def step(h, xp_t):
            h_new = jnp.tanh(xp_t + h @ W_hh.T)
            return (h_new, h_new)
        _, hiddens = jax.lax.scan(step, h0, xp)
        return hiddens

    def _L3_ffn_ref(x, W1, b1, Wg, bg, Wd, bd):
        import jax, jax.numpy as jnp
        import numpy as np
        C = 64
        HID = 256
        E = 8
        TEMP = 1.0
        orig_shape = x.shape
        xf = x.reshape(-1, orig_shape[-1])
        H = jax.nn.gelu(xf @ W1 + b1, approximate=False)
        probs = jax.nn.softmax((H @ Wg + bg) / TEMP, axis=-1)
        assign = jnp.argmax(probs, axis=-1)
        out = jnp.zeros_like(xf)
        for e in range(Wd.shape[0]):
            y = H @ Wd[e] + bd[e]
            sel = (assign == e)[:, None]
            out = out + jnp.where(sel, probs[:, e:e + 1] * y, 0.0)
        return out.reshape(orig_shape)
    h = _L0_tok_ref(x, L0_tok_W)
    h = jnp.concatenate([jnp.broadcast_to(cls_tok, (h.shape[0], 1, h.shape[2])), h], axis=1)
    h = h + _L0_attn_ref(_layernorm(h, axis=-1), L0_attn_kp_w1, L0_attn_kp_b1, L0_attn_kp_w2, L0_attn_kp_b2, L0_attn_qp_w1, L0_attn_qp_b1, L0_attn_qp_w2, L0_attn_qp_b2, L0_attn_kh_w1, L0_attn_kh_b1, L0_attn_kh_w2, L0_attn_kh_b2, L0_attn_qh_w1, L0_attn_qh_b1, L0_attn_qh_w2, L0_attn_qh_b2, L0_attn_v_w, L0_attn_v_b, L0_attn_ln_g, L0_attn_ln_b, L0_attn_out_w, L0_attn_out_b)
    h = h + _L0_ffn_ref(_layernorm(h, axis=-1), L0_ffn_ln1_w, L0_ffn_ln2_w, L0_ffn_wq, L0_ffn_wk, L0_ffn_wv, L0_ffn_wo, L0_ffn_router_w, L0_ffn_w1, L0_ffn_w2, L0_ffn_w3)
    h = h + _L1_attn_ref(_layernorm(h, axis=-1), L1_attn_W_in, L1_attn_conv_w, L1_attn_conv_b, L1_attn_W_xproj, L1_attn_w_dt, L1_attn_b_dt, L1_attn_A, L1_attn_D, L1_attn_W_out)
    h = h + _L1_ffn_ref(_layernorm(h, axis=-1), L1_ffn_Wq_pk, L1_ffn_pk_keys, L1_ffn_Wq, L1_ffn_keys_table, L1_ffn_values_table, L1_ffn_Wo)
    h = h + _L2_attn_ref(_layernorm(h, axis=-1), L2_attn_x_r, L2_attn_y, L2_attn_W_in, L2_attn_b_in, L2_attn_W_slice, L2_attn_b_slice, L2_attn_temperature, L2_attn_W_q, L2_attn_b_q, L2_attn_W_k, L2_attn_b_k, L2_attn_W_v, L2_attn_b_v, L2_attn_W_out, L2_attn_b_out)
    h = h + _L2_ffn_ref(_layernorm(h, axis=-1), L2_ffn_router_w, L2_ffn_w1, L2_ffn_b1, L2_ffn_w2, L2_ffn_b2)
    h = h + _L3_attn_ref(_layernorm(h, axis=-1), L3_attn_W_ih, L3_attn_W_hh, L3_attn_b_ih, L3_attn_b_hh)
    h = h + _L3_ffn_ref(_layernorm(h, axis=-1), L3_ffn_W1, L3_ffn_b1, L3_ffn_Wg, L3_ffn_bg, L3_ffn_Wd, L3_ffn_bd)
    return h

_drawn_inputs = setup_inputs


def setup_inputs(seed=0):
    import zlib

    import numpy as np

    out = dict(_drawn_inputs(seed))
    spreads = {'L0_attn_kp_b1': (0.0, 0.8),
     'L0_attn_kp_b2': (0.0, 0.8),
     'L0_attn_qp_b1': (0.0, 0.8),
     'L0_attn_qp_b2': (0.0, 0.8),
     'L0_attn_kh_b1': (0.0, 0.8),
     'L0_attn_kh_b2': (0.0, 0.8),
     'L0_attn_qh_b1': (0.0, 0.8),
     'L0_attn_qh_b2': (0.0, 0.8),
     'L0_attn_v_b': (0.0, 0.1),
     'L0_attn_ln_g': (1.0, 0.6),
     'L0_attn_ln_b': (0.0, 0.502),
     'L0_attn_out_b': (0.0, 0.1),
     'L0_ffn_ln1_w': (1.0, 0.6),
     'L0_ffn_ln2_w': (1.0, 0.6),
     'L2_attn_b_in': (0.0, 2.0),
     'L2_attn_b_slice': (0.0, 2.0),
     'L2_attn_temperature': (0.3535533845424652, 0.6),
     'L2_attn_b_q': (0.0, 2.0),
     'L2_attn_b_k': (0.0, 2.0),
     'L2_attn_b_v': (0.0, 0.8),
     'L2_attn_b_out': (0.0, 1.371),
     'L2_ffn_b1': (0.0, 2.0),
     'L2_ffn_b2': (0.0, 1.855),
     'L3_ffn_b1': (0.0, 0.8),
     'L3_ffn_bg': (0.0, 0.8),
     'L3_ffn_bd': (0.0, 2.0)}
    factors = {'L0_attn_kp_w1': 8.0,
     'L0_attn_kp_w2': 8.0,
     'L0_attn_qp_w1': 8.0,
     'L0_attn_qp_w2': 8.0,
     'L0_attn_kh_w1': 8.0,
     'L0_attn_kh_w2': 8.0,
     'L0_attn_qh_w1': 8.0,
     'L0_attn_qh_w2': 8.0,
     'L0_attn_v_w': 3.237,
     'L0_ffn_wq': 8.0,
     'L0_ffn_wk': 8.0,
     'L0_ffn_wv': 8.0,
     'L0_ffn_wo': 8.0,
     'L0_ffn_router_w': 8.0,
     'L0_ffn_w1': 8.0,
     'L0_ffn_w2': 8.0,
     'L0_ffn_w3': 8.0,
     'L1_attn_W_in': 8.0,
     'L1_attn_conv_w': 8.0,
     'L1_attn_conv_b': 8.0,
     'L1_attn_W_xproj': 8.0,
     'L1_attn_w_dt': 59.465,
     'L1_attn_b_dt': 34.854,
     'L1_attn_A': 200.0,
     'L1_attn_D': 8.0,
     'L1_attn_W_out': 8.0,
     'L1_ffn_Wq_pk': 58.616,
     'L1_ffn_pk_keys': 61.228,
     'L1_ffn_Wq': 64.0,
     'L1_ffn_keys_table': 64.0,
     'L1_ffn_values_table': 48.374,
     'L1_ffn_Wo': 46.764,
     'L2_attn_W_in': 23.985,
     'L2_attn_W_slice': 112.244,
     'L2_attn_W_q': 180.625,
     'L2_attn_W_k': 38.292,
     'L2_attn_W_v': 8.0,
     'L2_attn_W_out': 6.38,
     'L3_attn_b_ih': 14.368,
     'L3_attn_b_hh': 16.544,
     'L3_ffn_W1': 8.0,
     'L3_ffn_Wg': 8.0,
     'L3_ffn_Wd': 8.0,
     'L3_attn_W_hh': 4.56}
    for name, (base, spread) in spreads.items():
        noise = np.random.default_rng([zlib.crc32(name.encode()), seed]).standard_normal(out[name].shape)
        drawn = base * np.exp(spread * noise) if base else spread * noise
        out[name] = jnp.asarray(drawn.astype(out[name].dtype))
    for name, factor in factors.items():
        out[name] = (out[name] * factor).astype(out[name].dtype)
    return out
```

```python
import math
from contextlib import ExitStack, contextmanager

import numpy as np
import concourse.bass as bass
from concourse import mybir

F32 = mybir.dt.float32
U32 = mybir.dt.uint32
ALU = mybir.AluOpType
ACT = mybir.ActivationFunctionType
AX = mybir.AxisListType

P = 128
C = 64
N_BATCH = 8
N_PATCH, PATCH, HOP = 16, 16, 8
N_VAR, N_TIME = 64, 128
N_TOK = 1 + N_VAR * N_PATCH
NT = -(-N_TOK // P)
NP = NT * P
CHUNKS = [(a, min(a + 512, NP)) for a in range(0, NP, 512)]
NPER, NHYP = 48, 16
NE, HID0 = 8, 170
HB = HID0 // 2
NSTATE, TAPS = 16, 4
PKH, PKK, TOPK = 8, 64, 16
NEG = -1e30
LOWEST = -3.0e38
LN_EPS, RMS_EPS = 1e-5, 1e-6

PAIRS = []
_off = 0
for _i0, _i1, _j in [(0, 1, 16), (1, 2, 8), (2, 3, 5), (3, 4, 4), (4, 5, 3), (5, 8, 2), (8, 16, 1)]:
    PAIRS.append((_off, _i0, _i1, _j))
    _off += (_i1 - _i0) * _j
NPAIR = _off


def constants():
    t = np.arange(PATCH)
    f = np.arange(PATCH // 2 + 1)
    ang = 2 * np.pi * np.outer(f, t) / PATCH
    dft = np.concatenate([np.cos(ang), -np.sin(ang)], 0) / math.sqrt(PATCH)
    tok = np.arange(NP).reshape(NT, P).T
    inv = 1.0 / 10000.0 ** (np.arange(0, 16, 2, dtype=np.float32) / 16)
    fr = (tok[..., None].astype(np.float32) * inv).astype(np.float32)
    sin, cos = np.sin(fr), np.cos(fr)
    q, k = np.arange(P)[:, None], np.arange(P)[None, :]
    row = np.arange(P)[:, None]
    head_of_row = np.arange(4)[None, :, None] * 2 + row[:, :, None] // 64
    return {
        "c_dft": dft,
        "c_pos": 1.0 / np.sqrt((tok + 1) * 64.0),
        "c_cos": np.concatenate([cos, cos], -1),
        "c_sin": np.concatenate([-sin, sin], -1),
        "c_ident": np.eye(P),
        "c_after": np.where(k > q, NEG, 0.0),
        "c_afterT": np.where(q > k, NEG, 0.0),
        "c_upto": np.where(q <= k, 1.0, 0.0),
        "c_rank": np.broadcast_to(8.0 - np.arange(NE), (P, NE)),
        "c_headoff": np.broadcast_to(np.arange(PKH) * float(PKK * PKK), (P, PKH)),
        "c_iota": np.broadcast_to(np.arange(NPAIR), (P, NPAIR)),
        "c_ownhead": (np.arange(C)[None, None, :] // 8 == head_of_row),
        "c_valid": (tok < N_TOK),
        "c_headrow": (np.arange(P)[:, None] // TOPK == np.arange(PKH)[None, :]),
    }


class Phases:

    def __init__(self, nc):
        self.nc = nc
        self.stale = []

    def clear(self):
        for s in self.stale:
            self.nc.gpsimd.sem_clear(s)
        self.stale = []

    def close_loop(self):
        self.clear()
        self.nc.all_engine_barrier()

    @contextmanager
    def phase(self, *names):
        self.clear()
        with ExitStack() as ctx:
            sems = [ctx.enter_context(self.nc.semaphore(n)) for n in names]
            with self.nc.Block() as block:
                yield (block, *sems)
        self.stale = sems


class Steps:

    def __init__(self, eng, sem):
        self.eng, self.sem, self.n = eng, sem, 0

    def __call__(self, ins):
        self.n += 1
        ins.then_inc(self.sem, 1)
        self.eng.wait_ge(self.sem, self.n)


def build(nc, io, out, n_batch=N_BATCH, upto=99):
    ctx = ExitStack()
    with ctx:
        ph = Phases(nc)

        def sb(name, shape, dt=F32):
            return ctx.enter_context(nc.sbuf_tensor(name, shape, dt))

        taken = {}

        def scratch(name, shape, dt=F32):
            taken[name] = taken.get(name, 0) + 1
            return nc.sbuf_tensor(f"{name}_{taken[name]}", shape, dt)

        psum = ctx.enter_context(nc.psum_tensor("psum", [P, 8 * 512], F32))
        A, B, D = 0, 3 * 512, 6 * 512
        loads = []

        def const(key, shape, name=None, dst=None, src=None):
            t = dst if dst is not None else sb(name or "sb_" + key, shape)[:]
            loads.append((t, src if src is not None else io[key]))
            return t

        ident = const("c_ident", [P, P])
        after = const("c_after", [P, P])
        afterT = const("c_afterT", [P, P])
        upto_q = const("c_upto", [P, P])
        pos_norm = const("c_pos", [P, NT])
        cos = const("c_cos", [P, NT, 16])
        sin = const("c_sin", [P, NT, 16])
        rank = const("c_rank", [P, NE])
        headoff = const("c_headoff", [P, PKH])
        iota = const("c_iota", [P, NPAIR])
        ownhead = const("c_ownhead", [P, 4, C])
        valid = const("c_valid", [P, NT])
        headrow = const("c_headrow", [P, PKH])
        a_w1p = const("a_w1p", [C, P])
        a_w1h = const("a_w1h", [C, P])
        a_b1p = const("a_b1p", [P, 1])
        a_b1h = const("a_b1h", [P, 1])
        a_b2 = const("a_b2", [1, 160])
        a_vw = const("a_vw", [C, C])
        a_vb = const("a_vb", [1, C])
        a_ow = const("a_ow", [C, C])
        a_ob = const("a_ob", [1, C])
        a_g = const("a_g", [P, C], src=io["a_g"].partition_broadcast(P))
        a_b = const("a_b", [P, C], src=io["a_b"].partition_broadcast(P))
        f_ln1 = const("f_ln1", [P, C], src=io["f_ln1"].partition_broadcast(P))
        f_ln2 = const("f_ln2", [P, C], src=io["f_ln2"].partition_broadcast(P))
        f_qkv = const("f_qkv", [C, P])
        f_wo = const("f_wo", [C, C])
        f_router = const("f_router", [C, NE])
        f_w1 = const("f_w1", [C, NE * HID0])
        f_w3 = const("f_w3", [C, NE * HID0])
        f_w2 = const("f_w2", [HB, 2 * NE, C])
        m_in = const("m_in", [C, 2 * P])
        m_cw = const("m_cw", [P, TAPS])
        m_cb = const("m_cb", [P, 1])
        m_xp = const("m_xp", [P, 1 + 2 * NSTATE])
        m_wdt = const("m_wdt", [P, 1])
        m_bdt = const("m_bdt", [P, 1])
        m_A = const("m_A", [P, NSTATE])
        m_D = const("m_D", [P, 1])
        m_out = const("m_out", [P, C])
        k_wqpk = const("k_wqpk", [C, 512])
        k_wq = const("k_wq", [C, 512])
        k_wo = const("k_wo", [P, 4, C])
        s_win = const("s_win", [C, C])
        s_bin_row = const("s_bin_row", [1, C])
        s_bin_col = const("s_bin_col", [C, 1])
        s_bslice = const("s_bslice", [1, 512])
        s_temp = const("s_temp", [P, 8], src=io["s_temp"].partition_broadcast(P))
        s_qkvw = const("s_qkvw", [C, 24])
        s_bq = const("s_bq", [8, 1])
        s_bk = const("s_bk", [8, 1])
        s_bv = const("s_bv", [1, 8])
        s_wout = const("s_wout", [C, C])
        s_bout = const("s_bout", [1, C])
        e_router = const("e_router", [C, NE])
        e_w1 = const("e_w1", [C, 512])
        e_b1 = const("e_b1", [P, 4])
        e_b2 = const("e_b2", [1, 512])
        r_ih = const("r_ih", [C, C])
        r_hh = const("r_hh", [C, C])
        r_b = const("r_b", [C, 2])
        g_w1 = const("g_w1", [C, 256])
        g_b1 = const("g_b1", [P, 2])
        g_wg = const("g_wg", [P, 2, NE])
        g_bg = const("g_bg", [1, NE])
        g_wd = const("g_wd", [P, 2, 512])
        g_bd = const("g_bd", [1, 512])

        a_w2p = sb("a_w2p_sb", [P, 96])
        a_w2h = sb("a_w2h_sb", [P, 64])
        k_keys = sb("k_keys_sb", [P, 4, 256])
        s_slice = sb("s_slice_sb", [C, 512])
        e_w2 = sb("e_w2_sb", [P, 4, P])
        blocks = []
        for j in range(2):
            blocks.append((a_w2p[j * 64:(j + 1) * 64, j * 48:(j + 1) * 48], io["a_w2p"][j]))
            blocks.append((a_w2h[j * 64:(j + 1) * 64, j * 32:(j + 1) * 32], io["a_w2h"][j]))
        for c in range(4):
            for j in range(4):
                blocks.append((k_keys[32 * j:32 * j + 32, c, 64 * j:64 * j + 64], io["k_keys"][c, j]))
            for j in range(2):
                blocks.append((e_w2[64 * j:64 * j + 64, c, 64 * j:64 * j + 64], io["e_w2"][2 * c + j]))
        for h in range(8):
            blocks.append((s_slice[8 * h:8 * h + 8, 64 * h:64 * h + 64], io["s_wslice"]))

        w_tok = sb("w_tok", [P, 8, C])
        w_rep = sb("w_rep", [P, 1 + 2 * NSTATE, P])
        ones = sb("ones", [P, P])
        eps = sb("eps", [P, 3])
        s_rtemp = sb("s_rtemp", [P, 8])
        r_bias = sb("r_bias", [C, 1])

        h_tok = sb("h_tok", [P, NT, C])
        x_tok = sb("x_tok", [P, NT, C])
        xT = sb("xT", [C, NP])
        y_tok = sb("y_tok", [P, NT, C])
        yT = sb("yT", [C, NP])
        hidden = sb("hidden", [C, NP])
        stat = sb("stat", [P, 8, NT])
        tmp = sb("tmp", [P, NT, C])
        rt_l, rt_p, rt_k, rt_m, rt_o, rt_w = [sb(f"rt{i}", [P, NT, NE]) for i in range(6)]
        rt_s = sb("rt_s", [P, 4, NT])

        dram_w = nc.dram_tensor("dram_w", [PATCH, C, C], F32, kind="Internal").ap()

        def bc(ap, shape, axis):
            return ap.unsqueeze(axis).broadcast_to(shape)

        def flat(t):
            return t[:].rearrange("p a b -> p (a b)")

        def columns(base, rows, pairs):
            for a, b in CHUNKS:
                for n, (w, d) in enumerate(pairs):
                    last = nc.tensor.matmul(psum[0:rows, base + a:base + b], w, d[:, a:b],
                                            start=(n == 0), stop=(n == len(pairs) - 1))
            return last

        def turn_tiles(base, src, rows):
            for t in range(NT):
                last = nc.tensor.transpose(psum[0:rows, base + t * P:base + (t + 1) * P],
                                           src[:, t, :], ident)
            return last

        with ph.phase("cleared", "loaded", "fold_in", "folded", "fold_out", "fold_back", "sp_blocks",
                      "dve_step") as (block, cleared, loaded, fold_in, folded, fold_out, fold_back,
                                      blocks_in, dve_step):
            with scratch("w_freq", [18, C, C]) as w_freq, \
                    scratch("dft", [18, PATCH]) as dft, \
                    scratch("w_fold", [PATCH, C * C]) as w_fold:

                @block.sync
                def _(sp):
                    sp.dma_start(w_freq[:], io["t_w"]).then_inc(fold_in, 16)
                    sp.dma_start(dft[:], io["c_dft"]).then_inc(fold_in, 16)
                    for dst, src in loads:
                        sp.dma_start(dst, src).then_inc(loaded, 16)
                    sp.wait_ge(cleared, 1)
                    for dst, src in blocks:
                        sp.dma_start(dst, src).then_inc(blocks_in, 16)
                    sp.wait_ge(fold_out, 2)
                    sp.dma_start(dram_w, w_fold[:].rearrange("t (c o) -> t c o", c=C)).then_inc(fold_back, 16)
                    sp.wait_ge(fold_back, 16)
                    for r in range(2):
                        sp.dma_start(w_tok[r * C:(r + 1) * C],
                                     dram_w.rearrange("(u r) c o -> r c u o", r=2)[r]).then_inc(fold_back, 16)
                    sp.wait_ge(fold_back, 48)
                    sp.wait_ge(loaded, 16 * len(loads))
                    sp.wait_ge(blocks_in, 16 * len(blocks))

                @block.tensor
                def _(pe):
                    pe.wait_ge(fold_in, 32)
                    wf = w_freq[:].rearrange("f c o -> f (c o)")
                    for n in range(8):
                        nc.tensor.matmul(psum[0:PATCH, n * 512:(n + 1) * 512], dft[:],
                                         wf[:, n * 512:(n + 1) * 512], start=True, stop=True).then_inc(folded, 1)

                @block.vector
                def _(dve):
                    for t in (a_w2p, a_w2h, k_keys, s_slice):
                        nc.vector.memset(t[:], 0.0)
                    nc.vector.memset(e_w2[:], 0.0).then_inc(cleared, 1)
                    nc.vector.memset(ones[:], 1.0)
                    nc.vector.memset(eps[:, 0:1], LN_EPS)
                    nc.vector.memset(eps[:, 1:2], RMS_EPS)
                    nc.vector.memset(eps[:, 2:3], math.pi / 2)
                    nc.vector.memset(hidden[:], 0.0)
                    dve.wait_ge(folded, 8)
                    nc.vector.tensor_copy(w_fold[:], psum[0:PATCH, :]).then_inc(fold_out, 2)
                    dve.wait_ge(loaded, 16 * len(loads))
                    nc.vector.reciprocal(s_rtemp[:], s_temp)
                    nc.vector.tensor_tensor(r_bias[:], r_b[:, 0:1], r_b[:, 1:2], ALU.add)
                    nc.vector.tensor_copy(w_rep[:], bc(m_xp, [P, 1 + 2 * NSTATE, P], 2))

        def layer_norm(rms_weight=None, src=None, dst=None, want_T=True):
            src = src or h_tok
            dst = dst or x_tok
            rms = rms_weight is not None
            with ph.phase("variance", "deviation", "normed", "turned", "dve_step") as (
                    block, variance, deviation, normed, turned, dve_step):
                @block.vector
                def _(dve):
                    step = Steps(dve, dve_step)
                    cen = src
                    if not rms:
                        step(nc.vector.tensor_reduce(stat[:, 0], src[:], AX.X, ALU.add))
                        step(nc.vector.tensor_scalar(stat[:, 1], stat[:, 0], 1.0 / C, None, ALU.mult))
                        step(nc.vector.tensor_tensor(dst[:], src[:], bc(stat[:, 1], [P, NT, C], 2), ALU.subtract))
                        cen = dst
                    step(nc.vector.tensor_tensor(tmp[:], cen[:], cen[:], ALU.mult))
                    nc.vector.tensor_reduce(stat[:, 2], tmp[:], AX.X, ALU.add).then_inc(variance, 1)
                    dve.wait_ge(deviation, 1)
                    step(nc.vector.reciprocal(stat[:, 4], stat[:, 3]))
                    ins = nc.vector.tensor_tensor(dst[:], cen[:], bc(stat[:, 4], [P, NT, C], 2), ALU.mult)
                    if rms:
                        step(ins)
                        ins = nc.vector.tensor_tensor(dst[:], dst[:], bc(rms_weight, [P, NT, C], 1), ALU.mult)
                    ins.then_inc(normed, 1)

                @block.scalar
                def _(act):
                    act.wait_ge(variance, 1)
                    nc.scalar.activation(stat[:, 3], stat[:, 2], ACT.Sqrt, scale=1.0 / C,
                                         bias=eps[:, 1:2] if rms else eps[:, 0:1]).then_inc(deviation, 1)
                    if want_T:
                        act.wait_ge(turned, 1)
                        nc.scalar.copy(xT[:], psum[0:C, A:A + NP])

                @block.tensor
                def _(pe):
                    pe.wait_ge(normed, 1)
                    if want_T:
                        turn_tiles(A, dst, C).then_inc(turned, 1)

        def project_add(srcT, weights, bias, extra=None):
            with ph.phase("projected", "dve_step") as (block, projected, dve_step):
                @block.tensor
                def _(pe):
                    for t in range(NT):
                        o = psum[:, A + t * C:A + (t + 1) * C]
                        for n, (s, w) in enumerate(zip(srcT, weights)):
                            last = nc.tensor.matmul(o, s[:, t * P:(t + 1) * P], w, start=(n == 0),
                                                    stop=(n == len(srcT) - 1 and bias is None))
                        if bias is not None:
                            last = nc.tensor.matmul(o, ones[0:1, :], bias, start=False, stop=True)
                    last.then_inc(projected, 1)

                @block.vector
                def _(dve):
                    step = Steps(dve, dve_step)
                    if extra is not None:
                        step(nc.vector.tensor_tensor(flat(h_tok), flat(h_tok), flat(extra), ALU.add))
                    dve.wait_ge(projected, 1)
                    nc.vector.tensor_tensor(flat(h_tok), flat(h_tok), psum[:, A:A + NT * C], ALU.add)

        def softmax_experts(step, logits):
            step(nc.vector.tensor_reduce(rt_s[:, 0], logits, AX.X, ALU.max))
            step(nc.vector.tensor_tensor(rt_l[:], logits, bc(rt_s[:, 0], [P, NT, NE], 2), ALU.subtract))

        def pick_best(step, probs, picked, top):
            step(nc.vector.tensor_reduce(top, probs, AX.X, ALU.max))
            step(nc.vector.tensor_tensor(rt_k[:], probs, bc(top, [P, NT, NE], 2), ALU.is_ge))
            step(nc.vector.tensor_tensor(rt_k[:], rt_k[:], bc(rank, [P, NT, NE], 1), ALU.mult))
            step(nc.vector.tensor_reduce(rt_s[:, 3], rt_k[:], AX.X, ALU.max))
            step(nc.vector.tensor_tensor(picked, rt_k[:], bc(rt_s[:, 3], [P, NT, NE], 2), ALU.is_equal))

        def route(logit_products, top2, floor_add, floor_max):
            with ph.phase("logits", "shifted", "exps", "dve_step") as (block, logits, shifted, exps, dve_step):
                @block.tensor
                def _(pe):
                    for t in range(NT):
                        last = logit_products(t, psum[:, D + t * NE:D + (t + 1) * NE])
                    last.then_inc(logits, 1)

                @block.scalar
                def _(act):
                    act.wait_ge(shifted, 1)
                    nc.scalar.activation(rt_p[:], rt_l[:], ACT.Exp).then_inc(exps, 1)

                @block.vector
                def _(dve):
                    step = Steps(dve, dve_step)
                    lg = psum[:, D:D + NT * NE].rearrange("p (t e) -> p t e", e=NE)
                    dve.wait_ge(logits, 1)
                    softmax_experts(step, lg)
                    nc.vector.tensor_copy(rt_s[:, 1], rt_s[:, 0]).then_inc(shifted, 1)
                    dve.wait_ge(exps, 1)
                    dve.wait_ge(shifted, 1)
                    step(nc.vector.tensor_reduce(rt_s[:, 1], rt_p[:], AX.X, ALU.add))
                    step(nc.vector.reciprocal(rt_s[:, 2], rt_s[:, 1]))
                    step(nc.vector.tensor_tensor(rt_p[:], rt_p[:], bc(rt_s[:, 2], [P, NT, NE], 2), ALU.mult))
                    pick_best(step, rt_p[:], rt_m[:], rt_s[:, 0])
                    if not top2:
                        step(nc.vector.tensor_tensor(rt_w[:], rt_m[:], rt_p[:], ALU.mult))
                        return
                    step(nc.vector.scalar_tensor_tensor(rt_l[:].rearrange("p a b -> p (a b)"), flat(rt_m), -4.0,
                                                        flat(rt_p), ALU.mult, ALU.add))
                    pick_best(step, rt_l[:], rt_o[:], rt_s[:, 1])
                    step(nc.vector.tensor_tensor(rt_m[:], rt_m[:], rt_o[:], ALU.add))
                    step(nc.vector.tensor_tensor(rt_w[:], rt_m[:], rt_p[:], ALU.mult))
                    step(nc.vector.tensor_reduce(rt_s[:, 1], rt_w[:], AX.X, ALU.add))
                    step(nc.vector.tensor_scalar(rt_s[:, 1], rt_s[:, 1], floor_add, floor_max, ALU.add, ALU.max))
                    step(nc.vector.reciprocal(rt_s[:, 2], rt_s[:, 1]))
                    step(nc.vector.tensor_tensor(rt_w[:], rt_w[:], bc(rt_s[:, 2], [P, NT, NE], 2), ALU.mult))

        def mix_experts(tile_products, extra=None):
            with scratch("mixed", [P, 2, NE, C]) as mixed, \
                    ph.phase("tile_out", "tile_used", "dve_step") as (block, tile_out, tile_used, dve_step):
                @block.tensor
                def _(pe):
                    for t in range(NT):
                        if t >= 4:
                            pe.wait_ge(tile_used, t - 3)
                        tile_products(t, psum[:, (t % 4) * 512:(t % 4 + 1) * 512]).then_inc(tile_out, 1)

                @block.vector
                def _(dve):
                    step = Steps(dve, dve_step)
                    for t in range(NT):
                        dve.wait_ge(tile_out, t + 1)
                        if t >= 2:
                            dve.wait_ge(dve_step, t - 1)
                        o = psum[:, (t % 4) * 512:(t % 4 + 1) * 512].rearrange("p (e c) -> p e c", c=C)
                        nc.vector.tensor_tensor(mixed[:, t % 2], o, bc(rt_w[:, t], [P, NE, C], 2),
                                                ALU.mult).then_inc(tile_used, 1)
                        dve.wait_ge(tile_used, t + 1)
                        nc.vector.tensor_reduce(tmp[:, t], mixed[:, t % 2].rearrange("p e c -> p c e"),
                                                AX.X, ALU.add).then_inc(dve_step, 1)
                    step.n = NT
                    dve.wait_ge(dve_step, NT)
                    step(nc.vector.tensor_tensor(flat(h_tok), flat(h_tok), flat(tmp), ALU.add))
                    if extra is not None:
                        step(nc.vector.tensor_tensor(flat(h_tok), flat(h_tok), flat(extra), ALU.add))

        def attention(n_heads, hd, k_row, scale, q_of, k_of, v_of, out_of, buf):
            q_h, k_h, v_h, qT, kT, neg_max, probsT, r_sum = buf
            kk = k_row + 1
            w_of = [(t + 1) * P for t in range(NT)]
            start_of = [sum(NP - P * j for j in range(t)) for t in range(NT)]
            per_bank = 512 // (hd + 1)

            def o_of(t):
                b = D + (t // per_bank) * 512 + (t % per_bank) * (hd + 1)
                return psum[:, b:b + hd + 1]

            with nc.Fori(0, n_heads) as h:
                with ph.phase("head_in", "q_turned", "k_turned", "qT_out", "kT_out", "scores", "maxed",
                              "max_turned", "max_row", "scoresT", "exped", "weighed", "dve_step") as (
                        block, head_in, q_turned, k_turned, qT_out, kT_out, scores, maxed,
                        max_turned, max_row, scoresT, exped, weighed, dve_step):
                    @block.vector
                    def _(dve):
                        nc.vector.tensor_copy(q_h[:, :, 0:hd], q_of(h)).then_inc(head_in, 1)
                        nc.vector.tensor_copy(k_h[:, :, 0:hd], k_of(h)).then_inc(head_in, 1)
                        nc.vector.tensor_copy(v_h[:, :, 0:hd], v_of(h)).then_inc(head_in, 1)
                        for t in range(NT):
                            r = A if t % 2 == 0 else B
                            dve.wait_ge(scores, t + 1)
                            nc.vector.tensor_reduce(neg_max[:, t:t + 1], psum[:, r:r + w_of[t]], AX.X, ALU.max,
                                                    negate=True).then_inc(maxed, 1)
                        dve.wait_ge(max_turned, 1)
                        nc.vector.tensor_copy(qT[k_row:kk, :], psum[0:1, A:A + NP]).then_inc(max_row, 1)
                        dve.wait_ge(weighed, NT)
                        nb = -(-NT // per_bank)
                        for b in range(nb):
                            n = min(per_bank, NT - b * per_bank)
                            o = psum[:, D + b * 512:D + b * 512 + n * (hd + 1)].rearrange("p (t d) -> p t d", d=hd + 1)
                            nc.vector.reciprocal(r_sum[:, b * per_bank:b * per_bank + n],
                                                 o[:, :, hd]).then_inc(dve_step, 1)
                        dve.wait_ge(dve_step, nb)
                        for b in range(nb):
                            n = min(per_bank, NT - b * per_bank)
                            o = psum[:, D + b * 512:D + b * 512 + n * (hd + 1)].rearrange("p (t d) -> p t d", d=hd + 1)
                            nc.vector.tensor_tensor(out_of(h, b * per_bank, b * per_bank + n), o[:, :, 0:hd],
                                                    bc(r_sum[:, b * per_bank:b * per_bank + n], [P, n, hd], 2), ALU.mult)

                    @block.scalar
                    def _(act):
                        act.wait_ge(q_turned, 1)
                        nc.scalar.mul(qT[0:hd, :], psum[0:hd, A:A + NP], 1.0).then_inc(qT_out, 1)
                        act.wait_ge(k_turned, 1)
                        nc.scalar.mul(kT[0:hd, :], psum[0:hd, B:B + NP], 1.0).then_inc(kT_out, 1)
                        for t in range(NT):
                            r = B if t % 2 == 0 else A
                            act.wait_ge(scoresT, t + 1)
                            nc.scalar.activation(probsT[:, start_of[t]:start_of[t] + NP - t * P],
                                                 psum[:, r + t * P:r + NP], ACT.Exp, scale=scale).then_inc(exped, 1)

                    @block.tensor
                    def _(pe):
                        pe.wait_ge(head_in, 1)
                        turn_tiles(A, q_h, hd).then_inc(q_turned, 1)
                        pe.wait_ge(head_in, 2)
                        turn_tiles(B, k_h, hd).then_inc(k_turned, 1)
                        pe.wait_ge(qT_out, 1)
                        pe.wait_ge(kT_out, 1)
                        for t in range(NT):
                            r = A if t % 2 == 0 else B
                            if t >= 2:
                                pe.wait_ge(maxed, t - 1)
                            for a, b in CHUNKS:
                                b = min(b, w_of[t])
                                if a >= b:
                                    continue
                                full = min(b, t * P)
                                if a < full:
                                    nc.tensor.matmul(psum[:, r + a:r + full], qT[0:hd, t * P:(t + 1) * P],
                                                     kT[0:hd, a:full], start=True, stop=True)
                                if full < b:
                                    nc.tensor.matmul(psum[:, r + full:r + b], qT[0:hd, t * P:(t + 1) * P],
                                                     kT[0:hd, full:b], start=True, stop=False)
                                    last = nc.tensor.matmul(psum[:, r + full:r + b], ident, after,
                                                            start=False, stop=True)
                            last.then_inc(scores, 1)
                        pe.wait_ge(maxed, NT)
                        for t in range(NT):
                            last = nc.tensor.transpose(psum[0:1, A + t * P:A + (t + 1) * P],
                                                       neg_max[:, t:t + 1], ident)
                        last.then_inc(max_turned, 1)
                        pe.wait_ge(max_row, 1)
                        pe.wait_ge(head_in, 3)

                        def weigh(t):
                            pe.wait_ge(exped, t + 1)
                            for j in range(t + 1):
                                s = start_of[j] + (t - j) * P
                                m = nc.tensor.matmul(o_of(t), probsT[:, s:s + P], v_h[:, j, :],
                                                     start=(j == 0), stop=(j == t))
                            m.then_inc(weighed, 1)

                        for t in range(NT):
                            r = B if t % 2 == 0 else A
                            if t >= 2:
                                pe.wait_ge(exped, t - 1)
                            for a, b in CHUNKS:
                                a = max(a, t * P)
                                if a >= b:
                                    continue
                                full = a
                                if a == t * P:
                                    full = a + P
                                    nc.tensor.matmul(psum[:, r + a:r + full], kT[0:kk, t * P:(t + 1) * P],
                                                     qT[0:kk, a:full], start=True, stop=False)
                                    last = nc.tensor.matmul(psum[:, r + a:r + full], ident, afterT,
                                                            start=False, stop=True)
                                if full < b:
                                    last = nc.tensor.matmul(psum[:, r + full:r + b], kT[0:kk, t * P:(t + 1) * P],
                                                            qT[0:kk, full:b], start=True, stop=True)
                            last.then_inc(scoresT, 1)
                            if t >= 1:
                                weigh(t - 1)
                        weigh(NT - 1)
                ph.close_loop()

        def attention_buffers(c2, hd, k_row):
            def b(name, shape):
                return c2.enter_context(scratch(name, shape))
            return [b("q_h", [P, NT, hd]), b("k_h", [P, NT, hd]), b("v_h", [P, NT, hd + 1]), b("qT", [k_row + 1, NP]),
                    b("kT", [k_row + 1, NP]), b("neg_max", [P, NT]),
                    b("probsT", [P, sum(NP - P * j for j in range(NT))]), b("r_sum", [P, NT])]

        def init_attention(buf, hd, k_row):
            q_h, k_h, v_h, qT, kT = buf[:5]
            with ph.phase("dve_step") as (block, dve_step):
                @block.vector
                def _(dve):
                    step = Steps(dve, dve_step)
                    nc.vector.memset(v_h[:, :, hd:hd + 1], 1.0)
                    if k_row > hd:
                        nc.vector.memset(qT[:], 0.0)
                        step(nc.vector.memset(kT[0:k_row, :], 0.0))
                    nc.vector.memset(kT[k_row:k_row + 1, :], 1.0)

        def tokens(b):
            U = N_TIME // 2
            with scratch("series", [P, U + 4, N_VAR]) as series, \
                    scratch("edge", [P, N_VAR]) as edge, \
                    scratch("hT", [C, NP]) as hT, \
                    ph.phase("series_in", "padded", "embedded", "hT_out", "turned") as (
                        block, series_in, padded, embedded, hT_out, turned):
                @block.sync
                def _(sp):
                    xb = io["x"][bass.ds(b, 1)].rearrange("a c (u r) v -> (a r) c u v", r=2)
                    for r in range(2):
                        sp.dma_start(series[r * C:(r + 1) * C, 0:U, :], xb[r]).then_inc(series_in, 16)
                        sp.dma_start(edge[r * C:(r + 1) * C, :],
                                     io["x"][bass.ds(b, 1), :, N_TIME - 1, :].rearrange("a c v -> (a c) v")
                                     ).then_inc(series_in, 16)
                    sp.dma_start(hT[:, 0:1], io["cls"]).then_inc(series_in, 16)

                @block.vector
                def _(dve):
                    nc.vector.memset(hT[:, N_TOK:NP], 0.0)
                    dve.wait_ge(series_in, 80)
                    nc.vector.tensor_copy(series[:, U:U + 4, :], bc(edge[:], [P, 4, N_VAR], 1)).then_inc(padded, 1)
                    dve.wait_ge(embedded, 1)
                    nc.vector.tensor_copy(hT[:, 1:N_TOK], psum[0:C, A:A + N_TOK - 1]).then_inc(hT_out, 1)
                    dve.wait_ge(turned, 1)
                    nc.vector.tensor_copy(flat(h_tok), psum[:, B:B + NT * C])

                @block.tensor
                def _(pe):
                    pe.wait_ge(padded, 1)
                    for half in range(2):
                        o = psum[0:C, A + half * 512:A + (half + 1) * 512]
                        for u in range(8):
                            rhs = series[:, u:u + 4 * (N_PATCH - 1) + 1:4, half * 32:(half + 1) * 32]
                            last = nc.tensor.matmul(o, w_tok[:, u, :], rhs.rearrange("p n v -> p v n"),
                                                    start=(u == 0), stop=(u == 7))
                    last.then_inc(embedded, 1)
                    pe.wait_ge(hT_out, 1)
                    for t in range(NT):
                        last = nc.tensor.transpose(psum[:, B + t * C:B + (t + 1) * C],
                                                   hT[:, t * P:(t + 1) * P], ident[0:C, 0:C])
                    last.then_inc(turned, 1)

        def phasor():
            layer_norm()
            with ExitStack() as c2:
                def b(name, shape):
                    return c2.enter_context(scratch(name, shape))
                hid_p, hid_h = b("hid_p", [P, NP]), b("hid_h", [P, NP])
                pre = b("pre", [P, NT, 160])
                val = b("val", [P, NT, C])
                half_sin, half_cos = b("half_sin", [P, NT, 96]), b("half_cos", [P, NT, 96])
                feat = b("feat", [P, 2, NT, P])
                featT = b("featT", [P, 2, NP])
                rad = b("rad", [P, 4, NT, 32])
                ret = b("ret", [P, NT, C])
                local = b("local", [P, 2, P])
                memory = b("memory", [P, 2, C])
                with ph.phase("hid_in", "hid_out", "pre_in", "val_in") as (block, hid_in, hid_out, pre_in, val_in):
                    @block.tensor
                    def _(pe):
                        columns(A, P, [(a_w1p, xT[:])]).then_inc(hid_in, 1)
                        columns(B, P, [(a_w1h, xT[:])]).then_inc(hid_in, 1)
                        for t in range(NT):
                            o = psum[:, D + t * C:D + (t + 1) * C]
                            nc.tensor.matmul(o, xT[:, t * P:(t + 1) * P], a_vw, start=True, stop=False)
                            last = nc.tensor.matmul(o, ones[0:1, :], a_vb, start=False, stop=True)
                        last.then_inc(val_in, 1)
                        pe.wait_ge(hid_out, 2)
                        for t in range(NT):
                            o = A + (t // 3) * 512 + (t % 3) * 160
                            s = slice(t * P, (t + 1) * P)
                            nc.tensor.matmul(psum[:, o:o + 96], hid_p[:, s], a_w2p[:], start=True, stop=False)
                            nc.tensor.matmul(psum[:, o + 96:o + 160], hid_h[:, s], a_w2h[:], start=False, stop=False)
                            last = nc.tensor.matmul(psum[:, o:o + 160], ones[0:1, :], a_b2, start=False, stop=True)
                        last.then_inc(pre_in, 1)

                    @block.scalar
                    def _(act):
                        act.wait_ge(hid_in, 1)
                        nc.scalar.activation(hid_p[:], psum[:, A:A + NP], ACT.Gelu, bias=a_b1p).then_inc(hid_out, 1)
                        act.wait_ge(hid_in, 2)
                        nc.scalar.activation(hid_h[:], psum[:, B:B + NP], ACT.Gelu, bias=a_b1h).then_inc(hid_out, 1)
                        act.wait_ge(pre_in, 1)
                        for j in range(3):
                            o = psum[:, A + j * 512:A + j * 512 + 480].rearrange("p (t f) -> p t f", f=160)
                            nc.scalar.activation(pre[:, 3 * j:3 * j + 3, :], o, ACT.Tanh)

                    @block.vector
                    def _(dve):
                        dve.wait_ge(val_in, 1)
                        nc.vector.tensor_copy(flat(val), psum[:, D:D + NT * C])

                with ph.phase("angles", "radii2", "sines", "radii", "featured", "turned", "dve_step") as (
                        block, angles, radii2, sines, radii, featured, turned, dve_step):
                    ang = pre[:, :, 0:96]
                    pair = pre[:, :, 96:160].rearrange("p t (n c) -> p t n c", c=2)

                    @block.vector
                    def _(dve):
                        step = Steps(dve, dve_step)
                        nc.vector.scalar_tensor_tensor(half_cos[:], ang, -1.0, ang, ALU.mult, ALU.max).then_inc(angles, 1)
                        step(nc.vector.tensor_scalar(pair, pair, 0.9, None, ALU.mult))
                        step(nc.vector.tensor_tensor(rad[:, 0], pair[:, :, :, 0], pair[:, :, :, 0], ALU.mult))
                        step(nc.vector.tensor_tensor(rad[:, 1], pair[:, :, :, 1], pair[:, :, :, 1], ALU.mult))
                        step(nc.vector.tensor_tensor(rad[:, 0], rad[:, 0], rad[:, 1], ALU.add))
                        step(nc.vector.tensor_scalar(rad[:, 1], rad[:, 0], 0.0, None, ALU.is_equal))
                        nc.vector.tensor_tensor(pair[:, :, :, 0], pair[:, :, :, 0], rad[:, 1], ALU.add).then_inc(radii2, 1)
                        dve.wait_ge(radii2, 1)
                        dve.wait_ge(radii, 1)
                        step(nc.vector.tensor_tensor(rad[:, 3], rad[:, 2], rad[:, 1], ALU.add))
                        step(nc.vector.reciprocal(rad[:, 3], rad[:, 3]))
                        step(nc.vector.tensor_scalar(rad[:, 2], rad[:, 2], -1.0, 1.0, ALU.mult, ALU.add))
                        step(nc.vector.tensor_tensor(rad[:, 3], rad[:, 3], rad[:, 2], ALU.mult))
                        for kq in range(2):
                            s = slice(kq * 16, (kq + 1) * 16)
                            nc.vector.tensor_tensor(feat[:, kq, :, NPER:64], pair[:, :, s, 0], rad[:, 3, :, s], ALU.mult)
                            nc.vector.tensor_tensor(feat[:, kq, :, 64 + NPER:P], pair[:, :, s, 1], rad[:, 3, :, s], ALU.mult)
                        dve.wait_ge(sines, 1)
                        step(nc.vector.scalar_tensor_tensor(half_cos[:], half_cos[:], 2.0, half_sin[:], ALU.mult, ALU.mult))
                        step(nc.vector.tensor_tensor(half_sin[:], half_sin[:], half_sin[:], ALU.mult))
                        for kq in range(2):
                            s = slice(kq * NPER, (kq + 1) * NPER)
                            step(nc.vector.tensor_copy(feat[:, kq, :, 64:64 + NPER], half_cos[:, :, s]))
                            step(nc.vector.tensor_scalar(feat[:, kq, :, 0:NPER], half_sin[:, :, s], -2.0, 1.0,
                                                         ALU.mult, ALU.add))
                        nc.vector.tensor_copy(stat[:, 0], stat[:, 4]).then_inc(featured, 1)

                    @block.scalar
                    def _(act):
                        act.wait_ge(radii2, 1)
                        nc.scalar.activation(rad[:, 2], rad[:, 0], ACT.Sqrt).then_inc(radii, 1)
                        nc.scalar.activation(half_sin[:], ang, ACT.Sin, scale=math.pi / 2)
                        nc.scalar.activation(half_cos[:], half_cos[:], ACT.Sin, scale=-math.pi / 2,
                                             bias=eps[:, 2:3]).then_inc(sines, 1)
                        for kq in range(2):
                            act.wait_ge(turned, kq + 1)
                            r = A if kq == 0 else B
                            nc.scalar.copy(featT[:, kq, :], psum[:, r:r + NP])

                    @block.tensor
                    def _(pe):
                        pe.wait_ge(featured, 1)
                        turn_tiles(A, feat[:, 0], P).then_inc(turned, 1)
                        turn_tiles(B, feat[:, 1], P).then_inc(turned, 1)

                with ph.phase("scored", "masked", "grown", "kept", "read", "read_out", "dve_step") as (
                        block, scored, masked, grown, kept, read, read_out, dve_step):
                    @block.tensor
                    def _(pe):
                        for t in range(NT):
                            s = slice(t * P, (t + 1) * P)
                            if t >= 2:
                                pe.wait_ge(masked, t - 1)
                            nc.tensor.matmul(psum[:, A + (t % 2) * 512:A + (t % 2) * 512 + P], featT[:, 0, s],
                                             featT[:, 1, s], start=True, stop=True).then_inc(scored, 1)
                            if t >= 1:
                                pe.wait_ge(kept, t)
                            nc.tensor.matmul(psum[:, B:B + C], feat[:, 0, t, :], val[:, t, :],
                                             start=True, stop=True).then_inc(grown, 1)
                            pe.wait_ge(masked, t + 1)
                            if t >= 2:
                                pe.wait_ge(read_out, t - 1)
                            o = psum[:, D + (t % 2) * 512:D + (t % 2) * 512 + C]
                            m = nc.tensor.matmul(o, local[:, t % 2, :], val[:, t, :], start=True, stop=(t == 0))
                            if t >= 1:
                                m = nc.tensor.matmul(o, featT[:, 1, s], memory[:, (t - 1) % 2, :], start=False, stop=True)
                            m.then_inc(read, 1)

                    @block.vector
                    def _(dve):
                        for t in range(NT):
                            dve.wait_ge(scored, t + 1)
                            if t >= 2:
                                dve.wait_ge(read, t - 1)
                            nc.vector.tensor_tensor(local[:, t % 2, :], psum[:, A + (t % 2) * 512:A + (t % 2) * 512 + P],
                                                    upto_q, ALU.mult).then_inc(masked, 1)
                            dve.wait_ge(grown, t + 1)
                            if t == 0:
                                nc.vector.tensor_copy(memory[:, 0, :], psum[:, B:B + C]).then_inc(kept, 1)
                            else:
                                dve.wait_ge(kept, t)
                                nc.vector.tensor_tensor(memory[:, t % 2, :], memory[:, (t - 1) % 2, :], psum[:, B:B + C],
                                                        ALU.add).then_inc(kept, 1)
                            dve.wait_ge(read, t + 1)
                            nc.vector.tensor_scalar(ret[:, t, :], psum[:, D + (t % 2) * 512:D + (t % 2) * 512 + C],
                                                    pos_norm[:, t:t + 1], None, ALU.mult).then_inc(read_out, 1)
                layer_norm(src=ret, dst=y_tok, want_T=False)
                with ph.phase("scaled", "turned", "dve_step") as (block, scaled, turned, dve_step):
                    @block.vector
                    def _(dve):
                        step = Steps(dve, dve_step)
                        step(nc.vector.tensor_tensor(y_tok[:], y_tok[:], bc(a_g, [P, NT, C], 1), ALU.mult))
                        nc.vector.tensor_tensor(y_tok[:], y_tok[:], bc(a_b, [P, NT, C], 1), ALU.add).then_inc(scaled, 1)

                    @block.tensor
                    def _(pe):
                        pe.wait_ge(scaled, 1)
                        turn_tiles(A, y_tok, C).then_inc(turned, 1)

                    @block.scalar
                    def _(act):
                        act.wait_ge(turned, 1)
                        nc.scalar.copy(yT[:], psum[0:C, A:A + NP])
            project_add([yT], [a_ow], a_ob, extra=x_tok)

        def turn_y(src):
            with ph.phase("turned") as (block, turned):
                @block.tensor
                def _(pe):
                    turn_tiles(A, src, C).then_inc(turned, 1)

                @block.scalar
                def _(act):
                    act.wait_ge(turned, 1)
                    nc.scalar.copy(yT[:], psum[0:C, A:A + NP])

        def rotary_moe():
            layer_norm()
            layer_norm(rms_weight=f_ln1, src=x_tok, dst=y_tok)
            with ExitStack() as c2:
                def b(name, shape):
                    return c2.enter_context(scratch(name, shape))
                qkv = b("qkv", [P, NT, P])
                q_all, k_all, v_all = b("q_all", [P, NT, C]), b("k_all", [P, NT, C]), b("v_all", [P, NT, C])
                rot = b("rot", [P, NT, 6, 16])
                buf = attention_buffers(c2, 16, 32)
                with ph.phase("qkv_in", "dve_step") as (block, qkv_in, dve_step):
                    @block.tensor
                    def _(pe):
                        for t in range(NT):
                            last = nc.tensor.matmul(psum[:, A + t * P:A + (t + 1) * P], xT[:, t * P:(t + 1) * P], f_qkv,
                                                    start=True, stop=True)
                        last.then_inc(qkv_in, 1)

                    @block.vector
                    def _(dve):
                        step = Steps(dve, dve_step)
                        dve.wait_ge(qkv_in, 1)
                        step(nc.vector.tensor_copy(flat(qkv), psum[:, A:A + NP]))
                        qk = qkv[:, :, 0:96].rearrange("p t (h d) -> p t h d", d=16)
                        step(nc.vector.tensor_tensor(rot[:, :, :, 0:8], qk[:, :, :, 8:16],
                                                     bc(sin[:, :, 0:8], [P, NT, 6, 8], 2), ALU.mult))
                        step(nc.vector.tensor_tensor(rot[:, :, :, 8:16], qk[:, :, :, 0:8],
                                                     bc(sin[:, :, 8:16], [P, NT, 6, 8], 2), ALU.mult))
                        step(nc.vector.tensor_tensor(qk, qk, bc(cos, [P, NT, 6, 16], 2), ALU.mult))
                        r6 = rot[:].rearrange("p t h d -> p t (h d)")
                        nc.vector.tensor_tensor(q_all[:], qkv[:, :, 0:64], r6[:, :, 0:64], ALU.add)
                        for h in range(4):
                            g = h // 2
                            nc.vector.tensor_tensor(k_all[:, :, h * 16:h * 16 + 16], qkv[:, :, 64 + g * 16:80 + g * 16],
                                                    r6[:, :, 64 + g * 16:80 + g * 16], ALU.add)
                            nc.vector.tensor_copy(v_all[:, :, h * 16:h * 16 + 16], qkv[:, :, 96 + g * 16:112 + g * 16])
                init_attention(buf, 16, 32)
                attention(4, 16, 32, 0.25, lambda h: q_all[:, :, bass.ds(h * 16, 16)],
                          lambda h: k_all[:, :, bass.ds(h * 16, 16)], lambda h: v_all[:, :, bass.ds(h * 16, 16)],
                          lambda h, t0, t1: y_tok[:, t0:t1, bass.ds(h * 16, 16)], buf)
            turn_y(y_tok)
            with ph.phase("projected", "dve_step") as (block, projected, dve_step):
                @block.tensor
                def _(pe):
                    for t in range(NT):
                        last = nc.tensor.matmul(psum[:, A + t * C:A + (t + 1) * C], yT[:, t * P:(t + 1) * P], f_wo,
                                                start=True, stop=True)
                    last.then_inc(projected, 1)

                @block.vector
                def _(dve):
                    dve.wait_ge(projected, 1)
                    nc.vector.tensor_tensor(flat(x_tok), flat(x_tok), psum[:, A:A + NT * C], ALU.add)
            layer_norm(rms_weight=f_ln2, src=x_tok, dst=y_tok)
            route(lambda t, o: nc.tensor.matmul(o, xT[:, t * P:(t + 1) * P], f_router, start=True, stop=True),
                  True, 1e-9, 0.0)
            with scratch("gate", [HB, 2, NP]) as gate, \
                    scratch("hid", [HB, 2, NP]) as hid, \
                    scratch("part", [P, 2, NT, C]) as part, \
                    ph.phase("gate_in", "up_in", "gated", "hid_out", "expert_out", "weighed", "dve_step") as (
                        block, gate_in, up_in, gated, hid_out, expert_out, weighed, dve_step):
                @block.tensor
                def _(pe):
                    def down(e):
                        pe.wait_ge(hid_out, 2 * e + 2)
                        if e >= 1:
                            pe.wait_ge(weighed, e)
                        for t in range(NT):
                            o = psum[:, D + t * C:D + (t + 1) * C]
                            for j in range(2):
                                last = nc.tensor.matmul(o, hid[:, j, t * P:(t + 1) * P], f_w2[:, 2 * e + j, :],
                                                        start=(j == 0), stop=(j == 1))
                        last.then_inc(expert_out, 1)

                    for i in range(2 * NE):
                        w = slice(i * HB, (i + 1) * HB)
                        if i >= 1:
                            pe.wait_ge(gated, i)
                        columns(A, HB, [(f_w1[:, w], xT[:])]).then_inc(gate_in, 1)
                        if i >= 1:
                            pe.wait_ge(hid_out, i)
                        columns(B, HB, [(f_w3[:, w], xT[:])]).then_inc(up_in, 1)
                        if i % 2 == 1:
                            down(i // 2)

                @block.scalar
                def _(act):
                    for i in range(2 * NE):
                        act.wait_ge(gate_in, i + 1)
                        if i >= 2:
                            act.wait_ge(hid_out, i - 1)
                        nc.scalar.activation(gate[:, i % 2, :], psum[0:HB, A:A + NP], ACT.Silu).then_inc(gated, 1)

                @block.vector
                def _(dve):
                    for i in range(2 * NE):
                        e = i // 2
                        dve.wait_ge(gated, i + 1)
                        dve.wait_ge(up_in, i + 1)
                        if e >= 1:
                            dve.wait_ge(expert_out, e)
                        nc.vector.tensor_tensor(hid[:, i % 2, :], gate[:, i % 2, :], psum[0:HB, B:B + NP],
                                                ALU.mult).then_inc(hid_out, 1)
                        if i % 2 == 1:
                            dve.wait_ge(expert_out, e + 1)
                            o = psum[:, D:D + NT * C].rearrange("p (t c) -> p t c", c=C)
                            nc.vector.tensor_tensor(part[:, e % 2], o, bc(rt_w[:, :, e], [P, NT, C], 2),
                                                    ALU.mult).then_inc(weighed, 1)
                            dve.wait_ge(weighed, e + 1)
                            dve.wait_ge(dve_step, e) if e else None
                            nc.vector.tensor_tensor(flat(x_tok), flat(x_tok), part[:, e % 2].rearrange("p t c -> p (t c)"),
                                                    ALU.add).then_inc(dve_step, 1)
                    dve.wait_ge(dve_step, NE)
                    nc.vector.tensor_tensor(flat(h_tok), flat(h_tok), flat(x_tok), ALU.add)

        def state_space():
            layer_norm()
            with ExitStack() as c2:
                def b(name, shape):
                    return c2.enter_context(scratch(name, shape))
                xin = b("xin", [P, TAPS - 1 + NP])
                gz, u, dt, dtu, ys = b("gz", [P, NP]), b("u", [P, NP]), b("dt", [P, NP]), b("dtu", [P, NP]), b("ys", [P, NP])
                decay, drive, state, part = b("decay", [P, 2, NP]), b("drive", [P, 2, NP]), b("state", [P, 2, NP]), b("part", [P, 2, NP])
                with ph.phase("xz_in", "gate_out", "conv_done", "u_out", "dt_in", "pre_out", "e_out", "l_out",
                              "dve_step") as (block, xz_in, gate_out, conv_done, u_out, dt_in, pre_out, e_out, l_out,
                                              dve_step):
                    @block.tensor
                    def _(pe):
                        columns(A, P, [(m_in[:, 0:P], xT[:])]).then_inc(xz_in, 1)
                        columns(B, P, [(m_in[:, P:2 * P], xT[:])]).then_inc(xz_in, 1)
                        pe.wait_ge(u_out, 1)
                        columns(A, P, [(w_rep[:, 0, :], u[:])]).then_inc(dt_in, 1)

                    @block.scalar
                    def _(act):
                        act.wait_ge(xz_in, 2)
                        nc.scalar.activation(gz[:], psum[:, B:B + NP], ACT.Sigmoid).then_inc(gate_out, 1)
                        act.wait_ge(pre_out, 1)
                        nc.scalar.activation(gz[:], gz[:], ACT.Exp, scale=-1.0).then_inc(e_out, 1)
                        act.wait_ge(e_out, 1)
                        nc.scalar.activation(gz[:], gz[:], ACT.Ln, bias=ones[:, 0:1]).then_inc(l_out, 1)

                    @block.vector
                    def _(dve):
                        step = Steps(dve, dve_step)
                        nc.vector.memset(xin[:, 0:TAPS - 1], 0.0)
                        dve.wait_ge(xz_in, 1)
                        step(nc.vector.tensor_copy(xin[:, TAPS - 1:], psum[:, A:A + NP]))
                        step(nc.vector.tensor_scalar(u[:], xin[:, 0:NP], m_cw[:, 0:1], m_cb[:, 0:1], ALU.mult, ALU.add))
                        for k in range(1, TAPS):
                            step(nc.vector.scalar_tensor_tensor(u[:], xin[:, k:k + NP], m_cw[:, k:k + 1], u[:],
                                                                ALU.mult, ALU.add))
                        dve.wait_ge(gate_out, 1)
                        nc.vector.tensor_tensor(u[:], u[:], gz[:], ALU.mult).then_inc(u_out, 1)
                        dve.wait_ge(dt_in, 1)
                        step(nc.vector.tensor_scalar(dtu[:], psum[:, A:A + NP], m_wdt[:, 0:1], m_bdt[:, 0:1],
                                                     ALU.mult, ALU.add))
                        nc.vector.scalar_tensor_tensor(gz[:], dtu[:], -1.0, dtu[:], ALU.mult, ALU.max).then_inc(pre_out, 1)
                        dve.wait_ge(l_out, 1)
                        step(nc.vector.scalar_tensor_tensor(dt[:], dtu[:], 0.0, gz[:], ALU.max, ALU.add))
                        nc.vector.tensor_tensor(dtu[:], dt[:], u[:], ALU.mult)
                        nc.vector.tensor_scalar(ys[:], u[:], m_D[:, 0:1], None, ALU.mult)

                with ph.phase("decayed", "b_in", "c_in", "driven", "scanned", "shown", "summed") as (
                        block, decayed, b_in, c_in, driven, scanned, shown, summed):
                    @block.tensor
                    def _(pe):
                        for n in range(NSTATE):
                            if n >= 1:
                                pe.wait_ge(driven, n)
                            columns(A, P, [(w_rep[:, 1 + n, :], u[:])]).then_inc(b_in, 1)
                            if n >= 1:
                                pe.wait_ge(shown, n)
                            columns(B, P, [(w_rep[:, 1 + NSTATE + n, :], u[:])]).then_inc(c_in, 1)

                    @block.scalar
                    def _(act):
                        for n in range(NSTATE):
                            if n >= 2:
                                act.wait_ge(scanned, n - 1)
                            nc.scalar.activation(decay[:, n % 2, :], dt[:], ACT.Exp, scale=m_A[:, n:n + 1]).then_inc(decayed, 1)

                    @block.vector
                    def _(dve):
                        for n in range(NSTATE):
                            s = n % 2
                            dve.wait_ge(b_in, n + 1)
                            if n >= 2:
                                dve.wait_ge(scanned, n - 1)
                            nc.vector.tensor_tensor(drive[:, s, :], dtu[:], psum[:, A:A + NP], ALU.mult).then_inc(driven, 1)
                            dve.wait_ge(driven, n + 1)
                            dve.wait_ge(decayed, n + 1)
                            if n >= 2:
                                dve.wait_ge(shown, n - 1)
                            nc.vector.tensor_tensor_scan(state[:, s, :], decay[:, s, :], drive[:, s, :], 0.0,
                                                         ALU.mult, ALU.add).then_inc(scanned, 1)
                            dve.wait_ge(scanned, n + 1)
                            dve.wait_ge(c_in, n + 1)
                            if n >= 2:
                                dve.wait_ge(summed, n - 1)
                            nc.vector.tensor_tensor(part[:, s, :], state[:, s, :], psum[:, B:B + NP], ALU.mult).then_inc(shown, 1)

                    @block.gpsimd
                    def _(pool):
                        for n in range(NSTATE):
                            pool.wait_ge(shown, n + 1)
                            if n >= 1:
                                pool.wait_ge(summed, n)
                            nc.gpsimd.tensor_tensor(ys[:], ys[:], part[:, n % 2, :], ALU.add).then_inc(summed, 1)
                project_add([ys], [m_out], None)

        def product_keys():
            layer_norm()
            with ExitStack() as c2:
                def b(name, shape, dt=F32):
                    return c2.enter_context(scratch(name, shape, dt))
                q_all = b("q_all8", [P, NT, 512])
                kv_all = b("kv_all", [P, NT, PKH, P])
                with ExitStack() as c3:
                    def b3(name, shape, dt=F32):
                        return c3.enter_context(scratch(name, shape, dt))
                    qpkT = b3("qpkT", [P, 4, NP])
                    qt = b3("qt", [P, 4, P])
                    sim2 = b3("sim2", [P, 16, PKK])
                    best = b3("best", [P, 16, TOPK])
                    bidx = b3("bidx", [P, 16, TOPK], U32)
                    bidf = b3("bidf", [P, 16, TOPK])
                    cand, cand2, cidx = [b3(f"cand{i}", [P, PKH, NPAIR]) for i in range(3)]
                    fin = b3("fin", [P, PKH, TOPK])
                    fpos = b3("fpos", [P, PKH, TOPK], U32)
                    fposf = b3("fposf", [P, PKH, TOPK])
                    wgt = b3("wgt", [P, PKH, TOPK])
                    wsum = b3("wsum", [P, 2, PKH])
                    hot = b3("hot", [P, TOPK, NPAIR])
                    gidf = b3("gidf", [P, PKH, TOPK])
                    gidx = b3("gidx", [P, PKH, TOPK], U32)
                    rows = b3("rows", [P, 2, TOPK, P])
                    acc = b3("acc", [P, 2, P])
                    lastcol = b3("lastcol", [P, 2])
                    lastw = b3("lastw", [P, PKH])
                    lastix = b3("lastix", [P, 1], U32)

                    with ph.phase("q_in", "q_out") as (block, q_in, q_out):
                        @block.tensor
                        def _(pe):
                            for t in range(NT):
                                if t >= 2:
                                    pe.wait_ge(q_out, t - 1)
                                nc.tensor.matmul(psum[:, D + (t % 2) * 512:D + (t % 2 + 1) * 512], xT[:, t * P:(t + 1) * P],
                                                 k_wq, start=True, stop=True).then_inc(q_in, 1)
                            for c in range(4):
                                if c >= 2:
                                    pe.wait_ge(q_out, NT + c - 1)
                                columns(A if c % 2 == 0 else B, P, [(k_wqpk[:, c * P:(c + 1) * P], xT[:])]).then_inc(q_in, 1)

                        @block.scalar
                        def _(act):
                            for t in range(NT):
                                act.wait_ge(q_in, t + 1)
                                nc.scalar.mul(q_all[:, t, :], psum[:, D + (t % 2) * 512:D + (t % 2 + 1) * 512],
                                              C ** -0.5).then_inc(q_out, 1)
                            for c in range(4):
                                r = A if c % 2 == 0 else B
                                act.wait_ge(q_in, NT + c + 1)
                                nc.scalar.copy(qpkT[:, c, :], psum[:, r:r + NP]).then_inc(q_out, 1)

                    def search(dve, step, sims, exps_ready, shifted, found):
                        sim = psum[:, A:A + 16 * PKK].rearrange("p (g k) -> p g k", k=PKK)
                        dve.wait_ge(sims, 1)
                        G = range(2 * PKH)

                        def all_of(rng, f):
                            for g in rng:
                                ins = f(g)
                            step(ins)
                        all_of(G, lambda g: nc.vector.max(best[:, g, 0:8], sim[:, g, :]))
                        all_of(G, lambda g: nc.vector.match_replace(sim2[:, g, :], best[:, g, 0:8], sim[:, g, :], LOWEST))
                        all_of(G, lambda g: nc.vector.max(best[:, g, 8:16], sim2[:, g, :]))
                        all_of(G, lambda g: nc.vector.max_index(bidx[:, g, 0:8], best[:, g, 0:8], sim[:, g, :]))
                        all_of(G, lambda g: nc.vector.max_index(bidx[:, g, 8:16], best[:, g, 8:16], sim2[:, g, :]))
                        step(nc.vector.tensor_copy(flat(bidf), flat(bidx)))
                        step(nc.vector.tensor_scalar(bidf[:, PKH:, :], bidf[:, PKH:, :], float(PKK), None, ALU.mult))
                        step(nc.vector.tensor_tensor(bidf[:, 0:PKH, :], bidf[:, 0:PKH, :],
                                                     bc(headoff, [P, PKH, TOPK], 2), ALU.add))
                        for dst, src in ((cand, best), (cidx, bidf)):
                            for o, i0, i1, nj in PAIRS:
                                ni = i1 - i0
                                d = dst[:, :, o:o + ni * nj].rearrange("p h (i j) -> p h i j", j=nj)
                                ins = nc.vector.tensor_tensor(d, bc(src[:, 0:PKH, i0:i1], [P, PKH, ni, nj], 3),
                                                              bc(src[:, PKH:, 0:nj], [P, PKH, ni, nj], 2), ALU.add)
                        step(ins)
                        H = range(PKH)
                        all_of(H, lambda h: nc.vector.max(fin[:, h, 0:8], cand[:, h, :]))
                        all_of(H, lambda h: nc.vector.match_replace(cand2[:, h, :], fin[:, h, 0:8], cand[:, h, :], LOWEST))
                        all_of(H, lambda h: nc.vector.max(fin[:, h, 8:16], cand2[:, h, :]))
                        all_of(H, lambda h: nc.vector.max_index(fpos[:, h, 0:8], fin[:, h, 0:8], cand[:, h, :]))
                        all_of(H, lambda h: nc.vector.max_index(fpos[:, h, 8:16], fin[:, h, 8:16], cand2[:, h, :]))
                        nc.vector.tensor_tensor(wgt[:], fin[:], fin[:, :, 0:1].broadcast_to([P, PKH, TOPK]),
                                                ALU.subtract).then_inc(shifted, 1)
                        step(nc.vector.tensor_copy(flat(fposf), flat(fpos)))
                        for h in H:
                            s = hot[:]
                            step(nc.vector.tensor_tensor(s, bc(fposf[:, h, :], [P, TOPK, NPAIR], 2),
                                                         bc(iota, [P, TOPK, NPAIR], 1), ALU.is_equal))
                            step(nc.vector.tensor_tensor(s, s, bc(cidx[:, h, :], [P, TOPK, NPAIR], 1), ALU.mult))
                            step(nc.vector.tensor_reduce(gidf[:, h, :], s, AX.X, ALU.add))
                        nc.vector.tensor_copy(flat(gidx), flat(gidf)).then_inc(found, 1)
                        dve.wait_ge(exps_ready, 1)
                        step(nc.vector.tensor_reduce(wsum[:, 0], wgt[:], AX.X, ALU.add))
                        step(nc.vector.reciprocal(wsum[:, 1], wsum[:, 0]))
                        step(nc.vector.tensor_tensor(wgt[:], wgt[:], bc(wsum[:, 1], [P, PKH, TOPK], 2), ALU.mult))

                    def similarities(pe, staged, sims):
                        pe.wait_ge(staged, 1)
                        for c in range(4):
                            last = nc.tensor.matmul(psum[:, A + c * 256:A + (c + 1) * 256], qt[:, c, :], k_keys[:, c, :],
                                                    start=True, stop=True)
                        last.then_inc(sims, 1)

                    def stage_and_exp(act, tile_view, staged, shifted, exps):
                        nc.scalar.copy(qt[:], tile_view).then_inc(staged, 1)
                        act.wait_ge(shifted, 1)
                        nc.scalar.activation(wgt[:], wgt[:], ACT.Exp).then_inc(exps, 1)

                    with nc.Fori(0, NT - 1) as t:
                        with ph.phase("staged", "sims", "shifted", "exps", "found", "rows_even", "rows_odd", "rows_used",
                                      "acc_even", "acc_odd", "dve_step") as (
                                block, staged, sims, shifted, exps, found, rows_even, rows_odd, rows_used,
                                acc_even, acc_odd, dve_step):
                            @block.scalar
                            def _(act):
                                stage_and_exp(act, qpkT[:, :, bass.ds(t * P, P)], staged, shifted, exps)

                            @block.tensor
                            def _(pe):
                                similarities(pe, staged, sims)

                            @block.gpsimd
                            def _(pool):
                                pool.wait_ge(found, 1)
                                for h in range(PKH):
                                    if h >= 2:
                                        pool.wait_ge(rows_used, h - 1)
                                    for k in range(TOPK):
                                        nc.gpsimd.indirect_dma_start(
                                            out=rows[:, h % 2, k, :], out_offset=None, in_=io["k_table"],
                                            in_offset=bass.IndirectOffsetOnAxis(ap=gidx[:, h, k:k + 1], axis=0),
                                        ).then_inc(rows_even if h % 2 == 0 else rows_odd, 16)
                                for s in (rows_even, rows_odd):
                                    pool.wait_ge(s, 16 * TOPK * PKH // 2)
                                pool.wait_ge(rows_used, PKH)
                                nc.gpsimd.dma_reset()

                            @block.vector
                            def _(dve):
                                step = Steps(dve, dve_step)
                                search(dve, step, sims, exps, shifted, found)
                                for h in range(PKH):
                                    dve.wait_ge(rows_even if h % 2 == 0 else rows_odd, 16 * TOPK * (h // 2 + 1))
                                    for k in range(TOPK):
                                        s, sem = k % 2, (acc_even, acc_odd)[k % 2]
                                        n = (TOPK // 2) * h + k // 2
                                        if n:
                                            dve.wait_ge(sem, n)
                                        if k < 2:
                                            if h and k == 0:
                                                dve.wait_ge(rows_used, h)
                                            nc.vector.tensor_scalar(acc[:, s], rows[:, h % 2, k, :], wgt[:, h, k:k + 1],
                                                                    None, ALU.mult).then_inc(sem, 1)
                                        else:
                                            nc.vector.scalar_tensor_tensor(acc[:, s], rows[:, h % 2, k, :],
                                                                           wgt[:, h, k:k + 1], acc[:, s],
                                                                           ALU.mult, ALU.add).then_inc(sem, 1)
                                    for sem in (acc_even, acc_odd):
                                        dve.wait_ge(sem, (TOPK // 2) * (h + 1))
                                    nc.vector.tensor_tensor(kv_all[:, bass.ds(t, 1), h, :].rearrange("p a d -> p (a d)"),
                                                            acc[:, 0], acc[:, 1], ALU.add).then_inc(rows_used, 1)
                        ph.close_loop()

                    with ph.phase("staged", "sims", "shifted", "exps", "found", "stood", "last_ix", "last_rows", "last_in",
                                  "dve_step", "cleared") as (block, staged, sims, shifted, exps, found, stood, last_ix,
                                                             last_rows, last_in, dve_step, cleared):
                        @block.scalar
                        def _(act):
                            stage_and_exp(act, qpkT[:, :, (NT - 1) * P:NP], staged, shifted, exps)

                        @block.tensor
                        def _(pe):
                            similarities(pe, staged, sims)
                            pe.wait_ge(found, 2)
                            nc.tensor.transpose(psum[:, B:B + 1], gidf[0:1].rearrange("p h k -> p (h k)"), ident[0:1, 0:1])
                            nc.tensor.transpose(psum[:, B + 1:B + 2], wgt[0:1].rearrange("p h k -> p (h k)"),
                                                ident[0:1, 0:1]).then_inc(stood, 1)
                            pe.wait_ge(last_ix, 2)
                            pe.wait_ge(last_rows, 16)
                            for h in range(PKH):
                                m = nc.tensor.matmul(psum[0:1, D + h * P:D + (h + 1) * P], lastw[:, h:h + 1], rows[:, 0, 0, :],
                                                     start=True, stop=True)
                            m.then_inc(last_in, 1)

                        @block.gpsimd
                        def _(pool):
                            pool.wait_ge(last_ix, 1)
                            nc.gpsimd.indirect_dma_start(out=rows[:, 0, 0, :], out_offset=None, in_=io["k_table"],
                                                         in_offset=bass.IndirectOffsetOnAxis(ap=lastix[:, 0:1], axis=0),
                                                         ).then_inc(last_rows, 16)
                            pool.wait_ge(last_rows, 16)
                            nc.gpsimd.dma_reset()

                        @block.vector
                        def _(dve):
                            step = Steps(dve, dve_step)
                            nc.vector.memset(kv_all[:, NT - 1], 0.0).then_inc(cleared, 1)
                            search(dve, step, sims, exps, shifted, found)
                            nc.vector.memset(lastcol[:], 0.0).then_inc(found, 1)
                            dve.wait_ge(found, 2)
                            dve.wait_ge(stood, 1)
                            nc.vector.tensor_copy(lastix[:], psum[:, B:B + 1]).then_inc(last_ix, 1)
                            step(nc.vector.tensor_copy(lastcol[:, 0:1], psum[:, B + 1:B + 2]))
                            nc.vector.tensor_scalar(lastw[:], headrow, lastcol[:, 0:1], None, ALU.mult).then_inc(last_ix, 1)
                            dve.wait_ge(last_in, 1)
                            dve.wait_ge(cleared, 1)
                            nc.vector.tensor_copy(kv_all[0:1, NT - 1].rearrange("p h d -> p (h d)"), psum[0:1, D:D + PKH * P])

                y_all = q_all
                with ExitStack() as c4:
                    buf = attention_buffers(c4, C, C)
                    init_attention(buf, C, C)
                    attention(8, C, C, 1.0, lambda h: q_all[:, :, bass.ds(h * C, C)],
                              lambda h: kv_all[:, :, bass.ds(h, 1), 0:C].rearrange("p t a d -> p t (a d)"),
                              lambda h: kv_all[:, :, bass.ds(h, 1), C:P].rearrange("p t a d -> p t (a d)"),
                              lambda h, t0, t1: y_all[:, t0:t1, bass.ds(h * C, C)], buf)
                with scratch("yaT", [P, 4, NP]) as yaT:
                    with ph.phase("turned", "turned_out") as (block, turned, turned_out):
                        @block.tensor
                        def _(pe):
                            for c in range(4):
                                if c >= 2:
                                    pe.wait_ge(turned_out, c - 1)
                                turn_tiles(A if c % 2 == 0 else B, y_all[:, :, c * P:(c + 1) * P], P).then_inc(turned, 1)

                        @block.scalar
                        def _(act):
                            for c in range(4):
                                r = A if c % 2 == 0 else B
                                act.wait_ge(turned, c + 1)
                                nc.scalar.copy(yaT[:, c, :], psum[:, r:r + NP]).then_inc(turned_out, 1)
                    project_add([yaT[:, c] for c in range(4)], [k_wo[:, c] for c in range(4)], None)

        def slices():
            layer_norm()
            with ExitStack() as c2:
                def b(name, shape):
                    return c2.enter_context(scratch(name, shape))
                t_tok = b("t_tok", [P, NT, C + 1])
                tT = b("tT", [C, NP])
                sw = b("sw", [P, NT, 8, C])
                swT = b("swT", [P, 4, NP])
                red = b("red", [P, NT, 2, 8])
                tokn = b("tokn", [P, 4, C])
                nrm = b("nrm", [P, 2, 4])
                tokT = b("tokT", [C, 512])
                qs, ks = b("qs", [8, 512]), b("ks", [8, 512])
                vs = b("vs", [C, 8, 8])
                att = b("att", [C, 8, C])
                attT = b("attT", [C, 8, C])
                ared = b("ared", [C, 2, 8])
                obd = b("obd", [P, 4, C])
                oT = b("oT", [C, NP])
                with ph.phase("t_in", "t_out", "logit", "scaled", "swept", "exped", "sw_out", "dve_step", "pool_step") as (
                        block, t_in, t_out, logit, scaled, swept, exped, sw_out, dve_step, pool_step):
                    @block.tensor
                    def _(pe):
                        columns(A, C, [(s_win, xT[:])]).then_inc(t_in, 1)
                        for t in range(NT):
                            o = psum[:, D + t * C:D + (t + 1) * C]
                            nc.tensor.matmul(o, xT[:, t * P:(t + 1) * P], s_win, start=True, stop=False)
                            last = nc.tensor.matmul(o, ones[0:1, :], s_bin_row, start=False, stop=True)
                        last.then_inc(t_in, 1)
                        pe.wait_ge(t_out, 1)
                        for t in range(NT):
                            if t >= 2:
                                pe.wait_ge(scaled, t - 1)
                            o = psum[:, B + (t % 2) * 512:B + (t % 2 + 1) * 512]
                            nc.tensor.matmul(o, tT[:, t * P:(t + 1) * P], s_slice[:], start=True, stop=False)
                            nc.tensor.matmul(o, ones[0:1, :], s_bslice, start=False, stop=True).then_inc(logit, 1)

                    @block.scalar
                    def _(act):
                        act.wait_ge(t_in, 1)
                        nc.scalar.activation(tT[:], psum[0:C, A:A + NP], ACT.Identity, bias=s_bin_col).then_inc(t_out, 1)
                        for t in range(NT):
                            act.wait_ge(swept, t + 1)
                            nc.scalar.activation(sw[:, t], sw[:, t], ACT.Exp).then_inc(exped, 1)

                    @block.vector
                    def _(dve):
                        dve.wait_ge(t_in, 2)
                        o = psum[:, D:D + NT * C].rearrange("p (t c) -> p t c", c=C)
                        nc.vector.tensor_tensor(t_tok[:, :, 0:C], o, bc(valid, [P, NT, C], 2), ALU.mult)
                        nc.vector.tensor_copy(t_tok[:, :, C], valid)
                        step = Steps(dve, dve_step)

                        def finish(t):
                            dve.wait_ge(exped, t + 1)
                            step(nc.vector.tensor_reduce(red[:, t, 1], sw[:, t], AX.X, ALU.add))
                            step(nc.vector.reciprocal(red[:, t, 1], red[:, t, 1]))
                            nc.vector.tensor_tensor(sw[:, t], sw[:, t], bc(red[:, t, 1], [P, 8, C], 2),
                                                    ALU.mult).then_inc(sw_out, 1)
                        for t in range(NT):
                            dve.wait_ge(logit, t + 1)
                            o = psum[:, B + (t % 2) * 512:B + (t % 2 + 1) * 512].rearrange("p (h g) -> p h g", g=C)
                            nc.vector.tensor_tensor(sw[:, t], o, bc(s_rtemp[:], [P, 8, C], 2), ALU.mult).then_inc(scaled, 1)
                            dve.wait_ge(scaled, t + 1)
                            step(nc.vector.tensor_reduce(red[:, t, 0], sw[:, t], AX.X, ALU.max))
                            nc.vector.tensor_tensor(sw[:, t], sw[:, t], bc(red[:, t, 0], [P, 8, C], 2),
                                                    ALU.subtract).then_inc(swept, 1)
                            if t >= 1:
                                finish(t - 1)
                        finish(NT - 1)

                with ph.phase("sliced", "normed", "turned", "tokT_out", "qkv_in", "qkv_out", "sim", "shifted", "exped",
                              "att_out", "att_turned", "attT_out", "mixed", "cleared", "obd_out", "sw_turned",
                              "swT_out", "dve_step") as (
                        block, sliced, normed, turned, tokT_out, qkv_in, qkv_out, sim, shifted, exped, att_out,
                        att_turned, attT_out, mixed, cleared, obd_out, sw_turned, swT_out, dve_step):
                    @block.tensor
                    def _(pe):
                        for c in range(4):
                            o = psum[:, A + c * 512:A + c * 512 + C + 1]
                            for t in range(NT):
                                last = nc.tensor.matmul(o, sw[:, t, 2 * c:2 * c + 2, :].rearrange("p h g -> p (h g)"),
                                                        t_tok[:, t, :], start=(t == 0), stop=(t == NT - 1))
                        last.then_inc(sliced, 1)
                        pe.wait_ge(normed, 1)
                        for c in range(4):
                            last = nc.tensor.transpose(psum[0:C, D + c * P:D + (c + 1) * P], tokn[:, c, :], ident)
                        last.then_inc(turned, 1)
                        pe.wait_ge(tokT_out, 1)
                        nc.tensor.matmul(psum[0:8, A:A + 512], s_qkvw[:, 0:8], tokT[:], start=True, stop=True)
                        nc.tensor.matmul(psum[0:8, A + 512:A + 1024], s_qkvw[:, 8:16], tokT[:], start=True, stop=True)
                        for h in range(8):
                            o = psum[0:C, A + 1024 + 8 * h:A + 1024 + 8 * h + 8]
                            nc.tensor.matmul(o, tokT[:, h * C:(h + 1) * C], s_qkvw[:, 16:24], start=True, stop=False)
                            last = nc.tensor.matmul(o, ones[0:1, 0:C], s_bv, start=False, stop=True)
                        last.then_inc(qkv_in, 1)
                        pe.wait_ge(qkv_out, 2)
                        for h in range(8):
                            last = nc.tensor.matmul(psum[0:C, B + h * C:B + (h + 1) * C], qs[:, h * C:(h + 1) * C],
                                                    ks[:, h * C:(h + 1) * C], start=True, stop=True)
                        last.then_inc(sim, 1)
                        pe.wait_ge(att_out, 1)
                        for h in range(8):
                            last = nc.tensor.transpose(psum[0:C, B + 512 + h * C:B + 512 + (h + 1) * C], att[:, h, :],
                                                       ident[0:C, 0:C])
                        last.then_inc(att_turned, 1)
                        pe.wait_ge(attT_out, 1)
                        for h in range(8):
                            last = nc.tensor.matmul(psum[0:C, B + 1024 + 8 * h:B + 1024 + 8 * h + 8], attT[:, h, :],
                                                    vs[:, h, :], start=True, stop=True)
                        last.then_inc(mixed, 1)
                        for c in range(4):
                            if c >= 1:
                                pe.wait_ge(swT_out, c)
                            turn_tiles(A, sw[:, :, 2 * c:2 * c + 2, :].rearrange("p t h g -> p t (h g)"), P).then_inc(sw_turned, 1)
                        pe.wait_ge(swT_out, 4)
                        pe.wait_ge(obd_out, 1)
                        columns(A, C, [(obd[:, c, :], swT[:, c, :]) for c in range(4)]).then_inc(sw_turned, 1)

                    @block.scalar
                    def _(act):
                        act.wait_ge(turned, 1)
                        nc.scalar.copy(tokT[:], psum[0:C, D:D + 512]).then_inc(tokT_out, 1)
                        act.wait_ge(qkv_in, 1)
                        nc.scalar.activation(qs[:], psum[0:8, A:A + 512], ACT.Identity, bias=s_bq)
                        nc.scalar.activation(ks[:], psum[0:8, A + 512:A + 1024], ACT.Identity, bias=s_bk).then_inc(qkv_out, 1)
                        act.wait_ge(shifted, 1)
                        nc.scalar.activation(att[:], att[:], ACT.Exp, scale=8 ** -0.5).then_inc(exped, 1)
                        act.wait_ge(att_turned, 1)
                        nc.scalar.copy(attT[:].rearrange("p h g -> p (h g)"), psum[0:C, B + 512:B + 1024]).then_inc(attT_out, 1)
                        for c in range(4):
                            act.wait_ge(sw_turned, c + 1)
                            nc.scalar.copy(swT[:, c, :], psum[:, A:A + NP]).then_inc(swT_out, 1)
                        act.wait_ge(sw_turned, 5)
                        nc.scalar.copy(oT[:], psum[0:C, A:A + NP])

                    @block.vector
                    def _(dve):
                        step = Steps(dve, dve_step)
                        nc.vector.memset(obd[:], 0.0).then_inc(cleared, 1)
                        dve.wait_ge(sliced, 1)
                        sl = psum[:, A:A + 4 * 512].rearrange("p (c f) -> p c f", f=512)
                        step(nc.vector.tensor_scalar(nrm[:, 0], sl[:, :, C], 1e-5, None, ALU.add))
                        step(nc.vector.reciprocal(nrm[:, 1], nrm[:, 0]))
                        step(nc.vector.tensor_tensor(tokn[:], sl[:, :, 0:C], bc(nrm[:, 1], [P, 4, C], 2), ALU.mult))
                        nc.vector.tensor_tensor(tokn[:], tokn[:], ownhead, ALU.mult).then_inc(normed, 1)
                        dve.wait_ge(qkv_in, 1)
                        nc.vector.tensor_copy(vs[:].rearrange("p h d -> p (h d)"),
                                              psum[0:C, A + 1024:A + 1024 + 64]).then_inc(qkv_out, 1)
                        dve.wait_ge(sim, 1)
                        s = psum[0:C, B:B + 512].rearrange("p (h g) -> p h g", g=C)
                        step(nc.vector.tensor_reduce(ared[:, 0], s, AX.X, ALU.max))
                        nc.vector.tensor_tensor(att[:], s, bc(ared[:, 0], [C, 8, C], 2), ALU.subtract).then_inc(shifted, 1)
                        dve.wait_ge(exped, 1)
                        step(nc.vector.tensor_reduce(ared[:, 0], att[:], AX.X, ALU.add))
                        step(nc.vector.reciprocal(ared[:, 1], ared[:, 0]))
                        nc.vector.tensor_tensor(att[:], att[:], bc(ared[:, 1], [C, 8, C], 2), ALU.mult).then_inc(att_out, 1)
                        dve.wait_ge(mixed, 1)
                        dve.wait_ge(cleared, 1)
                        for h in range(8):
                            ins = nc.vector.tensor_copy(obd[64 * (h % 2):64 * (h % 2) + 64, h // 2, 8 * h:8 * h + 8],
                                                        psum[0:C, B + 1024 + 8 * h:B + 1024 + 8 * h + 8])
                        ins.then_inc(obd_out, 1)
                project_add([oT], [s_wout], s_bout)

        def moe():
            layer_norm()
            route(lambda t, o: nc.tensor.matmul(o, xT[:, t * P:(t + 1) * P], e_router, start=True, stop=True),
                  True, 0.0, 1e-12)
            with scratch("ehid", [P, 4, NP]) as ehid:
                with ph.phase("hid_in", "hid_out") as (block, hid_in, hid_out):
                    @block.tensor
                    def _(pe):
                        for c in range(4):
                            if c >= 2:
                                pe.wait_ge(hid_out, c - 1)
                            columns(A if c % 2 == 0 else B, P, [(e_w1[:, c * P:(c + 1) * P], xT[:])]).then_inc(hid_in, 1)

                    @block.scalar
                    def _(act):
                        for c in range(4):
                            r = A if c % 2 == 0 else B
                            act.wait_ge(hid_in, c + 1)
                            nc.scalar.activation(ehid[:, c, :], psum[:, r:r + NP], ACT.Gelu, bias=e_b1[:, c:c + 1]).then_inc(hid_out, 1)

                def products(t, o):
                    for c in range(4):
                        nc.tensor.matmul(o[:, c * P:(c + 1) * P], ehid[:, c, t * P:(t + 1) * P], e_w2[:, c, :],
                                         start=(c == 0), stop=False)
                    return nc.tensor.matmul(o, ones[0:1, :], e_b2, start=False, stop=True)
                mix_experts(products, extra=x_tok)

        def recurrence():
            layer_norm()
            with ph.phase("sum_in", "stepped", "turned") as (block, sum_in, stepped, turned):
                @block.tensor
                def _(pe):
                    columns(A, C, [(r_ih, xT[:]), (r_hh, hidden[:])]).then_inc(sum_in, 1)
                    pe.wait_ge(stepped, 1)
                    for t in range(NT):
                        last = nc.tensor.transpose(psum[:, B + t * C:B + (t + 1) * C], hidden[:, t * P:(t + 1) * P],
                                                   ident[0:C, 0:C])
                    last.then_inc(turned, 1)

                @block.scalar
                def _(act):
                    act.wait_ge(sum_in, 1)
                    nc.scalar.activation(hidden[:], psum[0:C, A:A + NP], ACT.Tanh, bias=r_bias[:]).then_inc(stepped, 1)

                @block.vector
                def _(dve):
                    dve.wait_ge(turned, 1)
                    nc.vector.tensor_tensor(flat(h_tok), flat(h_tok), psum[:, B:B + NT * C], ALU.add)

        def gated():
            layer_norm()
            with scratch("ghid", [P, 2, NP]) as ghid:
                with ph.phase("hid_in") as (block, hid_in):
                    @block.tensor
                    def _(pe):
                        for c in range(2):
                            columns(A if c == 0 else B, P, [(g_w1[:, c * P:(c + 1) * P], xT[:])]).then_inc(hid_in, 1)

                    @block.scalar
                    def _(act):
                        for c in range(2):
                            r = A if c == 0 else B
                            act.wait_ge(hid_in, c + 1)
                            nc.scalar.activation(ghid[:, c, :], psum[:, r:r + NP], ACT.Gelu, bias=g_b1[:, c:c + 1])

                def logit(t, o):
                    for c in range(2):
                        nc.tensor.matmul(o, ghid[:, c, t * P:(t + 1) * P], g_wg[:, c, :], start=(c == 0), stop=False)
                    return nc.tensor.matmul(o, ones[0:1, :], g_bg, start=False, stop=True)
                route(logit, False, 0.0, 0.0)

                def products(t, o):
                    nc.tensor.matmul(o, ones[0:1, :], g_bd, start=True, stop=False)
                    for c in range(2):
                        m = nc.tensor.matmul(o, ghid[:, c, t * P:(t + 1) * P], g_wd[:, c, :], start=False, stop=(c == 1))
                    return m
                mix_experts(products)

        def store(b):
            with ph.phase("stored") as (block, stored):
                @block.sync
                def _(sp):
                    ob = out[bass.ds(b, 1)].rearrange("a n c -> (a n) c")
                    sp.dma_start(ob[0:(NT - 1) * P].rearrange("(t p) c -> p t c", p=P), h_tok[:, 0:NT - 1, :]).then_inc(stored, 16)
                    sp.dma_start(ob[(NT - 1) * P:N_TOK], h_tok[0:N_TOK - (NT - 1) * P, NT - 1, :]).then_inc(stored, 16)
                    sp.wait_ge(stored, 32)

        with nc.Fori(0, n_batch) as b:
            tokens(b)
            for n, layer in enumerate((phasor, rotary_moe, state_space, product_keys, slices, moe, recurrence, gated)):
                if n < upto:
                    layer()
            store(b)
            ph.close_loop()


def layouts(i):
    cat, T = np.concatenate, np.transpose
    col = lambda a: np.reshape(a, (-1, 1))
    row = lambda a: np.reshape(a, (1, -1))
    w = {k: np.asarray(v) for k, v in i.items()}
    g = lambda k: w[k]
    d = {
        "x": g("x"), "cls": col(g("cls_tok")),
        "t_w": T(g("L0_tok_W").reshape(C, 18, C), (1, 2, 0)),
        "a_w1p": cat([g("L0_attn_kp_w1").T, g("L0_attn_qp_w1").T], 1),
        "a_w1h": cat([g("L0_attn_kh_w1").T, g("L0_attn_qh_w1").T], 1),
        "a_b1p": col(cat([g("L0_attn_kp_b1"), g("L0_attn_qp_b1")])),
        "a_b1h": col(cat([g("L0_attn_kh_b1"), g("L0_attn_qh_b1")])),
        "a_b2": row(cat([g("L0_attn_kp_b2"), g("L0_attn_qp_b2"), g("L0_attn_kh_b2"), g("L0_attn_qh_b2")])),
        "a_w2p": np.stack([g("L0_attn_kp_w2").T, g("L0_attn_qp_w2").T]),
        "a_w2h": np.stack([g("L0_attn_kh_w2").T, g("L0_attn_qh_w2").T]),
        "a_vw": g("L0_attn_v_w").T, "a_vb": row(g("L0_attn_v_b")),
        "a_ow": g("L0_attn_out_w").T, "a_ob": row(g("L0_attn_out_b")),
        "a_g": g("L0_attn_ln_g"), "a_b": g("L0_attn_ln_b"),
        "f_ln1": g("L0_ffn_ln1_w"), "f_ln2": g("L0_ffn_ln2_w"),
        "f_qkv": cat([g("L0_ffn_wq").T, g("L0_ffn_wk").T, g("L0_ffn_wv").T], 1),
        "f_wo": g("L0_ffn_wo").T, "f_router": g("L0_ffn_router_w").T,
        "f_w1": T(g("L0_ffn_w1"), (2, 0, 1)).reshape(C, -1),
        "f_w3": T(g("L0_ffn_w3"), (2, 0, 1)).reshape(C, -1),
        "f_w2": T(T(g("L0_ffn_w2"), (0, 2, 1)).reshape(2 * NE, HB, C), (1, 0, 2)),
        "m_in": g("L1_attn_W_in"), "m_cw": g("L1_attn_conv_w").reshape(P, TAPS), "m_cb": col(g("L1_attn_conv_b")),
        "m_xp": g("L1_attn_W_xproj"), "m_wdt": col(g("L1_attn_w_dt")), "m_bdt": col(g("L1_attn_b_dt")),
        "m_A": g("L1_attn_A"), "m_D": col(g("L1_attn_D")), "m_out": g("L1_attn_W_out"),
        "k_wqpk": g("L1_ffn_Wq_pk"), "k_wq": g("L1_ffn_Wq"),
        "k_keys": T(g("L1_ffn_pk_keys"), (0, 2, 3, 1)).reshape(4, 4, 32, PKK),
        "k_table": cat([g("L1_ffn_keys_table"), g("L1_ffn_values_table")], 1),
        "k_wo": T(g("L1_ffn_Wo").reshape(4, P, C), (1, 0, 2)),
        "s_win": g("L2_attn_W_in"), "s_bin_row": row(g("L2_attn_b_in")), "s_bin_col": col(g("L2_attn_b_in")),
        "s_wslice": g("L2_attn_W_slice"), "s_bslice": row(np.tile(g("L2_attn_b_slice"), 8)),
        "s_temp": g("L2_attn_temperature").reshape(8),
        "s_qkvw": np.tile(cat([g("L2_attn_W_q"), g("L2_attn_W_k"), g("L2_attn_W_v")], 1), (8, 1)),
        "s_bq": col(g("L2_attn_b_q")), "s_bk": col(g("L2_attn_b_k")), "s_bv": row(g("L2_attn_b_v")),
        "s_wout": g("L2_attn_W_out"), "s_bout": row(g("L2_attn_b_out")),
        "e_router": g("L2_ffn_router_w").T, "e_w1": T(g("L2_ffn_w1"), (1, 0, 2)).reshape(C, 512),
        "e_b1": T(g("L2_ffn_b1").reshape(4, P)), "e_w2": g("L2_ffn_w2"), "e_b2": row(g("L2_ffn_b2")),
        "r_ih": g("L3_attn_W_ih").T, "r_hh": g("L3_attn_W_hh").T,
        "r_b": np.stack([g("L3_attn_b_ih"), g("L3_attn_b_hh")], 1),
        "g_w1": g("L3_ffn_W1"), "g_b1": T(g("L3_ffn_b1").reshape(2, P)),
        "g_wg": T(g("L3_ffn_Wg").reshape(2, P, NE), (1, 0, 2)), "g_bg": row(g("L3_ffn_bg")),
        "g_wd": T(T(g("L3_ffn_Wd"), (1, 0, 2)).reshape(2, P, 512), (1, 0, 2)), "g_bd": row(g("L3_ffn_bd")),
    }
    d = {k: np.ascontiguousarray(v) for k, v in d.items()}
    for k, v in constants().items():
        d[k] = np.ascontiguousarray(v, dtype=np.float32)
    return d


UPTO, NBATCH = 99, N_BATCH


def kernel(**inputs):
    import concourse.bacc as bacc
    from concourse.bass_utils import run_bass_kernel_spmd

    nc = bacc.Bacc("TRN2", target_bir_lowering=False, num_devices=1)
    arrays, io = {}, {}
    for name, a in layouts(inputs).items():
        arrays["in_" + name] = a
        io[name] = nc.dram_tensor("in_" + name, a.shape, mybir.dt.from_np(a.dtype), kind="ExternalInput").ap()
    out = nc.dram_tensor("out_0", (N_BATCH, N_TOK, C), F32, kind="ExternalOutput").ap()
    build(nc, io, out, NBATCH, UPTO)
    r = run_bass_kernel_spmd(nc, [arrays], core_ids=[0])
    return r.results[0]["out_0"]
```

```python
import math
from contextlib import ExitStack, contextmanager

import numpy as np
import concourse.bass as bass
from concourse import mybir

F32 = mybir.dt.float32
U32 = mybir.dt.uint32
ALU = mybir.AluOpType
ACT = mybir.ActivationFunctionType
AX = mybir.AxisListType

P = 128
C = 64
N_BATCH = 8
N_PATCH, PATCH, HOP = 16, 16, 8
N_VAR, N_TIME = 64, 128
N_TOK = 1 + N_VAR * N_PATCH
NT = -(-N_TOK // P)
NP = NT * P
CHUNKS = [(a, min(a + 512, NP)) for a in range(0, NP, 512)]
NPER, NHYP = 48, 16
NE, HID0 = 8, 170
HB = HID0 // 2
NSTATE, TAPS = 16, 4
PKH, PKK, TOPK = 8, 64, 16
NEG = -1e30
LOWEST = -3.0e38
LN_EPS, RMS_EPS = 1e-5, 1e-6

PAIRS = []
_off = 0
for _i0, _i1, _j in [(0, 1, 16), (1, 2, 8), (2, 3, 5), (3, 4, 4), (4, 5, 3), (5, 8, 2), (8, 16, 1)]:
    PAIRS.append((_off, _i0, _i1, _j))
    _off += (_i1 - _i0) * _j
NPAIR = _off


def constants():
    t = np.arange(PATCH)
    f = np.arange(PATCH // 2 + 1)
    ang = 2 * np.pi * np.outer(f, t) / PATCH
    dft = np.concatenate([np.cos(ang), -np.sin(ang)], 0) / math.sqrt(PATCH)
    tok = np.arange(NP).reshape(NT, P).T
    inv = 1.0 / 10000.0 ** (np.arange(0, 16, 2, dtype=np.float32) / 16)
    fr = (tok[..., None].astype(np.float32) * inv).astype(np.float32)
    sin, cos = np.sin(fr), np.cos(fr)
    q, k = np.arange(P)[:, None], np.arange(P)[None, :]
    row = np.arange(P)[:, None]
    head_of_row = np.arange(4)[None, :, None] * 2 + row[:, :, None] // 64
    return {
        "c_dft": dft,
        "c_pos": 1.0 / np.sqrt((tok + 1) * 64.0),
        "c_cos": np.concatenate([cos, cos], -1),
        "c_sin": np.concatenate([-sin, sin], -1),
        "c_ident": np.eye(P),
        "c_after": np.where(k > q, NEG, 0.0),
        "c_afterT": np.where(q > k, NEG, 0.0),
        "c_upto": np.where(q <= k, 1.0, 0.0),
        "c_rank": np.broadcast_to(8.0 - np.arange(NE), (P, NE)),
        "c_headoff": np.broadcast_to(np.arange(PKH) * float(PKK * PKK), (P, PKH)),
        "c_iota": np.broadcast_to(np.arange(NPAIR), (P, NPAIR)),
        "c_ownhead": (np.arange(C)[None, None, :] // 8 == head_of_row),
        "c_valid": (tok < N_TOK),
        "c_headrow": (np.arange(P)[:, None] // TOPK == np.arange(PKH)[None, :]),
    }


class Phases:

    def __init__(self, nc):
        self.nc = nc
        self.stale = []

    def clear(self):
        for s in self.stale:
            self.nc.gpsimd.sem_clear(s)
        self.stale = []

    def close_loop(self):
        self.clear()
        self.nc.all_engine_barrier()

    @contextmanager
    def phase(self, *names):
        self.clear()
        with ExitStack() as ctx:
            sems = [ctx.enter_context(self.nc.semaphore(n)) for n in names]
            with self.nc.Block() as block:
                yield (block, *sems)
        self.stale = sems


class Steps:

    def __init__(self, eng, sem):
        self.eng, self.sem, self.n = eng, sem, 0

    def __call__(self, ins):
        self.n += 1
        ins.then_inc(self.sem, 1)
        self.eng.wait_ge(self.sem, self.n)


def build(nc, io, out, n_batch=N_BATCH, upto=99):
    ctx = ExitStack()
    with ctx:
        ph = Phases(nc)

        def sb(name, shape, dt=F32):
            return ctx.enter_context(nc.sbuf_tensor(name, shape, dt))

        taken = {}

        def scratch(name, shape, dt=F32):
            taken[name] = taken.get(name, 0) + 1
            return nc.sbuf_tensor(f"{name}_{taken[name]}", shape, dt)

        psum = ctx.enter_context(nc.psum_tensor("psum", [P, 8 * 512], F32))
        A, B, D = 0, 3 * 512, 6 * 512
        loads, zeroed = [], []

        def const(key, shape, src=None):
            t = sb("sb_" + key, shape)[:]
            loads.append((t, src if src is not None else io[key]))
            return t

        def padded(key, shape):
            t = sb("sb_" + key, [P, *shape[1:]])
            zeroed.append(t)
            loads.append((t[0:shape[0]], io[key]))
            return t[:]

        ident = const("c_ident", [P, P])
        after = const("c_after", [P, P])
        afterT = const("c_afterT", [P, P])
        upto_q = const("c_upto", [P, P])
        pos_norm = const("c_pos", [P, NT])
        cos = const("c_cos", [P, NT, 16])
        sin = const("c_sin", [P, NT, 16])
        rank = const("c_rank", [P, NE])
        headoff = const("c_headoff", [P, PKH])
        iota = const("c_iota", [P, NPAIR])
        ownhead = const("c_ownhead", [P, 4, C])
        valid = const("c_valid", [P, NT])
        headrow = const("c_headrow", [P, PKH])
        a_w1p = padded("a_w1p", [C, P])
        a_w1h = padded("a_w1h", [C, P])
        a_b1p = const("a_b1p", [P, 1])
        a_b1h = const("a_b1h", [P, 1])
        a_b2 = const("a_b2", [1, 160])
        a_vw = padded("a_vw", [C, C])
        a_vb = const("a_vb", [1, C])
        a_ow = padded("a_ow", [C, C])
        a_ob = const("a_ob", [1, C])
        a_g = const("a_g", [P, C], src=io["a_g"].partition_broadcast(P))
        a_b = const("a_b", [P, C], src=io["a_b"].partition_broadcast(P))
        f_ln1 = const("f_ln1", [P, C], src=io["f_ln1"].partition_broadcast(P))
        f_ln2 = const("f_ln2", [P, C], src=io["f_ln2"].partition_broadcast(P))
        f_qkv = padded("f_qkv", [C, P])
        f_wo = padded("f_wo", [C, C])
        f_router = padded("f_router", [C, NE])
        f_w1 = padded("f_w1", [C, NE * HID0])
        f_w3 = padded("f_w3", [C, NE * HID0])
        f_w2 = const("f_w2", [HB, 2 * NE, C])
        m_in = padded("m_in", [C, 2 * P])
        m_cw = const("m_cw", [P, TAPS])
        m_cb = const("m_cb", [P, 1])
        m_xp = const("m_xp", [P, 1 + 2 * NSTATE])
        m_wdt = const("m_wdt", [P, 1])
        m_bdt = const("m_bdt", [P, 1])
        m_A = const("m_A", [P, NSTATE])
        m_D = const("m_D", [P, 1])
        m_out = const("m_out", [P, C])
        k_wqpk = padded("k_wqpk", [C, 512])
        k_wq = padded("k_wq", [C, 512])
        k_wo = const("k_wo", [P, 4, C])
        s_win = padded("s_win", [C, C])
        s_bin_row = const("s_bin_row", [1, C])
        s_bin_col = const("s_bin_col", [C, 1])
        s_bslice = const("s_bslice", [1, 512])
        s_temp = const("s_temp", [P, 8], src=io["s_temp"].partition_broadcast(P))
        s_qkvw = const("s_qkvw", [C, 24])
        s_bq = const("s_bq", [8, 1])
        s_bk = const("s_bk", [8, 1])
        s_bv = const("s_bv", [1, 8])
        s_wout = const("s_wout", [C, C])
        s_bout = const("s_bout", [1, C])
        e_router = padded("e_router", [C, NE])
        e_w1 = padded("e_w1", [C, 512])
        e_b1 = const("e_b1", [P, 4])
        e_b2 = const("e_b2", [1, 512])
        r_ih = padded("r_ih", [C, C])
        r_hh = padded("r_hh", [C, C])
        r_b = const("r_b", [C, 2])
        g_w1 = padded("g_w1", [C, 256])
        g_b1 = const("g_b1", [P, 2])
        g_wg = const("g_wg", [P, 2, NE])
        g_bg = const("g_bg", [1, NE])
        g_wd = const("g_wd", [P, 2, 512])
        g_bd = const("g_bd", [1, 512])

        a_w2p = sb("a_w2p_sb", [P, 96])
        a_w2h = sb("a_w2h_sb", [P, 64])
        k_keys = sb("k_keys_sb", [P, 4, 256])
        s_slice = sb("s_slice_sb", [C, 512])
        e_w2 = sb("e_w2_sb", [P, 4, P])
        blocks = []
        for j in range(2):
            blocks.append((a_w2p[j * 64:(j + 1) * 64, j * 48:(j + 1) * 48], io["a_w2p"][j]))
            blocks.append((a_w2h[j * 64:(j + 1) * 64, j * 32:(j + 1) * 32], io["a_w2h"][j]))
        for c in range(4):
            for j in range(4):
                blocks.append((k_keys[32 * j:32 * j + 32, c, 64 * j:64 * j + 64], io["k_keys"][c, j]))
            for j in range(2):
                blocks.append((e_w2[64 * j:64 * j + 64, c, 64 * j:64 * j + 64], io["e_w2"][2 * c + j]))
        for h in range(8):
            blocks.append((s_slice[8 * h:8 * h + 8, 64 * h:64 * h + 64], io["s_wslice"]))

        w_tok = sb("w_tok", [P, 8, C])
        ones = sb("ones", [P, P])
        eps = sb("eps", [P, 3])
        s_rtemp = sb("s_rtemp", [P, 8])
        r_bias = sb("r_bias", [C, 1])

        h_new = sb("h_new", [P, NT, C])
        h_old = sb("h_old", [P, NT, C])
        h_tok = h_new
        x_tok = sb("x_tok", [P, NT, C])
        xT = sb("xT", [P, NP])
        y_tok = sb("y_tok", [P, NT, C])
        yT = sb("yT", [P, NP])
        hidden = sb("hidden", [P, NP])
        stat = sb("stat", [P, 8, NT])
        tmp = sb("tmp", [P, NT, C])
        rt_l, rt_p, rt_k, rt_m, rt_o, rt_w = [sb(f"rt{i}", [P, NT, NE]) for i in range(6)]
        rt_s = sb("rt_s", [P, 4, NT])

        dram_w = nc.dram_tensor("dram_w", [PATCH, C, C], F32, kind="Internal").ap()

        def bc(ap, shape, axis):
            return ap.unsqueeze(axis).broadcast_to(shape)

        def flat(t):
            return t[:].rearrange("p a b -> p (a b)")

        def columns(base, rows, pairs):
            for a, b in CHUNKS:
                for n, (w, d) in enumerate(pairs):
                    last = nc.tensor.matmul(psum[0:rows, base + a:base + b], w, d[:, a:b],
                                            start=(n == 0), stop=(n == len(pairs) - 1))
            return last

        def turn_tiles(base, src, rows):
            for t in range(NT):
                last = nc.tensor.transpose(psum[0:rows, base + t * P:base + (t + 1) * P],
                                           src[:, t, :], ident)
            return last

        with ph.phase("cleared", "loaded", "fold_in", "folded", "fold_out", "fold_back", "sp_blocks",
                      "dve_step") as (block, cleared, loaded, fold_in, folded, fold_out, fold_back,
                                      blocks_in, dve_step):
            with scratch("w_freq", [18, C, C]) as w_freq, \
                    scratch("dft", [18, PATCH]) as dft, \
                    scratch("w_fold", [PATCH, C * C]) as w_fold:

                @block.sync
                def _(sp):
                    sp.dma_start(w_freq[:], io["t_w"]).then_inc(fold_in, 16)
                    sp.dma_start(dft[:], io["c_dft"]).then_inc(fold_in, 16)
                    sp.wait_ge(cleared, 1)
                    for dst, src in loads:
                        sp.dma_start(dst, src).then_inc(loaded, 16)
                    for dst, src in blocks:
                        sp.dma_start(dst, src).then_inc(blocks_in, 16)
                    sp.wait_ge(fold_out, 2)
                    sp.dma_start(dram_w, w_fold[:].rearrange("t (c o) -> t c o", c=C)).then_inc(fold_back, 16)
                    sp.wait_ge(fold_back, 16)
                    for r in range(2):
                        sp.dma_start(w_tok[r * C:(r + 1) * C],
                                     dram_w.rearrange("(u r) c o -> r c u o", r=2)[r]).then_inc(fold_back, 16)
                    sp.wait_ge(fold_back, 48)
                    sp.wait_ge(loaded, 16 * len(loads))
                    sp.wait_ge(blocks_in, 16 * len(blocks))

                @block.tensor
                def _(pe):
                    pe.wait_ge(fold_in, 32)
                    wf = w_freq[:].rearrange("f c o -> f (c o)")
                    for n in range(8):
                        nc.tensor.matmul(psum[0:PATCH, n * 512:(n + 1) * 512], dft[:],
                                         wf[:, n * 512:(n + 1) * 512], start=True, stop=True).then_inc(folded, 1)

                @block.vector
                def _(dve):
                    for t in (a_w2p, a_w2h, k_keys, s_slice, xT, yT, hidden, *zeroed):
                        nc.vector.memset(t[:], 0.0)
                    nc.vector.memset(e_w2[:], 0.0).then_inc(cleared, 1)
                    nc.vector.memset(ones[:], 1.0)
                    nc.vector.memset(eps[:, 0:1], LN_EPS)
                    nc.vector.memset(eps[:, 1:2], RMS_EPS)
                    nc.vector.memset(eps[:, 2:3], math.pi / 2)
                    dve.wait_ge(folded, 8)
                    nc.vector.tensor_copy(w_fold[:], psum[0:PATCH, :]).then_inc(fold_out, 2)
                    dve.wait_ge(loaded, 16 * len(loads))
                    nc.vector.reciprocal(s_rtemp[:], s_temp)
                    nc.vector.tensor_tensor(r_bias[:], r_b[:, 0:1], r_b[:, 1:2], ALU.add)

        def layer_norm(rms_weight=None, src=None, dst=None, want_T=True):
            src = src or h_tok
            dst = dst or x_tok
            rms = rms_weight is not None
            with ph.phase("variance", "deviation", "normed", "turned", "dve_step") as (
                    block, variance, deviation, normed, turned, dve_step):
                @block.vector
                def _(dve):
                    step = Steps(dve, dve_step)
                    cen = src
                    if not rms:
                        step(nc.vector.tensor_reduce(stat[:, 0], src[:], AX.X, ALU.add))
                        step(nc.vector.tensor_scalar(stat[:, 1], stat[:, 0], 1.0 / C, None, ALU.mult))
                        step(nc.vector.tensor_tensor(dst[:], src[:], bc(stat[:, 1], [P, NT, C], 2), ALU.subtract))
                        cen = dst
                    step(nc.vector.tensor_tensor(tmp[:], cen[:], cen[:], ALU.mult))
                    nc.vector.tensor_reduce(stat[:, 2], tmp[:], AX.X, ALU.add).then_inc(variance, 1)
                    dve.wait_ge(deviation, 1)
                    step(nc.vector.reciprocal(stat[:, 4], stat[:, 3]))
                    ins = nc.vector.tensor_tensor(dst[:], cen[:], bc(stat[:, 4], [P, NT, C], 2), ALU.mult)
                    if rms:
                        step(ins)
                        ins = nc.vector.tensor_tensor(dst[:], dst[:], bc(rms_weight, [P, NT, C], 1), ALU.mult)
                    ins.then_inc(normed, 1)

                @block.scalar
                def _(act):
                    act.wait_ge(variance, 1)
                    nc.scalar.activation(stat[:, 3], stat[:, 2], ACT.Sqrt, scale=1.0 / C,
                                         bias=eps[:, 1:2] if rms else eps[:, 0:1]).then_inc(deviation, 1)
                    if want_T:
                        act.wait_ge(turned, 1)
                        nc.scalar.copy(xT[0:C, :], psum[0:C, A:A + NP])

                @block.tensor
                def _(pe):
                    pe.wait_ge(normed, 1)
                    if want_T:
                        turn_tiles(A, dst, C).then_inc(turned, 1)

        def project_add(srcT, weights, bias, extra=None):
            with ph.phase("projected", "dve_step") as (block, projected, dve_step):
                @block.tensor
                def _(pe):
                    for t in range(NT):
                        o = psum[:, A + t * C:A + (t + 1) * C]
                        for n, (s, w) in enumerate(zip(srcT, weights)):
                            last = nc.tensor.matmul(o, s[:, t * P:(t + 1) * P], w, start=(n == 0),
                                                    stop=(n == len(srcT) - 1 and bias is None))
                        if bias is not None:
                            last = nc.tensor.matmul(o, ones[0:1, :], bias, start=False, stop=True)
                    last.then_inc(projected, 1)

                @block.vector
                def _(dve):
                    step = Steps(dve, dve_step)
                    if extra is not None:
                        step(nc.vector.tensor_tensor(flat(h_tok), flat(h_tok), flat(extra), ALU.add))
                    dve.wait_ge(projected, 1)
                    nc.vector.tensor_tensor(flat(h_tok), flat(h_tok), psum[:, A:A + NT * C], ALU.add)

        def softmax_experts(step, logits):
            step(nc.vector.tensor_reduce(rt_s[:, 0], logits, AX.X, ALU.max))
            step(nc.vector.tensor_tensor(rt_l[:], logits, bc(rt_s[:, 0], [P, NT, NE], 2), ALU.subtract))

        def pick_best(step, probs, picked, top):
            step(nc.vector.tensor_reduce(top, probs, AX.X, ALU.max))
            step(nc.vector.tensor_tensor(rt_k[:], probs, bc(top, [P, NT, NE], 2), ALU.is_ge))
            step(nc.vector.tensor_tensor(rt_k[:], rt_k[:], bc(rank, [P, NT, NE], 1), ALU.mult))
            step(nc.vector.tensor_reduce(rt_s[:, 3], rt_k[:], AX.X, ALU.max))
            step(nc.vector.tensor_tensor(picked, rt_k[:], bc(rt_s[:, 3], [P, NT, NE], 2), ALU.is_equal))

        def route(logit_products, top2, floor_add, floor_max):
            with ph.phase("logits", "shifted", "exps", "dve_step") as (block, logits, shifted, exps, dve_step):
                @block.tensor
                def _(pe):
                    for t in range(NT):
                        last = logit_products(t, psum[:, D + t * NE:D + (t + 1) * NE])
                    last.then_inc(logits, 1)

                @block.scalar
                def _(act):
                    act.wait_ge(shifted, 1)
                    nc.scalar.activation(rt_p[:], rt_l[:], ACT.Exp).then_inc(exps, 1)

                @block.vector
                def _(dve):
                    step = Steps(dve, dve_step)
                    lg = psum[:, D:D + NT * NE].rearrange("p (t e) -> p t e", e=NE)
                    dve.wait_ge(logits, 1)
                    softmax_experts(step, lg)
                    nc.vector.tensor_copy(rt_s[:, 1], rt_s[:, 0]).then_inc(shifted, 1)
                    dve.wait_ge(exps, 1)
                    dve.wait_ge(shifted, 1)
                    step(nc.vector.tensor_reduce(rt_s[:, 1], rt_p[:], AX.X, ALU.add))
                    step(nc.vector.reciprocal(rt_s[:, 2], rt_s[:, 1]))
                    step(nc.vector.tensor_tensor(rt_p[:], rt_p[:], bc(rt_s[:, 2], [P, NT, NE], 2), ALU.mult))
                    pick_best(step, rt_p[:], rt_m[:], rt_s[:, 0])
                    if not top2:
                        step(nc.vector.tensor_tensor(rt_w[:], rt_m[:], rt_p[:], ALU.mult))
                        return
                    step(nc.vector.scalar_tensor_tensor(rt_l[:].rearrange("p a b -> p (a b)"), flat(rt_m), -4.0,
                                                        flat(rt_p), ALU.mult, ALU.add))
                    pick_best(step, rt_l[:], rt_o[:], rt_s[:, 1])
                    step(nc.vector.tensor_tensor(rt_m[:], rt_m[:], rt_o[:], ALU.add))
                    step(nc.vector.tensor_tensor(rt_w[:], rt_m[:], rt_p[:], ALU.mult))
                    step(nc.vector.tensor_reduce(rt_s[:, 1], rt_w[:], AX.X, ALU.add))
                    step(nc.vector.tensor_scalar(rt_s[:, 1], rt_s[:, 1], floor_add, floor_max, ALU.add, ALU.max))
                    step(nc.vector.reciprocal(rt_s[:, 2], rt_s[:, 1]))
                    step(nc.vector.tensor_tensor(rt_w[:], rt_w[:], bc(rt_s[:, 2], [P, NT, NE], 2), ALU.mult))

        def mix_experts(tile_products, extra=None):
            with scratch("mixed", [P, 2, NE, C]) as mixed, \
                    ph.phase("tile_out", "tile_used", "dve_step") as (block, tile_out, tile_used, dve_step):
                @block.tensor
                def _(pe):
                    for t in range(NT):
                        if t >= 4:
                            pe.wait_ge(tile_used, t - 3)
                        tile_products(t, psum[:, (t % 4) * 512:(t % 4 + 1) * 512]).then_inc(tile_out, 1)

                @block.vector
                def _(dve):
                    step = Steps(dve, dve_step)
                    for t in range(NT):
                        dve.wait_ge(tile_out, t + 1)
                        if t >= 2:
                            dve.wait_ge(dve_step, t - 1)
                        o = psum[:, (t % 4) * 512:(t % 4 + 1) * 512].rearrange("p (e c) -> p e c", c=C)
                        nc.vector.tensor_tensor(mixed[:, t % 2], o, bc(rt_w[:, t], [P, NE, C], 2),
                                                ALU.mult).then_inc(tile_used, 1)
                        dve.wait_ge(tile_used, t + 1)
                        nc.vector.tensor_reduce(tmp[:, t], mixed[:, t % 2].rearrange("p e c -> p c e"),
                                                AX.X, ALU.add).then_inc(dve_step, 1)
                    step.n = NT
                    dve.wait_ge(dve_step, NT)
                    step(nc.vector.tensor_tensor(flat(h_tok), flat(h_tok), flat(tmp), ALU.add))
                    if extra is not None:
                        step(nc.vector.tensor_tensor(flat(h_tok), flat(h_tok), flat(extra), ALU.add))

        HEAD_SEMS = ("q_turned", "k_turned", "row_cleared", "qT_out", "kT_out", "scores", "maxed", "max_turned",
                     "max_row", "scoresT", "exped", "weighed", "summed")
        w_of = [(t + 1) * P for t in range(NT)]
        start_of = [sum(NP - P * j for j in range(t)) for t in range(NT)]

        def out_column(t, hd):
            per_bank = 512 // (hd + 1)
            return D + t * (hd + 1) if t < per_bank else A + (t - per_bank) * (hd + 1)

        class Head:

            def __init__(self, sems, buf, hd, k_row, scale):
                (self.q_turned, self.k_turned, self.row_cleared, self.qT_out, self.kT_out, self.scores, self.maxed,
                 self.max_turned, self.max_row, self.scoresT, self.exped, self.weighed, self.summed) = sems
                self.q_h, self.k_h, self.v_h, self.qT, self.kT, self.neg_max, self.probsT, self.r_sum = buf
                self.hd, self.k_row, self.scale = hd, k_row, scale
                self.per_bank = 512 // (hd + 1)

            def clear_row(self):
                nc.vector.memset(self.qT[self.k_row:self.k_row + 1, :], 0.0).then_inc(self.row_cleared, 1)

            def max_tiles(self, dve, tiles):
                for t in tiles:
                    r = A if t % 2 == 0 else B
                    dve.wait_ge(self.scores, t + 1)
                    nc.vector.tensor_reduce(self.neg_max[:, t:t + 1], psum[:, r:r + w_of[t]], AX.X, ALU.max,
                                            negate=True).then_inc(self.maxed, 1)

            def row_of_max(self, dve):
                dve.wait_ge(self.max_turned, 1)
                nc.vector.tensor_copy(self.qT[self.k_row:self.k_row + 1, :], psum[0:1, A:A + NP]).then_inc(self.max_row, 1)

            def normalize(self, dve, out_of):
                dve.wait_ge(self.weighed, NT)
                hd = self.hd
                parts = [(0, min(self.per_bank, NT))] + ([(self.per_bank, NT)] if NT > self.per_bank else [])
                views = []
                for a, b in parts:
                    c = out_column(a, hd)
                    views.append(psum[:, c:c + (b - a) * (hd + 1)].rearrange("p (t d) -> p t d", d=hd + 1))
                    nc.vector.reciprocal(self.r_sum[:, a:b], views[-1][:, :, hd]).then_inc(self.summed, 1)
                dve.wait_ge(self.summed, len(parts))
                for (a, b), o in zip(parts, views):
                    nc.vector.tensor_tensor(out_of(a, b), o[:, :, 0:hd], bc(self.r_sum[:, a:b], [P, b - a, hd], 2), ALU.mult)

            def run_scalar(self, act):
                hd = self.hd
                act.wait_ge(self.q_turned, 1)
                nc.scalar.copy(self.qT[0:hd, :], psum[0:hd, A:A + NP]).then_inc(self.qT_out, 1)
                act.wait_ge(self.k_turned, 1)
                nc.scalar.copy(self.kT[0:hd, :], psum[0:hd, B:B + NP]).then_inc(self.kT_out, 1)
                for t in range(NT):
                    r = B if t % 2 == 0 else A
                    act.wait_ge(self.scoresT, t + 1)
                    nc.scalar.activation(self.probsT[:, start_of[t]:start_of[t] + NP - t * P],
                                         psum[:, r + t * P:r + NP], ACT.Exp, scale=self.scale).then_inc(self.exped, 1)

            def run_tensor(self, pe):
                hd, qT, kT = self.hd, self.qT, self.kT
                turn_tiles(A, self.q_h, hd).then_inc(self.q_turned, 1)
                turn_tiles(B, self.k_h, hd).then_inc(self.k_turned, 1)
                pe.wait_ge(self.qT_out, 1)
                pe.wait_ge(self.kT_out, 1)
                pe.wait_ge(self.row_cleared, 1)
                for t in range(NT):
                    r = A if t % 2 == 0 else B
                    if t >= 2:
                        pe.wait_ge(self.maxed, t - 1)
                    for a, b in CHUNKS:
                        b = min(b, w_of[t])
                        if a >= b:
                            continue
                        own = min(b, t * P)
                        if a < own:
                            nc.tensor.matmul(psum[:, r + a:r + own], qT[:, t * P:(t + 1) * P], kT[:, a:own],
                                             start=True, stop=True)
                        if own < b:
                            nc.tensor.matmul(psum[:, r + own:r + b], qT[:, t * P:(t + 1) * P], kT[:, own:b],
                                             start=True, stop=False)
                            last = nc.tensor.matmul(psum[:, r + own:r + b], ident, after, start=False, stop=True)
                    last.then_inc(self.scores, 1)
                pe.wait_ge(self.maxed, NT)
                for t in range(NT):
                    last = nc.tensor.transpose(psum[0:1, A + t * P:A + (t + 1) * P], self.neg_max[:, t:t + 1], ident)
                last.then_inc(self.max_turned, 1)
                pe.wait_ge(self.max_row, 1)

                def weigh(t):
                    pe.wait_ge(self.exped, t + 1)
                    c = out_column(t, hd)
                    for j in range(t + 1):
                        s = start_of[j] + (t - j) * P
                        m = nc.tensor.matmul(psum[:, c:c + hd + 1], self.probsT[:, s:s + P], self.v_h[:, j, :],
                                             start=(j == 0), stop=(j == t))
                    m.then_inc(self.weighed, 1)

                for t in range(NT):
                    r = B if t % 2 == 0 else A
                    if t >= 2:
                        pe.wait_ge(self.exped, t - 1)
                    for a, b in CHUNKS:
                        a = max(a, t * P)
                        if a >= b:
                            continue
                        rest = a
                        if a == t * P:
                            rest = a + P
                            nc.tensor.matmul(psum[:, r + a:r + rest], kT[:, t * P:(t + 1) * P], qT[:, a:rest],
                                             start=True, stop=False)
                            last = nc.tensor.matmul(psum[:, r + a:r + rest], ident, afterT, start=False, stop=True)
                        if rest < b:
                            last = nc.tensor.matmul(psum[:, r + rest:r + b], kT[:, t * P:(t + 1) * P], qT[:, rest:b],
                                                    start=True, stop=True)
                    last.then_inc(self.scoresT, 1)
                    if t >= 1:
                        weigh(t - 1)
                weigh(NT - 1)

        def head_buffers(c2, hd):
            def b(name, shape):
                return c2.enter_context(scratch(name, shape))
            return [b("q_h", [P, NT, hd]), b("k_h", [P, NT, hd]), b("v_h", [P, NT, hd + 1]), b("qT", [P, NP]),
                    b("kT", [P, NP]), b("neg_max", [P, NT]),
                    b("probsT", [P, sum(NP - P * j for j in range(NT))]), b("r_sum", [P, NT])]

        def init_head(buf, hd, k_row):
            q_h, k_h, v_h, qT, kT = buf[:5]
            with ph.phase("dve_step") as (block, dve_step):
                @block.vector
                def _(dve):
                    step = Steps(dve, dve_step)
                    nc.vector.memset(q_h[:, NT - 1], 0.0)
                    nc.vector.memset(k_h[:, NT - 1], 0.0)
                    step(nc.vector.memset(v_h[:, NT - 1], 0.0))
                    nc.vector.memset(v_h[:, :, hd:hd + 1], 1.0)
                    nc.vector.memset(qT[:], 0.0)
                    step(nc.vector.memset(kT[:], 0.0))
                    nc.vector.memset(kT[k_row:k_row + 1, :], 1.0)

        def rotary_heads(q_all, k_all, v_all, buf):
            hd = 16
            with nc.Fori(0, 4) as h:
                with ph.phase(*HEAD_SEMS, "head_in") as (block, *sems, head_in):
                    head = Head(sems, buf, hd, 32, hd ** -0.5)
                    of_head = bass.ds(h * hd, hd)

                    @block.vector
                    def _(dve):
                        nc.vector.tensor_copy(head.q_h[:], q_all[:, :, of_head]).then_inc(head_in, 1)
                        nc.vector.tensor_copy(head.k_h[:], k_all[:, :, of_head]).then_inc(head_in, 1)
                        nc.vector.tensor_copy(head.v_h[:, :, 0:hd], v_all[:, :, of_head]).then_inc(head_in, 1)
                        head.clear_row()
                        head.max_tiles(dve, range(NT))
                        head.row_of_max(dve)
                        head.normalize(dve, lambda t0, t1: y_tok[:, t0:t1, of_head])

                    @block.scalar
                    def _(act):
                        head.run_scalar(act)

                    @block.tensor
                    def _(pe):
                        pe.wait_ge(head_in, 3)
                        head.run_tensor(pe)
                ph.close_loop()

        def tokens(b):
            U = N_TIME // 2
            with scratch("series", [P, U + 4, N_VAR]) as series, \
                    scratch("edge", [P, N_VAR]) as edge, \
                    scratch("hT", [C, NP]) as hT, \
                    ph.phase("series_in", "padded", "embedded", "hT_out", "turned") as (
                        block, series_in, padded, embedded, hT_out, turned):
                @block.sync
                def _(sp):
                    xb = io["x"][bass.ds(b, 1)].rearrange("a c (u r) v -> (a r) c u v", r=2)
                    for r in range(2):
                        sp.dma_start(series[r * C:(r + 1) * C, 0:U, :], xb[r]).then_inc(series_in, 16)
                        sp.dma_start(edge[r * C:(r + 1) * C, :],
                                     io["x"][bass.ds(b, 1), :, N_TIME - 1, :].rearrange("a c v -> (a c) v")
                                     ).then_inc(series_in, 16)
                    sp.dma_start(hT[:, 0:1], io["cls"]).then_inc(series_in, 16)

                @block.vector
                def _(dve):
                    nc.vector.memset(hT[:, N_TOK:NP], 0.0)
                    dve.wait_ge(series_in, 80)
                    nc.vector.tensor_copy(series[:, U:U + 4, :], bc(edge[:], [P, 4, N_VAR], 1)).then_inc(padded, 1)
                    dve.wait_ge(embedded, 1)
                    nc.vector.tensor_copy(hT[:, 1:N_TOK], psum[0:C, A:A + N_TOK - 1]).then_inc(hT_out, 1)
                    dve.wait_ge(turned, 1)
                    nc.vector.tensor_copy(flat(h_tok), psum[:, B:B + NT * C])

                @block.tensor
                def _(pe):
                    pe.wait_ge(padded, 1)
                    for half in range(2):
                        o = psum[0:C, A + half * 512:A + (half + 1) * 512]
                        for u in range(8):
                            rhs = series[:, u:u + 4 * (N_PATCH - 1) + 1:4, half * 32:(half + 1) * 32]
                            last = nc.tensor.matmul(o, w_tok[:, u, :], rhs.rearrange("p n v -> p v n"),
                                                    start=(u == 0), stop=(u == 7))
                    last.then_inc(embedded, 1)
                    pe.wait_ge(hT_out, 1)
                    for t in range(NT):
                        last = nc.tensor.transpose(psum[:, B + t * C:B + (t + 1) * C],
                                                   hT[:, t * P:(t + 1) * P], ident[0:C, 0:C])
                    last.then_inc(turned, 1)

        def phasor():
            layer_norm()
            with ExitStack() as c2:
                def b(name, shape):
                    return c2.enter_context(scratch(name, shape))
                hid_p, hid_h = b("hid_p", [P, NP]), b("hid_h", [P, NP])
                pre = b("pre", [P, NT, 160])
                val = b("val", [P, NT, C])
                half_sin, half_cos = b("half_sin", [P, NT, 96]), b("half_cos", [P, NT, 96])
                feat = b("feat", [P, 2, NT, P])
                featT = b("featT", [P, 2, NP])
                rad = b("rad", [P, 4, NT, 32])
                ret = b("ret", [P, NT, C])
                local = b("local", [P, 2, P])
                memory = b("memory", [P, 2, C])
                with ph.phase("hid_in", "hid_out", "pre_in", "val_in") as (block, hid_in, hid_out, pre_in, val_in):
                    @block.tensor
                    def _(pe):
                        columns(A, P, [(a_w1p, xT[:])]).then_inc(hid_in, 1)
                        columns(B, P, [(a_w1h, xT[:])]).then_inc(hid_in, 1)
                        for t in range(NT):
                            o = psum[:, D + t * C:D + (t + 1) * C]
                            nc.tensor.matmul(o, xT[:, t * P:(t + 1) * P], a_vw, start=True, stop=False)
                            last = nc.tensor.matmul(o, ones[0:1, :], a_vb, start=False, stop=True)
                        last.then_inc(val_in, 1)
                        pe.wait_ge(hid_out, 2)
                        for t in range(NT):
                            o = A + (t // 3) * 512 + (t % 3) * 160
                            s = slice(t * P, (t + 1) * P)
                            nc.tensor.matmul(psum[:, o:o + 96], hid_p[:, s], a_w2p[:], start=True, stop=False)
                            nc.tensor.matmul(psum[:, o + 96:o + 160], hid_h[:, s], a_w2h[:], start=False, stop=False)
                            last = nc.tensor.matmul(psum[:, o:o + 160], ones[0:1, :], a_b2, start=False, stop=True)
                        last.then_inc(pre_in, 1)

                    @block.scalar
                    def _(act):
                        act.wait_ge(hid_in, 1)
                        nc.scalar.activation(hid_p[:], psum[:, A:A + NP], ACT.Gelu, bias=a_b1p).then_inc(hid_out, 1)
                        act.wait_ge(hid_in, 2)
                        nc.scalar.activation(hid_h[:], psum[:, B:B + NP], ACT.Gelu, bias=a_b1h).then_inc(hid_out, 1)
                        act.wait_ge(pre_in, 1)
                        for j in range(3):
                            o = psum[:, A + j * 512:A + j * 512 + 480].rearrange("p (t f) -> p t f", f=160)
                            nc.scalar.activation(pre[:, 3 * j:3 * j + 3, :], o, ACT.Tanh)

                    @block.vector
                    def _(dve):
                        dve.wait_ge(val_in, 1)
                        nc.vector.tensor_copy(flat(val), psum[:, D:D + NT * C])

                with ph.phase("angles", "radii2", "sines", "radii", "featured", "turned", "dve_step") as (
                        block, angles, radii2, sines, radii, featured, turned, dve_step):
                    ang = pre[:, :, 0:96]
                    pair = pre[:, :, 96:160].rearrange("p t (n c) -> p t n c", c=2)

                    @block.vector
                    def _(dve):
                        step = Steps(dve, dve_step)
                        nc.vector.scalar_tensor_tensor(half_cos[:], ang, -1.0, ang, ALU.mult, ALU.max).then_inc(angles, 1)
                        step(nc.vector.tensor_scalar(pair, pair, 0.9, None, ALU.mult))
                        step(nc.vector.tensor_tensor(rad[:, 0], pair[:, :, :, 0], pair[:, :, :, 0], ALU.mult))
                        step(nc.vector.tensor_tensor(rad[:, 1], pair[:, :, :, 1], pair[:, :, :, 1], ALU.mult))
                        step(nc.vector.tensor_tensor(rad[:, 0], rad[:, 0], rad[:, 1], ALU.add))
                        step(nc.vector.tensor_scalar(rad[:, 1], rad[:, 0], 0.0, None, ALU.is_equal))
                        nc.vector.tensor_tensor(pair[:, :, :, 0], pair[:, :, :, 0], rad[:, 1], ALU.add).then_inc(radii2, 1)
                        dve.wait_ge(radii2, 1)
                        dve.wait_ge(radii, 1)
                        step(nc.vector.tensor_tensor(rad[:, 3], rad[:, 2], rad[:, 1], ALU.add))
                        step(nc.vector.reciprocal(rad[:, 3], rad[:, 3]))
                        step(nc.vector.tensor_scalar(rad[:, 2], rad[:, 2], -1.0, 1.0, ALU.mult, ALU.add))
                        step(nc.vector.tensor_tensor(rad[:, 3], rad[:, 3], rad[:, 2], ALU.mult))
                        for kq in range(2):
                            s = slice(kq * 16, (kq + 1) * 16)
                            nc.vector.tensor_tensor(feat[:, kq, :, NPER:64], pair[:, :, s, 0], rad[:, 3, :, s], ALU.mult)
                            nc.vector.tensor_tensor(feat[:, kq, :, 64 + NPER:P], pair[:, :, s, 1], rad[:, 3, :, s], ALU.mult)
                        dve.wait_ge(sines, 1)
                        step(nc.vector.scalar_tensor_tensor(half_cos[:], half_cos[:], 2.0, half_sin[:], ALU.mult, ALU.mult))
                        step(nc.vector.tensor_tensor(half_sin[:], half_sin[:], half_sin[:], ALU.mult))
                        for kq in range(2):
                            s = slice(kq * NPER, (kq + 1) * NPER)
                            step(nc.vector.tensor_copy(feat[:, kq, :, 64:64 + NPER], half_cos[:, :, s]))
                            step(nc.vector.tensor_scalar(feat[:, kq, :, 0:NPER], half_sin[:, :, s], -2.0, 1.0,
                                                         ALU.mult, ALU.add))
                        nc.vector.tensor_copy(stat[:, 0], stat[:, 4]).then_inc(featured, 1)

                    @block.scalar
                    def _(act):
                        act.wait_ge(radii2, 1)
                        nc.scalar.activation(rad[:, 2], rad[:, 0], ACT.Sqrt).then_inc(radii, 1)
                        nc.scalar.activation(half_sin[:], ang, ACT.Sin, scale=math.pi / 2)
                        nc.scalar.activation(half_cos[:], half_cos[:], ACT.Sin, scale=-math.pi / 2,
                                             bias=eps[:, 2:3]).then_inc(sines, 1)
                        for kq in range(2):
                            act.wait_ge(turned, kq + 1)
                            r = A if kq == 0 else B
                            nc.scalar.copy(featT[:, kq, :], psum[:, r:r + NP])

                    @block.tensor
                    def _(pe):
                        pe.wait_ge(featured, 1)
                        turn_tiles(A, feat[:, 0], P).then_inc(turned, 1)
                        turn_tiles(B, feat[:, 1], P).then_inc(turned, 1)

                with ph.phase("scored", "masked", "grown", "kept", "read", "read_out", "dve_step") as (
                        block, scored, masked, grown, kept, read, read_out, dve_step):
                    @block.tensor
                    def _(pe):
                        for t in range(NT):
                            s = slice(t * P, (t + 1) * P)
                            if t >= 2:
                                pe.wait_ge(masked, t - 1)
                            nc.tensor.matmul(psum[:, A + (t % 2) * 512:A + (t % 2) * 512 + P], featT[:, 0, s],
                                             featT[:, 1, s], start=True, stop=True).then_inc(scored, 1)
                            if t >= 1:
                                pe.wait_ge(kept, t)
                            nc.tensor.matmul(psum[:, B:B + C], feat[:, 0, t, :], val[:, t, :],
                                             start=True, stop=True).then_inc(grown, 1)
                            pe.wait_ge(masked, t + 1)
                            if t >= 2:
                                pe.wait_ge(read_out, t - 1)
                            o = psum[:, D + (t % 2) * 512:D + (t % 2) * 512 + C]
                            m = nc.tensor.matmul(o, local[:, t % 2, :], val[:, t, :], start=True, stop=(t == 0))
                            if t >= 1:
                                m = nc.tensor.matmul(o, featT[:, 1, s], memory[:, (t - 1) % 2, :], start=False, stop=True)
                            m.then_inc(read, 1)

                    @block.vector
                    def _(dve):
                        for t in range(NT):
                            dve.wait_ge(scored, t + 1)
                            if t >= 2:
                                dve.wait_ge(read, t - 1)
                            nc.vector.tensor_tensor(local[:, t % 2, :], psum[:, A + (t % 2) * 512:A + (t % 2) * 512 + P],
                                                    upto_q, ALU.mult).then_inc(masked, 1)
                            dve.wait_ge(grown, t + 1)
                            if t == 0:
                                nc.vector.tensor_copy(memory[:, 0, :], psum[:, B:B + C]).then_inc(kept, 1)
                            else:
                                dve.wait_ge(kept, t)
                                nc.vector.tensor_tensor(memory[:, t % 2, :], memory[:, (t - 1) % 2, :], psum[:, B:B + C],
                                                        ALU.add).then_inc(kept, 1)
                            dve.wait_ge(read, t + 1)
                            nc.vector.tensor_scalar(ret[:, t, :], psum[:, D + (t % 2) * 512:D + (t % 2) * 512 + C],
                                                    pos_norm[:, t:t + 1], None, ALU.mult).then_inc(read_out, 1)
                layer_norm(src=ret, dst=y_tok, want_T=False)
                with ph.phase("scaled", "turned", "dve_step") as (block, scaled, turned, dve_step):
                    @block.vector
                    def _(dve):
                        step = Steps(dve, dve_step)
                        step(nc.vector.tensor_tensor(y_tok[:], y_tok[:], bc(a_g, [P, NT, C], 1), ALU.mult))
                        nc.vector.tensor_tensor(y_tok[:], y_tok[:], bc(a_b, [P, NT, C], 1), ALU.add).then_inc(scaled, 1)

                    @block.tensor
                    def _(pe):
                        pe.wait_ge(scaled, 1)
                        turn_tiles(A, y_tok, C).then_inc(turned, 1)

                    @block.scalar
                    def _(act):
                        act.wait_ge(turned, 1)
                        nc.scalar.copy(yT[0:C, :], psum[0:C, A:A + NP])
            project_add([yT], [a_ow], a_ob, extra=x_tok)

        def turn_y(src):
            with ph.phase("turned") as (block, turned):
                @block.tensor
                def _(pe):
                    turn_tiles(A, src, C).then_inc(turned, 1)

                @block.scalar
                def _(act):
                    act.wait_ge(turned, 1)
                    nc.scalar.copy(yT[0:C, :], psum[0:C, A:A + NP])

        def rotary_moe():
            layer_norm()
            layer_norm(rms_weight=f_ln1, src=x_tok, dst=y_tok)
            with ExitStack() as c2:
                def b(name, shape):
                    return c2.enter_context(scratch(name, shape))
                qkv = b("qkv", [P, NT, P])
                q_all, k_all, v_all = b("q_all", [P, NT, C]), b("k_all", [P, NT, C]), b("v_all", [P, NT, C])
                rot = b("rot", [P, NT, 6, 16])
                buf = head_buffers(c2, 16)
                with ph.phase("qkv_in", "dve_step") as (block, qkv_in, dve_step):
                    @block.tensor
                    def _(pe):
                        for t in range(NT):
                            last = nc.tensor.matmul(psum[:, A + t * P:A + (t + 1) * P], xT[:, t * P:(t + 1) * P], f_qkv,
                                                    start=True, stop=True)
                        last.then_inc(qkv_in, 1)

                    @block.vector
                    def _(dve):
                        step = Steps(dve, dve_step)
                        dve.wait_ge(qkv_in, 1)
                        step(nc.vector.tensor_copy(flat(qkv), psum[:, A:A + NP]))
                        qk = qkv[:, :, 0:96].rearrange("p t (h d) -> p t h d", d=16)
                        step(nc.vector.tensor_tensor(rot[:, :, :, 0:8], qk[:, :, :, 8:16],
                                                     bc(sin[:, :, 0:8], [P, NT, 6, 8], 2), ALU.mult))
                        step(nc.vector.tensor_tensor(rot[:, :, :, 8:16], qk[:, :, :, 0:8],
                                                     bc(sin[:, :, 8:16], [P, NT, 6, 8], 2), ALU.mult))
                        step(nc.vector.tensor_tensor(qk, qk, bc(cos, [P, NT, 6, 16], 2), ALU.mult))
                        r6 = rot[:].rearrange("p t h d -> p t (h d)")
                        nc.vector.tensor_tensor(q_all[:], qkv[:, :, 0:64], r6[:, :, 0:64], ALU.add)
                        for h in range(4):
                            g = h // 2
                            nc.vector.tensor_tensor(k_all[:, :, h * 16:h * 16 + 16], qkv[:, :, 64 + g * 16:80 + g * 16],
                                                    r6[:, :, 64 + g * 16:80 + g * 16], ALU.add)
                            nc.vector.tensor_copy(v_all[:, :, h * 16:h * 16 + 16], qkv[:, :, 96 + g * 16:112 + g * 16])
                init_head(buf, 16, 32)
                rotary_heads(q_all, k_all, v_all, buf)
            turn_y(y_tok)
            with ph.phase("projected", "dve_step") as (block, projected, dve_step):
                @block.tensor
                def _(pe):
                    for t in range(NT):
                        last = nc.tensor.matmul(psum[:, A + t * C:A + (t + 1) * C], yT[:, t * P:(t + 1) * P], f_wo,
                                                start=True, stop=True)
                    last.then_inc(projected, 1)

                @block.vector
                def _(dve):
                    dve.wait_ge(projected, 1)
                    nc.vector.tensor_tensor(flat(x_tok), flat(x_tok), psum[:, A:A + NT * C], ALU.add)
            layer_norm(rms_weight=f_ln2, src=x_tok, dst=y_tok)
            route(lambda t, o: nc.tensor.matmul(o, xT[:, t * P:(t + 1) * P], f_router, start=True, stop=True),
                  True, 1e-9, 0.0)
            with scratch("gate", [HB, 2, NP]) as gate, \
                    scratch("hid", [HB, 2, NP]) as hid, \
                    scratch("part", [P, 2, NT, C]) as part, \
                    ph.phase("gate_in", "up_in", "gated", "hid_out", "expert_out", "weighed", "dve_step") as (
                        block, gate_in, up_in, gated, hid_out, expert_out, weighed, dve_step):
                @block.tensor
                def _(pe):
                    def down(e):
                        pe.wait_ge(hid_out, 2 * e + 2)
                        if e >= 1:
                            pe.wait_ge(weighed, e)
                        for t in range(NT):
                            o = psum[:, D + t * C:D + (t + 1) * C]
                            for j in range(2):
                                last = nc.tensor.matmul(o, hid[:, j, t * P:(t + 1) * P], f_w2[:, 2 * e + j, :],
                                                        start=(j == 0), stop=(j == 1))
                        last.then_inc(expert_out, 1)

                    for i in range(2 * NE):
                        w = slice(i * HB, (i + 1) * HB)
                        if i >= 1:
                            pe.wait_ge(gated, i)
                        columns(A, HB, [(f_w1[:, w], xT[:])]).then_inc(gate_in, 1)
                        if i >= 1:
                            pe.wait_ge(hid_out, i)
                        columns(B, HB, [(f_w3[:, w], xT[:])]).then_inc(up_in, 1)
                        if i % 2 == 1:
                            down(i // 2)

                @block.scalar
                def _(act):
                    for i in range(2 * NE):
                        act.wait_ge(gate_in, i + 1)
                        if i >= 2:
                            act.wait_ge(hid_out, i - 1)
                        nc.scalar.activation(gate[:, i % 2, :], psum[0:HB, A:A + NP], ACT.Silu).then_inc(gated, 1)

                @block.vector
                def _(dve):
                    for i in range(2 * NE):
                        e = i // 2
                        dve.wait_ge(gated, i + 1)
                        dve.wait_ge(up_in, i + 1)
                        if e >= 1:
                            dve.wait_ge(expert_out, e)
                        nc.vector.tensor_tensor(hid[:, i % 2, :], gate[:, i % 2, :], psum[0:HB, B:B + NP],
                                                ALU.mult).then_inc(hid_out, 1)
                        if i % 2 == 1:
                            dve.wait_ge(expert_out, e + 1)
                            o = psum[:, D:D + NT * C].rearrange("p (t c) -> p t c", c=C)
                            nc.vector.tensor_tensor(part[:, e % 2], o, bc(rt_w[:, :, e], [P, NT, C], 2),
                                                    ALU.mult).then_inc(weighed, 1)
                            dve.wait_ge(weighed, e + 1)
                            dve.wait_ge(dve_step, e) if e else None
                            nc.vector.tensor_tensor(flat(x_tok), flat(x_tok), part[:, e % 2].rearrange("p t c -> p (t c)"),
                                                    ALU.add).then_inc(dve_step, 1)
                    dve.wait_ge(dve_step, NE)
                    nc.vector.tensor_tensor(flat(h_tok), flat(h_tok), flat(x_tok), ALU.add)

        def state_space():
            layer_norm()
            with ExitStack() as c2:
                def b(name, shape):
                    return c2.enter_context(scratch(name, shape))
                xin = b("xin", [P, TAPS - 1 + NP])
                w_rep = b("w_rep", [P, 1 + 2 * NSTATE, P])
                gz, u, dt, dtu, ys = b("gz", [P, NP]), b("u", [P, NP]), b("dt", [P, NP]), b("dtu", [P, NP]), b("ys", [P, NP])
                decay, drive, state, part = b("decay", [P, 2, NP]), b("drive", [P, 2, NP]), b("state", [P, 2, NP]), b("part", [P, 2, NP])
                with ph.phase("xz_in", "gate_out", "repeated", "u_out", "dt_in", "pre_out", "e_out", "l_out",
                              "dve_step") as (block, xz_in, gate_out, repeated, u_out, dt_in, pre_out, e_out, l_out,
                                              dve_step):
                    @block.gpsimd
                    def _(pool):
                        nc.gpsimd.tensor_copy(w_rep[:], bc(m_xp, [P, 1 + 2 * NSTATE, P], 2)).then_inc(repeated, 1)

                    @block.tensor
                    def _(pe):
                        columns(A, P, [(m_in[:, 0:P], xT[:])]).then_inc(xz_in, 1)
                        columns(B, P, [(m_in[:, P:2 * P], xT[:])]).then_inc(xz_in, 1)
                        pe.wait_ge(u_out, 1)
                        pe.wait_ge(repeated, 1)
                        columns(A, P, [(w_rep[:, 0, :], u[:])]).then_inc(dt_in, 1)

                    @block.scalar
                    def _(act):
                        act.wait_ge(xz_in, 2)
                        nc.scalar.activation(gz[:], psum[:, B:B + NP], ACT.Sigmoid).then_inc(gate_out, 1)
                        act.wait_ge(pre_out, 1)
                        nc.scalar.activation(gz[:], gz[:], ACT.Exp, scale=-1.0).then_inc(e_out, 1)
                        act.wait_ge(e_out, 1)
                        nc.scalar.activation(gz[:], gz[:], ACT.Ln, bias=ones[:, 0:1]).then_inc(l_out, 1)

                    @block.vector
                    def _(dve):
                        step = Steps(dve, dve_step)
                        nc.vector.memset(xin[:, 0:TAPS - 1], 0.0)
                        dve.wait_ge(xz_in, 1)
                        step(nc.vector.tensor_copy(xin[:, TAPS - 1:], psum[:, A:A + NP]))
                        step(nc.vector.tensor_scalar(u[:], xin[:, 0:NP], m_cw[:, 0:1], m_cb[:, 0:1], ALU.mult, ALU.add))
                        for k in range(1, TAPS):
                            step(nc.vector.scalar_tensor_tensor(u[:], xin[:, k:k + NP], m_cw[:, k:k + 1], u[:],
                                                                ALU.mult, ALU.add))
                        dve.wait_ge(gate_out, 1)
                        nc.vector.tensor_tensor(u[:], u[:], gz[:], ALU.mult).then_inc(u_out, 1)
                        dve.wait_ge(dt_in, 1)
                        step(nc.vector.tensor_scalar(dtu[:], psum[:, A:A + NP], m_wdt[:, 0:1], m_bdt[:, 0:1],
                                                     ALU.mult, ALU.add))
                        nc.vector.scalar_tensor_tensor(gz[:], dtu[:], -1.0, dtu[:], ALU.mult, ALU.max).then_inc(pre_out, 1)
                        dve.wait_ge(l_out, 1)
                        step(nc.vector.scalar_tensor_tensor(dt[:], dtu[:], 0.0, gz[:], ALU.max, ALU.add))
                        nc.vector.tensor_tensor(dtu[:], dt[:], u[:], ALU.mult)
                        nc.vector.tensor_scalar(ys[:], u[:], m_D[:, 0:1], None, ALU.mult)

                with ph.phase("decayed", "b_in", "c_in", "driven", "scanned", "shown", "summed") as (
                        block, decayed, b_in, c_in, driven, scanned, shown, summed):
                    @block.tensor
                    def _(pe):
                        for n in range(NSTATE):
                            if n >= 1:
                                pe.wait_ge(driven, n)
                            columns(A, P, [(w_rep[:, 1 + n, :], u[:])]).then_inc(b_in, 1)
                            if n >= 1:
                                pe.wait_ge(shown, n)
                            columns(B, P, [(w_rep[:, 1 + NSTATE + n, :], u[:])]).then_inc(c_in, 1)

                    @block.scalar
                    def _(act):
                        for n in range(NSTATE):
                            if n >= 2:
                                act.wait_ge(scanned, n - 1)
                            nc.scalar.activation(decay[:, n % 2, :], dt[:], ACT.Exp, scale=m_A[:, n:n + 1]).then_inc(decayed, 1)

                    @block.vector
                    def _(dve):
                        for n in range(NSTATE):
                            s = n % 2
                            dve.wait_ge(b_in, n + 1)
                            if n >= 2:
                                dve.wait_ge(scanned, n - 1)
                            nc.vector.tensor_tensor(drive[:, s, :], dtu[:], psum[:, A:A + NP], ALU.mult).then_inc(driven, 1)
                            dve.wait_ge(driven, n + 1)
                            dve.wait_ge(decayed, n + 1)
                            if n >= 2:
                                dve.wait_ge(shown, n - 1)
                            nc.vector.tensor_tensor_scan(state[:, s, :], decay[:, s, :], drive[:, s, :], 0.0,
                                                         ALU.mult, ALU.add).then_inc(scanned, 1)
                            dve.wait_ge(scanned, n + 1)
                            dve.wait_ge(c_in, n + 1)
                            if n >= 2:
                                dve.wait_ge(summed, n - 1)
                            nc.vector.tensor_tensor(part[:, s, :], state[:, s, :], psum[:, B:B + NP], ALU.mult).then_inc(shown, 1)

                    @block.gpsimd
                    def _(pool):
                        for n in range(NSTATE):
                            pool.wait_ge(shown, n + 1)
                            if n >= 1:
                                pool.wait_ge(summed, n)
                            nc.gpsimd.tensor_tensor(ys[:], ys[:], part[:, n % 2, :], ALU.add).then_inc(summed, 1)
                project_add([ys], [m_out], None)

        dram_kv = nc.dram_tensor("dram_kv", [N_BATCH, N_TOK, PKH, P], F32, kind="Internal").ap()
        dram_q = nc.dram_tensor("dram_q", [N_BATCH, N_TOK, 512], F32, kind="Internal").ap()
        FULL = (NT - 1) * P

        def key_queries(b, qpkT):
            layer_norm()
            with scratch("q_all", [P, NT, 512]) as q_all, \
                    ph.phase("q_in", "q_out", "q_stored") as (block, q_in, q_out, q_stored):
                @block.tensor
                def _(pe):
                    for t in range(NT):
                        if t >= 2:
                            pe.wait_ge(q_out, t - 1)
                        nc.tensor.matmul(psum[:, D + (t % 2) * 512:D + (t % 2 + 1) * 512], xT[:, t * P:(t + 1) * P],
                                         k_wq, start=True, stop=True).then_inc(q_in, 1)
                    for c in range(4):
                        if c >= 2:
                            pe.wait_ge(q_out, NT + c - 1)
                        columns(A if c % 2 == 0 else B, P, [(k_wqpk[:, c * P:(c + 1) * P], xT[:])]).then_inc(q_in, 1)

                @block.scalar
                def _(act):
                    for t in range(NT):
                        act.wait_ge(q_in, t + 1)
                        nc.scalar.mul(q_all[:, t, :], psum[:, D + (t % 2) * 512:D + (t % 2 + 1) * 512],
                                      C ** -0.5).then_inc(q_out, 1)
                    for c in range(4):
                        r = A if c % 2 == 0 else B
                        act.wait_ge(q_in, NT + c + 1)
                        nc.scalar.copy(qpkT[:, c, :], psum[:, r:r + NP]).then_inc(q_out, 1)

                @block.sync
                def _(sp):
                    sp.wait_ge(q_out, NT)
                    qb = dram_q[bass.ds(b, 1)].rearrange("a n c -> (a n) c")
                    sp.dma_start(qb[0:FULL].rearrange("(t p) c -> p t c", p=P), q_all[:, 0:NT - 1, :]).then_inc(q_stored, 16)
                    sp.dma_start(qb[FULL:N_TOK], q_all[0:N_TOK - FULL, NT - 1, :]).then_inc(q_stored, 16)
                    sp.wait_ge(q_stored, 32)

        SEARCH_SEMS = ("staged", "half_in", "sims", "shifted", "exps", "found", "search_step")

        class Search:

            def __init__(self, sems, buf):
                self.staged, self.half_in, self.sims, self.shifted, self.exps, self.found, self.step_sem = sems
                (self.qpkT, self.qt, self.sim, self.sim2, self.best, self.bidx, self.bidf, self.cand, self.cand2,
                 self.cidx, self.fin, self.fpos, self.fposf, self.wgt, self.wsum, self.hot, self.gidf) = buf

            def stage(self, tile):
                nc.scalar.copy(self.qt[:], self.qpkT[:, :, tile]).then_inc(self.staged, 1)

            def fetch(self, act):
                for half in range(2):
                    act.wait_ge(self.half_in, half + 1)
                    nc.scalar.copy(self.sim[:, half * 512:(half + 1) * 512], psum[:, D + 512:D + 1024]).then_inc(self.sims, 1)

            def exponentials(self, act):
                act.wait_ge(self.shifted, 1)
                nc.scalar.activation(self.wgt[:], self.wgt[:], ACT.Exp).then_inc(self.exps, 1)

            def run_tensor(self, pe):
                pe.wait_ge(self.staged, 1)
                for half in range(2):
                    if half:
                        pe.wait_ge(self.sims, half)
                    for j in range(2):
                        last = nc.tensor.matmul(psum[:, D + 512 + j * 256:D + 768 + j * 256], self.qt[:, 2 * half + j, :],
                                                k_keys[:, 2 * half + j, :], start=True, stop=True)
                    last.then_inc(self.half_in, 1)

            def begin(self, dve):
                self.step = Steps(dve, self.step_sem)
                self.dve = dve

            def half(self, half):
                self.dve.wait_ge(self.sims, half + 1)
                sim = self.sim[:].rearrange("p (g k) -> p g k", k=PKK)
                best, bidx, sim2 = self.best, self.bidx, self.sim2
                G = range(half * PKH, (half + 1) * PKH)
                for g in G:
                    ins = nc.vector.max(best[:, g, 0:8], sim[:, g, :])
                self.step(ins)
                for g in G:
                    nc.vector.max_index(bidx[:, g, 0:8], best[:, g, 0:8], sim[:, g, :])
                    ins = nc.vector.match_replace(sim2[:, g, :], best[:, g, 0:8], sim[:, g, :], LOWEST)
                self.step(ins)
                for g in G:
                    ins = nc.vector.max(best[:, g, 8:16], sim2[:, g, :])
                self.step(ins)
                for g in G:
                    ins = nc.vector.max_index(bidx[:, g, 8:16], best[:, g, 8:16], sim2[:, g, :])
                self.step(ins)

            def pairs(self):
                step, best, bidf = self.step, self.best, self.bidf
                step(nc.vector.tensor_copy(flat(bidf), flat(self.bidx)))
                step(nc.vector.tensor_scalar(bidf[:, PKH:, :], bidf[:, PKH:, :], float(PKK), None, ALU.mult))
                step(nc.vector.tensor_tensor(bidf[:, 0:PKH, :], bidf[:, 0:PKH, :],
                                             bc(headoff, [P, PKH, TOPK], 2), ALU.add))
                for dst, src in ((self.cand, best), (self.cidx, bidf)):
                    for o, i0, i1, nj in PAIRS:
                        ni = i1 - i0
                        d = dst[:, :, o:o + ni * nj].rearrange("p h (i j) -> p h i j", j=nj)
                        ins = nc.vector.tensor_tensor(d, bc(src[:, 0:PKH, i0:i1], [P, PKH, ni, nj], 3),
                                                      bc(src[:, PKH:, 0:nj], [P, PKH, ni, nj], 2), ALU.add)
                step(ins)

            def top_pairs(self):
                step, fin, fpos, cand, cand2 = self.step, self.fin, self.fpos, self.cand, self.cand2
                for h in range(PKH):
                    ins = nc.vector.max(fin[:, h, 0:8], cand[:, h, :])
                step(ins)
                for h in range(PKH):
                    nc.vector.max_index(fpos[:, h, 0:8], fin[:, h, 0:8], cand[:, h, :])
                    ins = nc.vector.match_replace(cand2[:, h, :], fin[:, h, 0:8], cand[:, h, :], LOWEST)
                step(ins)
                for h in range(PKH):
                    ins = nc.vector.max(fin[:, h, 8:16], cand2[:, h, :])
                step(ins)
                nc.vector.tensor_tensor(self.wgt[:], fin[:], fin[:, :, 0:1].broadcast_to([P, PKH, TOPK]),
                                        ALU.subtract).then_inc(self.shifted, 1)
                for h in range(PKH):
                    ins = nc.vector.max_index(fpos[:, h, 8:16], fin[:, h, 8:16], cand2[:, h, :])
                step(ins)
                step(nc.vector.tensor_copy(flat(self.fposf), flat(fpos)))

            def rows_of(self, heads):
                for h in heads:
                    s = self.hot[:]
                    self.step(nc.vector.tensor_tensor(s, bc(self.fposf[:, h, :], [P, TOPK, NPAIR], 2),
                                                      bc(iota, [P, TOPK, NPAIR], 1), ALU.is_equal))
                    self.step(nc.vector.tensor_tensor(s, s, bc(self.cidx[:, h, :], [P, TOPK, NPAIR], 1), ALU.mult))
                    self.step(nc.vector.tensor_reduce(self.gidf[:, h, :], s, AX.X, ALU.add))

            def weights(self):
                self.dve.wait_ge(self.exps, 1)
                self.step(nc.vector.tensor_reduce(self.wsum[:, 0], self.wgt[:], AX.X, ALU.add))
                self.step(nc.vector.reciprocal(self.wsum[:, 1], self.wsum[:, 0]))
                self.step(nc.vector.tensor_tensor(self.wgt[:], self.wgt[:], bc(self.wsum[:, 1], [P, PKH, TOPK], 2), ALU.mult))

        def search_buffers(c2, qpkT):
            def b(name, shape, dt=F32):
                return c2.enter_context(scratch(name, shape, dt))
            return [qpkT, b("qt", [P, 4, P]), b("sim", [P, 16 * PKK]), b("sim2", [P, 16, PKK]), b("best", [P, 16, TOPK]),
                    b("bidx", [P, 16, TOPK], U32), b("bidf", [P, 16, TOPK]), b("cand", [P, PKH, NPAIR]),
                    b("cand2", [P, PKH, NPAIR]), b("cidx", [P, PKH, NPAIR]), b("fin", [P, PKH, TOPK]),
                    b("fpos", [P, PKH, TOPK], U32), b("fposf", [P, PKH, TOPK]), b("wgt", [P, PKH, TOPK]),
                    b("wsum", [P, 2, PKH]), b("hot", [P, TOPK, NPAIR]), b("gidf", [P, PKH, TOPK])]

        def slots(b_rows, b_heads, qpkT, y_all):
            with ExitStack() as c2:
                def b(name, shape, dt=F32):
                    return c2.enter_context(scratch(name, shape, dt))
                if b_heads is not None:
                    hbuf = head_buffers(c2, C)
                    init_head(hbuf, C, C)
                if b_rows is not None:
                    sbuf = search_buffers(c2, qpkT)
                    gidx = b("gidx", [P, PKH, TOPK], U32)
                    wnow = b("wnow", [P, PKH, TOPK])
                    rows = b("rows", [P, 2, TOPK, P])
                    acc = b("acc", [P, 2, P])
                    kv_tile = b("kv_tile", [P, PKH, P])
                    lastcol, lastw = b("lastcol", [P, 1]), b("lastw", [P, PKH])
                    lastix = b("lastix", [P, 1], U32)
                    with ph.phase(*SEARCH_SEMS) as (block, *sems):
                        first = Search(sems, sbuf)

                        @block.scalar
                        def _(act):
                            first.stage(slice(0, P))
                            first.fetch(act)
                            first.exponentials(act)

                        @block.tensor
                        def _(pe):
                            first.run_tensor(pe)

                        @block.vector
                        def _(dve):
                            first.begin(dve)
                            first.half(0)
                            first.half(1)
                            first.pairs()
                            first.top_pairs()
                            first.rows_of(range(PKH))
                            first.weights()

                with nc.Fori(0, NT - 1) as t:
                    with ph.phase(*HEAD_SEMS, *SEARCH_SEMS, "head_in", "rows_named", "rows_even", "rows_odd", "rows_used",
                                  "acc_even", "acc_odd", "tile_stored") as (block, *sems):
                        (head_in, rows_named, rows_even, rows_odd, rows_used, acc_even, acc_odd, tile_stored) = sems[-8:]
                        if b_heads is not None:
                            head = Head(sems[:len(HEAD_SEMS)], hbuf, C, C, 1.0)
                        if b_rows is not None:
                            search = Search(sems[len(HEAD_SEMS):-8], sbuf)

                        @block.sync
                        def _(sp):
                            if b_heads is not None:
                                kv = dram_kv[bass.ds(b_heads, 1), :, bass.ds(t, 1), :].rearrange("a n h d -> (a n) (h d)")
                                qb = dram_q[bass.ds(b_heads, 1), :, bass.ds(t * C, C)].rearrange("a n c -> (a n) c")
                                for dst, src in ((head.q_h, qb), (head.k_h, kv[:, 0:C]), (head.v_h, kv[:, C:P])):
                                    sp.dma_start(dst[:, 0:NT - 1, 0:C], src[0:FULL].rearrange("(t p) c -> p t c", p=P)
                                                 ).then_inc(head_in, 16)
                                    sp.dma_start(dst[0:N_TOK - FULL, NT - 1, 0:C], src[FULL:N_TOK]).then_inc(head_in, 16)
                            if b_rows is not None:
                                sp.wait_ge(rows_used, PKH)
                                sp.dma_start(dram_kv[bass.ds(b_rows, 1), bass.ds(t * P, P)].rearrange("a n h d -> (a n) (h d)"),
                                             flat(kv_tile)).then_inc(tile_stored, 16)
                                sp.wait_ge(tile_stored, 16)

                        @block.scalar
                        def _(act):
                            if b_rows is not None:
                                search.stage(bass.ds(t * P + P, P))
                                search.fetch(act)
                            if b_heads is not None:
                                head.run_scalar(act)
                            if b_rows is not None:
                                search.exponentials(act)

                        @block.tensor
                        def _(pe):
                            if b_rows is not None:
                                search.run_tensor(pe)
                            if b_heads is not None:
                                pe.wait_ge(head_in, 96)
                                head.run_tensor(pe)

                        @block.gpsimd
                        def _(pool):
                            if b_rows is None:
                                return
                            pool.wait_ge(rows_named, 1)
                            for h in range(PKH):
                                if h >= 2:
                                    pool.wait_ge(rows_used, h - 1)
                                for k in range(TOPK):
                                    nc.gpsimd.indirect_dma_start(
                                        out=rows[:, h % 2, k, :], out_offset=None, in_=io["k_table"],
                                        in_offset=bass.IndirectOffsetOnAxis(ap=gidx[:, h, k:k + 1], axis=0),
                                    ).then_inc(rows_even if h % 2 == 0 else rows_odd, 16)
                            for s in (rows_even, rows_odd):
                                pool.wait_ge(s, 16 * TOPK * PKH // 2)
                            nc.gpsimd.dma_reset()

                        @block.vector
                        def _(dve):
                            def sum_rows(h):
                                dve.wait_ge(rows_even if h % 2 == 0 else rows_odd, 16 * TOPK * (h // 2 + 1))
                                for k in range(TOPK):
                                    s, sem = k % 2, (acc_even, acc_odd)[k % 2]
                                    n = (TOPK // 2) * h + k // 2
                                    if k >= 2 or h:
                                        dve.wait_ge(sem, n)
                                    if k == 0 and h:
                                        dve.wait_ge(rows_used, h)
                                    if k < 2:
                                        ins = nc.vector.tensor_scalar(acc[:, s], rows[:, h % 2, k, :], wnow[:, h, k:k + 1],
                                                                      None, ALU.mult)
                                    else:
                                        ins = nc.vector.scalar_tensor_tensor(acc[:, s], rows[:, h % 2, k, :],
                                                                             wnow[:, h, k:k + 1], acc[:, s],
                                                                             ALU.mult, ALU.add)
                                    ins.then_inc(sem, 1)
                                for sem in (acc_even, acc_odd):
                                    dve.wait_ge(sem, (TOPK // 2) * (h + 1))
                                nc.vector.tensor_tensor(kv_tile[:, h, :], acc[:, 0], acc[:, 1], ALU.add).then_inc(rows_used, 1)

                            if b_rows is not None:
                                nc.vector.tensor_copy(flat(gidx), flat(search.gidf)).then_inc(rows_named, 1)
                                nc.vector.tensor_copy(flat(wnow), flat(search.wgt)).then_inc(rows_named, 1)
                                dve.wait_ge(rows_named, 2)
                                search.begin(dve)
                            if b_heads is not None:
                                head.clear_row()
                            for h in range(PKH):
                                if b_rows is not None:
                                    if h < 2:
                                        search.half(h)
                                    if h == 2:
                                        search.pairs()
                                        search.top_pairs()
                                    if h >= 3 and h < 7:
                                        search.rows_of(range(2 * h - 6, 2 * h - 4))
                                if b_heads is not None:
                                    if h < 3:
                                        head.max_tiles(dve, range(3 * h, 3 * h + 3))
                                    if h == 2:
                                        head.row_of_max(dve)
                                    if h == 7:
                                        head.normalize(dve, lambda t0, t1: y_all[:, t0:t1, bass.ds(t * C, C)])
                                if b_rows is not None:
                                    if h == 7:
                                        search.weights()
                                    sum_rows(h)
                    ph.close_loop()

                if b_rows is None:
                    return
                with ph.phase("stood", "last_ix", "last_rows", "last_in", "last_out", "dve_step") as (
                        block, stood, last_ix, last_rows, last_in, last_out, dve_step):
                    found = Search([None] * 7, sbuf)

                    @block.tensor
                    def _(pe):
                        nc.tensor.transpose(psum[:, B:B + 1], found.gidf[0:1].rearrange("p h k -> p (h k)"), ident[0:1, 0:1])
                        nc.tensor.transpose(psum[:, B + 1:B + 2], found.wgt[0:1].rearrange("p h k -> p (h k)"),
                                            ident[0:1, 0:1]).then_inc(stood, 1)
                        pe.wait_ge(last_ix, 2)
                        pe.wait_ge(last_rows, 16)
                        for h in range(PKH):
                            m = nc.tensor.matmul(psum[0:1, D + h * P:D + (h + 1) * P], lastw[:, h:h + 1], rows[:, 0, 0, :],
                                                 start=True, stop=True)
                        m.then_inc(last_in, 1)

                    @block.gpsimd
                    def _(pool):
                        pool.wait_ge(last_ix, 1)
                        nc.gpsimd.indirect_dma_start(out=rows[:, 0, 0, :], out_offset=None, in_=io["k_table"],
                                                     in_offset=bass.IndirectOffsetOnAxis(ap=lastix[:, 0:1], axis=0),
                                                     ).then_inc(last_rows, 16)
                        pool.wait_ge(last_rows, 16)
                        nc.gpsimd.dma_reset()

                    @block.vector
                    def _(dve):
                        step = Steps(dve, dve_step)
                        dve.wait_ge(stood, 1)
                        nc.vector.tensor_copy(lastix[:], psum[:, B:B + 1]).then_inc(last_ix, 1)
                        step(nc.vector.tensor_copy(lastcol[:], psum[:, B + 1:B + 2]))
                        nc.vector.tensor_scalar(lastw[:], headrow, lastcol[:], None, ALU.mult).then_inc(last_ix, 1)
                        dve.wait_ge(last_in, 1)
                        nc.vector.tensor_copy(kv_tile[0:1].rearrange("p h d -> p (h d)"),
                                              psum[0:1, D:D + PKH * P]).then_inc(last_out, 1)

                    @block.sync
                    def _(sp):
                        sp.wait_ge(last_out, 1)
                        sp.dma_start(dram_kv[bass.ds(b_rows, 1), FULL:N_TOK].rearrange("a n h d -> (a n) (h d)"),
                                     kv_tile[0:1].rearrange("p h d -> p (h d)")).then_inc(last_out, 16)
                        sp.wait_ge(last_out, 17)

        def heads_out(y_all):
            with scratch("yaT", [P, 4, NP]) as yaT:
                with ph.phase("turned", "turned_out") as (block, turned, turned_out):
                    @block.tensor
                    def _(pe):
                        for c in range(4):
                            if c >= 2:
                                pe.wait_ge(turned_out, c - 1)
                            turn_tiles(A if c % 2 == 0 else B, y_all[:, :, c * P:(c + 1) * P], P).then_inc(turned, 1)

                    @block.scalar
                    def _(act):
                        for c in range(4):
                            r = A if c % 2 == 0 else B
                            act.wait_ge(turned, c + 1)
                            nc.scalar.copy(yaT[:, c, :], psum[:, r:r + NP]).then_inc(turned_out, 1)
                project_add([yaT[:, c] for c in range(4)], [k_wo[:, c] for c in range(4)], None)

        def slices():
            layer_norm()
            with ExitStack() as c2:
                def b(name, shape):
                    return c2.enter_context(scratch(name, shape))
                t_tok = b("t_tok", [P, NT, C + 1])
                tT = b("tT", [C, NP])
                sw = b("sw", [P, NT, 8, C])
                swT = b("swT", [P, 4, NP])
                red = b("red", [P, NT, 2, 8])
                tokn = b("tokn", [P, 4, C])
                nrm = b("nrm", [P, 2, 4])
                tokT = b("tokT", [C, 512])
                qs, ks = b("qs", [8, 512]), b("ks", [8, 512])
                vs = b("vs", [C, 8, 8])
                att = b("att", [C, 8, C])
                attT = b("attT", [C, 8, C])
                ared = b("ared", [C, 2, 8])
                obd = b("obd", [P, 4, C])
                oT = b("oT", [C, NP])
                with ph.phase("t_in", "t_out", "logit", "scaled", "swept", "exped", "sw_out", "dve_step", "pool_step") as (
                        block, t_in, t_out, logit, scaled, swept, exped, sw_out, dve_step, pool_step):
                    @block.tensor
                    def _(pe):
                        columns(A, C, [(s_win, xT[:])]).then_inc(t_in, 1)
                        for t in range(NT):
                            o = psum[:, D + t * C:D + (t + 1) * C]
                            nc.tensor.matmul(o, xT[:, t * P:(t + 1) * P], s_win, start=True, stop=False)
                            last = nc.tensor.matmul(o, ones[0:1, :], s_bin_row, start=False, stop=True)
                        last.then_inc(t_in, 1)
                        pe.wait_ge(t_out, 1)
                        for t in range(NT):
                            if t >= 2:
                                pe.wait_ge(scaled, t - 1)
                            o = psum[:, B + (t % 2) * 512:B + (t % 2 + 1) * 512]
                            nc.tensor.matmul(o, tT[:, t * P:(t + 1) * P], s_slice[:], start=True, stop=False)
                            nc.tensor.matmul(o, ones[0:1, :], s_bslice, start=False, stop=True).then_inc(logit, 1)

                    @block.scalar
                    def _(act):
                        act.wait_ge(t_in, 1)
                        nc.scalar.activation(tT[:], psum[0:C, A:A + NP], ACT.Identity, bias=s_bin_col).then_inc(t_out, 1)
                        for t in range(NT):
                            act.wait_ge(swept, t + 1)
                            nc.scalar.activation(sw[:, t], sw[:, t], ACT.Exp).then_inc(exped, 1)

                    @block.vector
                    def _(dve):
                        dve.wait_ge(t_in, 2)
                        o = psum[:, D:D + NT * C].rearrange("p (t c) -> p t c", c=C)
                        nc.vector.tensor_tensor(t_tok[:, :, 0:C], o, bc(valid, [P, NT, C], 2), ALU.mult)
                        nc.vector.tensor_copy(t_tok[:, :, C], valid)
                        step = Steps(dve, dve_step)

                        def finish(t):
                            dve.wait_ge(exped, t + 1)
                            step(nc.vector.tensor_reduce(red[:, t, 1], sw[:, t], AX.X, ALU.add))
                            step(nc.vector.reciprocal(red[:, t, 1], red[:, t, 1]))
                            nc.vector.tensor_tensor(sw[:, t], sw[:, t], bc(red[:, t, 1], [P, 8, C], 2),
                                                    ALU.mult).then_inc(sw_out, 1)
                        for t in range(NT):
                            dve.wait_ge(logit, t + 1)
                            o = psum[:, B + (t % 2) * 512:B + (t % 2 + 1) * 512].rearrange("p (h g) -> p h g", g=C)
                            nc.vector.tensor_tensor(sw[:, t], o, bc(s_rtemp[:], [P, 8, C], 2), ALU.mult).then_inc(scaled, 1)
                            dve.wait_ge(scaled, t + 1)
                            step(nc.vector.tensor_reduce(red[:, t, 0], sw[:, t], AX.X, ALU.max))
                            nc.vector.tensor_tensor(sw[:, t], sw[:, t], bc(red[:, t, 0], [P, 8, C], 2),
                                                    ALU.subtract).then_inc(swept, 1)
                            if t >= 1:
                                finish(t - 1)
                        finish(NT - 1)

                with ph.phase("sliced", "normed", "turned", "tokT_out", "qkv_in", "qkv_out", "sim", "shifted", "exped",
                              "att_out", "att_turned", "attT_out", "mixed", "cleared", "obd_out", "sw_turned",
                              "swT_out", "dve_step") as (
                        block, sliced, normed, turned, tokT_out, qkv_in, qkv_out, sim, shifted, exped, att_out,
                        att_turned, attT_out, mixed, cleared, obd_out, sw_turned, swT_out, dve_step):
                    @block.tensor
                    def _(pe):
                        for c in range(4):
                            o = psum[:, A + c * 512:A + c * 512 + C + 1]
                            for t in range(NT):
                                last = nc.tensor.matmul(o, sw[:, t, 2 * c:2 * c + 2, :].rearrange("p h g -> p (h g)"),
                                                        t_tok[:, t, :], start=(t == 0), stop=(t == NT - 1))
                        last.then_inc(sliced, 1)
                        pe.wait_ge(normed, 1)
                        for c in range(4):
                            last = nc.tensor.transpose(psum[0:C, D + c * P:D + (c + 1) * P], tokn[:, c, :], ident)
                        last.then_inc(turned, 1)
                        pe.wait_ge(tokT_out, 1)
                        nc.tensor.matmul(psum[0:8, A:A + 512], s_qkvw[:, 0:8], tokT[:], start=True, stop=True)
                        nc.tensor.matmul(psum[0:8, A + 512:A + 1024], s_qkvw[:, 8:16], tokT[:], start=True, stop=True)
                        for h in range(8):
                            o = psum[0:C, A + 1024 + 8 * h:A + 1024 + 8 * h + 8]
                            nc.tensor.matmul(o, tokT[:, h * C:(h + 1) * C], s_qkvw[:, 16:24], start=True, stop=False)
                            last = nc.tensor.matmul(o, ones[0:1, 0:C], s_bv, start=False, stop=True)
                        last.then_inc(qkv_in, 1)
                        pe.wait_ge(qkv_out, 2)
                        for h in range(8):
                            last = nc.tensor.matmul(psum[0:C, B + h * C:B + (h + 1) * C], qs[:, h * C:(h + 1) * C],
                                                    ks[:, h * C:(h + 1) * C], start=True, stop=True)
                        last.then_inc(sim, 1)
                        pe.wait_ge(att_out, 1)
                        for h in range(8):
                            last = nc.tensor.transpose(psum[0:C, B + 512 + h * C:B + 512 + (h + 1) * C], att[:, h, :],
                                                       ident[0:C, 0:C])
                        last.then_inc(att_turned, 1)
                        pe.wait_ge(attT_out, 1)
                        for h in range(8):
                            last = nc.tensor.matmul(psum[0:C, B + 1024 + 8 * h:B + 1024 + 8 * h + 8], attT[:, h, :],
                                                    vs[:, h, :], start=True, stop=True)
                        last.then_inc(mixed, 1)
                        for c in range(4):
                            if c >= 1:
                                pe.wait_ge(swT_out, c)
                            turn_tiles(A, sw[:, :, 2 * c:2 * c + 2, :].rearrange("p t h g -> p t (h g)"), P).then_inc(sw_turned, 1)
                        pe.wait_ge(swT_out, 4)
                        pe.wait_ge(obd_out, 1)
                        columns(A, C, [(obd[:, c, :], swT[:, c, :]) for c in range(4)]).then_inc(sw_turned, 1)

                    @block.scalar
                    def _(act):
                        act.wait_ge(turned, 1)
                        nc.scalar.copy(tokT[:], psum[0:C, D:D + 512]).then_inc(tokT_out, 1)
                        act.wait_ge(qkv_in, 1)
                        nc.scalar.activation(qs[:], psum[0:8, A:A + 512], ACT.Identity, bias=s_bq)
                        nc.scalar.activation(ks[:], psum[0:8, A + 512:A + 1024], ACT.Identity, bias=s_bk).then_inc(qkv_out, 1)
                        act.wait_ge(shifted, 1)
                        nc.scalar.activation(att[:], att[:], ACT.Exp, scale=8 ** -0.5).then_inc(exped, 1)
                        act.wait_ge(att_turned, 1)
                        nc.scalar.copy(attT[:].rearrange("p h g -> p (h g)"), psum[0:C, B + 512:B + 1024]).then_inc(attT_out, 1)
                        for c in range(4):
                            act.wait_ge(sw_turned, c + 1)
                            nc.scalar.copy(swT[:, c, :], psum[:, A:A + NP]).then_inc(swT_out, 1)
                        act.wait_ge(sw_turned, 5)
                        nc.scalar.copy(oT[:], psum[0:C, A:A + NP])

                    @block.vector
                    def _(dve):
                        step = Steps(dve, dve_step)
                        nc.vector.memset(obd[:], 0.0).then_inc(cleared, 1)
                        dve.wait_ge(sliced, 1)
                        sl = psum[:, A:A + 4 * 512].rearrange("p (c f) -> p c f", f=512)
                        step(nc.vector.tensor_scalar(nrm[:, 0], sl[:, :, C], 1e-5, None, ALU.add))
                        step(nc.vector.reciprocal(nrm[:, 1], nrm[:, 0]))
                        step(nc.vector.tensor_tensor(tokn[:], sl[:, :, 0:C], bc(nrm[:, 1], [P, 4, C], 2), ALU.mult))
                        nc.vector.tensor_tensor(tokn[:], tokn[:], ownhead, ALU.mult).then_inc(normed, 1)
                        dve.wait_ge(qkv_in, 1)
                        nc.vector.tensor_copy(vs[:].rearrange("p h d -> p (h d)"),
                                              psum[0:C, A + 1024:A + 1024 + 64]).then_inc(qkv_out, 1)
                        dve.wait_ge(sim, 1)
                        s = psum[0:C, B:B + 512].rearrange("p (h g) -> p h g", g=C)
                        step(nc.vector.tensor_reduce(ared[:, 0], s, AX.X, ALU.max))
                        nc.vector.tensor_tensor(att[:], s, bc(ared[:, 0], [C, 8, C], 2), ALU.subtract).then_inc(shifted, 1)
                        dve.wait_ge(exped, 1)
                        step(nc.vector.tensor_reduce(ared[:, 0], att[:], AX.X, ALU.add))
                        step(nc.vector.reciprocal(ared[:, 1], ared[:, 0]))
                        nc.vector.tensor_tensor(att[:], att[:], bc(ared[:, 1], [C, 8, C], 2), ALU.mult).then_inc(att_out, 1)
                        dve.wait_ge(mixed, 1)
                        dve.wait_ge(cleared, 1)
                        for h in range(8):
                            ins = nc.vector.tensor_copy(obd[64 * (h % 2):64 * (h % 2) + 64, h // 2, 8 * h:8 * h + 8],
                                                        psum[0:C, B + 1024 + 8 * h:B + 1024 + 8 * h + 8])
                        ins.then_inc(obd_out, 1)
                project_add([oT], [s_wout], s_bout)

        def moe():
            layer_norm()
            route(lambda t, o: nc.tensor.matmul(o, xT[:, t * P:(t + 1) * P], e_router, start=True, stop=True),
                  True, 0.0, 1e-12)
            with scratch("ehid", [P, 4, NP]) as ehid:
                with ph.phase("hid_in", "hid_out") as (block, hid_in, hid_out):
                    @block.tensor
                    def _(pe):
                        for c in range(4):
                            if c >= 2:
                                pe.wait_ge(hid_out, c - 1)
                            columns(A if c % 2 == 0 else B, P, [(e_w1[:, c * P:(c + 1) * P], xT[:])]).then_inc(hid_in, 1)

                    @block.scalar
                    def _(act):
                        for c in range(4):
                            r = A if c % 2 == 0 else B
                            act.wait_ge(hid_in, c + 1)
                            nc.scalar.activation(ehid[:, c, :], psum[:, r:r + NP], ACT.Gelu, bias=e_b1[:, c:c + 1]).then_inc(hid_out, 1)

                def products(t, o):
                    for c in range(4):
                        nc.tensor.matmul(o[:, c * P:(c + 1) * P], ehid[:, c, t * P:(t + 1) * P], e_w2[:, c, :],
                                         start=(c == 0), stop=False)
                    return nc.tensor.matmul(o, ones[0:1, :], e_b2, start=False, stop=True)
                mix_experts(products, extra=x_tok)

        def recurrence():
            layer_norm()
            with ph.phase("sum_in", "stepped", "turned") as (block, sum_in, stepped, turned):
                @block.tensor
                def _(pe):
                    columns(A, C, [(r_ih, xT[:]), (r_hh, hidden[:])]).then_inc(sum_in, 1)
                    pe.wait_ge(stepped, 1)
                    for t in range(NT):
                        last = nc.tensor.transpose(psum[:, B + t * C:B + (t + 1) * C], hidden[0:C, t * P:(t + 1) * P],
                                                   ident[0:C, 0:C])
                    last.then_inc(turned, 1)

                @block.scalar
                def _(act):
                    act.wait_ge(sum_in, 1)
                    nc.scalar.activation(hidden[0:C, :], psum[0:C, A:A + NP], ACT.Tanh, bias=r_bias[:]).then_inc(stepped, 1)

                @block.vector
                def _(dve):
                    dve.wait_ge(turned, 1)
                    nc.vector.tensor_tensor(flat(h_tok), flat(h_tok), psum[:, B:B + NT * C], ALU.add)

        def gated():
            layer_norm()
            with scratch("ghid", [P, 2, NP]) as ghid:
                with ph.phase("hid_in") as (block, hid_in):
                    @block.tensor
                    def _(pe):
                        for c in range(2):
                            columns(A if c == 0 else B, P, [(g_w1[:, c * P:(c + 1) * P], xT[:])]).then_inc(hid_in, 1)

                    @block.scalar
                    def _(act):
                        for c in range(2):
                            r = A if c == 0 else B
                            act.wait_ge(hid_in, c + 1)
                            nc.scalar.activation(ghid[:, c, :], psum[:, r:r + NP], ACT.Gelu, bias=g_b1[:, c:c + 1])

                def logit(t, o):
                    for c in range(2):
                        nc.tensor.matmul(o, ghid[:, c, t * P:(t + 1) * P], g_wg[:, c, :], start=(c == 0), stop=False)
                    return nc.tensor.matmul(o, ones[0:1, :], g_bg, start=False, stop=True)
                route(logit, False, 0.0, 0.0)

                def products(t, o):
                    nc.tensor.matmul(o, ones[0:1, :], g_bd, start=True, stop=False)
                    for c in range(2):
                        m = nc.tensor.matmul(o, ghid[:, c, t * P:(t + 1) * P], g_wd[:, c, :], start=False, stop=(c == 1))
                    return m
                mix_experts(products)

        def store(b):
            with ph.phase("stored") as (block, stored):
                @block.sync
                def _(sp):
                    ob = out[bass.ds(b, 1)].rearrange("a n c -> (a n) c")
                    sp.dma_start(ob[0:(NT - 1) * P].rearrange("(t p) c -> p t c", p=P), h_tok[:, 0:NT - 1, :]).then_inc(stored, 16)
                    sp.dma_start(ob[(NT - 1) * P:N_TOK], h_tok[0:N_TOK - (NT - 1) * P, NT - 1, :]).then_inc(stored, 16)
                    sp.wait_ge(stored, 32)

        def before(b):
            tokens(b)
            phasor()
            rotary_moe()
            state_space()

        def after_heads(b, y_all):
            heads_out(y_all)
            slices()
            moe()
            recurrence()
            gated()
            store(b)

        def keep():
            with ph.phase("kept") as (block, kept):
                @block.vector
                def _(dve):
                    nc.vector.tensor_copy(flat(h_old), flat(h_new)).then_inc(kept, 1)

        before(0)
        with scratch("qpkT", [P, 4, NP]) as qpkT:
            key_queries(0, qpkT)
            slots(0, None, qpkT, None)
        keep()
        if n_batch > 1:
            with nc.Fori(1, n_batch) as b:
                before(b)
                with scratch("y_all", [P, NT, 512]) as y_all:
                    with scratch("qpkT", [P, 4, NP]) as qpkT:
                        key_queries(b, qpkT)
                        slots(b, b - 1, qpkT, y_all)
                    h_tok = h_old
                    after_heads(b - 1, y_all)
                    h_tok = h_new
                keep()
                ph.close_loop()
        with scratch("y_all", [P, NT, 512]) as y_all:
            slots(None, n_batch - 1, None, y_all)
            h_tok = h_old
            after_heads(n_batch - 1, y_all)


def layouts(i):
    cat, T = np.concatenate, np.transpose
    col = lambda a: np.reshape(a, (-1, 1))
    row = lambda a: np.reshape(a, (1, -1))
    w = {k: np.asarray(v) for k, v in i.items()}
    g = lambda k: w[k]
    d = {
        "x": g("x"), "cls": col(g("cls_tok")),
        "t_w": T(g("L0_tok_W").reshape(C, 18, C), (1, 2, 0)),
        "a_w1p": cat([g("L0_attn_kp_w1").T, g("L0_attn_qp_w1").T], 1),
        "a_w1h": cat([g("L0_attn_kh_w1").T, g("L0_attn_qh_w1").T], 1),
        "a_b1p": col(cat([g("L0_attn_kp_b1"), g("L0_attn_qp_b1")])),
        "a_b1h": col(cat([g("L0_attn_kh_b1"), g("L0_attn_qh_b1")])),
        "a_b2": row(cat([g("L0_attn_kp_b2"), g("L0_attn_qp_b2"), g("L0_attn_kh_b2"), g("L0_attn_qh_b2")])),
        "a_w2p": np.stack([g("L0_attn_kp_w2").T, g("L0_attn_qp_w2").T]),
        "a_w2h": np.stack([g("L0_attn_kh_w2").T, g("L0_attn_qh_w2").T]),
        "a_vw": g("L0_attn_v_w").T, "a_vb": row(g("L0_attn_v_b")),
        "a_ow": g("L0_attn_out_w").T, "a_ob": row(g("L0_attn_out_b")),
        "a_g": g("L0_attn_ln_g"), "a_b": g("L0_attn_ln_b"),
        "f_ln1": g("L0_ffn_ln1_w"), "f_ln2": g("L0_ffn_ln2_w"),
        "f_qkv": cat([g("L0_ffn_wq").T, g("L0_ffn_wk").T, g("L0_ffn_wv").T], 1),
        "f_wo": g("L0_ffn_wo").T, "f_router": g("L0_ffn_router_w").T,
        "f_w1": T(g("L0_ffn_w1"), (2, 0, 1)).reshape(C, -1),
        "f_w3": T(g("L0_ffn_w3"), (2, 0, 1)).reshape(C, -1),
        "f_w2": T(T(g("L0_ffn_w2"), (0, 2, 1)).reshape(2 * NE, HB, C), (1, 0, 2)),
        "m_in": g("L1_attn_W_in"), "m_cw": g("L1_attn_conv_w").reshape(P, TAPS), "m_cb": col(g("L1_attn_conv_b")),
        "m_xp": g("L1_attn_W_xproj"), "m_wdt": col(g("L1_attn_w_dt")), "m_bdt": col(g("L1_attn_b_dt")),
        "m_A": g("L1_attn_A"), "m_D": col(g("L1_attn_D")), "m_out": g("L1_attn_W_out"),
        "k_wqpk": g("L1_ffn_Wq_pk"), "k_wq": g("L1_ffn_Wq"),
        "k_keys": T(g("L1_ffn_pk_keys"), (0, 2, 3, 1)).reshape(4, 4, 32, PKK),
        "k_table": cat([g("L1_ffn_keys_table"), g("L1_ffn_values_table")], 1),
        "k_wo": T(g("L1_ffn_Wo").reshape(4, P, C), (1, 0, 2)),
        "s_win": g("L2_attn_W_in"), "s_bin_row": row(g("L2_attn_b_in")), "s_bin_col": col(g("L2_attn_b_in")),
        "s_wslice": g("L2_attn_W_slice"), "s_bslice": row(np.tile(g("L2_attn_b_slice"), 8)),
        "s_temp": g("L2_attn_temperature").reshape(8),
        "s_qkvw": np.tile(cat([g("L2_attn_W_q"), g("L2_attn_W_k"), g("L2_attn_W_v")], 1), (8, 1)),
        "s_bq": col(g("L2_attn_b_q")), "s_bk": col(g("L2_attn_b_k")), "s_bv": row(g("L2_attn_b_v")),
        "s_wout": g("L2_attn_W_out"), "s_bout": row(g("L2_attn_b_out")),
        "e_router": g("L2_ffn_router_w").T, "e_w1": T(g("L2_ffn_w1"), (1, 0, 2)).reshape(C, 512),
        "e_b1": T(g("L2_ffn_b1").reshape(4, P)), "e_w2": g("L2_ffn_w2"), "e_b2": row(g("L2_ffn_b2")),
        "r_ih": g("L3_attn_W_ih").T, "r_hh": g("L3_attn_W_hh").T,
        "r_b": np.stack([g("L3_attn_b_ih"), g("L3_attn_b_hh")], 1),
        "g_w1": g("L3_ffn_W1"), "g_b1": T(g("L3_ffn_b1").reshape(2, P)),
        "g_wg": T(g("L3_ffn_Wg").reshape(2, P, NE), (1, 0, 2)), "g_bg": row(g("L3_ffn_bg")),
        "g_wd": T(T(g("L3_ffn_Wd"), (1, 0, 2)).reshape(2, P, 512), (1, 0, 2)), "g_bd": row(g("L3_ffn_bd")),
    }
    d = {k: np.ascontiguousarray(v) for k, v in d.items()}
    for k, v in constants().items():
        d[k] = np.ascontiguousarray(v, dtype=np.float32)
    return d


UPTO, NBATCH = 99, N_BATCH


def kernel(**inputs):
    import concourse.bacc as bacc
    from concourse.bass_utils import run_bass_kernel_spmd

    nc = bacc.Bacc("TRN2", target_bir_lowering=False, num_devices=1)
    arrays, io = {}, {}
    for name, a in layouts(inputs).items():
        arrays["in_" + name] = a
        io[name] = nc.dram_tensor("in_" + name, a.shape, mybir.dt.from_np(a.dtype), kind="ExternalInput").ap()
    out = nc.dram_tensor("out_0", (N_BATCH, N_TOK, C), F32, kind="ExternalOutput").ap()
    build(nc, io, out, NBATCH, UPTO)
    r = run_bass_kernel_spmd(nc, [arrays], core_ids=[0])
    return r.results[0]["out_0"]
```

```python
import math
from contextlib import ExitStack, contextmanager

import numpy as np
import concourse.bass as bass
from concourse import mybir

F32 = mybir.dt.float32
U32 = mybir.dt.uint32
ALU = mybir.AluOpType
ACT = mybir.ActivationFunctionType
AX = mybir.AxisListType

P = 128
C = 64
N_BATCH = 8
N_PATCH, PATCH, HOP = 16, 16, 8
N_VAR, N_TIME = 64, 128
N_TOK = 1 + N_VAR * N_PATCH
NT = -(-N_TOK // P)
NP = NT * P
NPER, NHYP = 48, 16
NE, HID0 = 8, 170
HB = HID0 // 2
NSTATE, TAPS = 16, 4
PKH, PKK, TOPK = 8, 64, 16
NEG = -1e30
LOWEST = -3.0e38
LN_EPS, RMS_EPS = 1e-5, 1e-6

PAIRS = []
_off = 0
for _i0, _i1, _j in [(0, 1, 16), (1, 2, 8), (2, 3, 5), (3, 4, 4), (4, 5, 3), (5, 8, 2), (8, 16, 1)]:
    PAIRS.append((_off, _i0, _i1, _j))
    _off += (_i1 - _i0) * _j
NPAIR = _off


def constants():
    t = np.arange(PATCH)
    f = np.arange(PATCH // 2 + 1)
    ang = 2 * np.pi * np.outer(f, t) / PATCH
    dft = np.concatenate([np.cos(ang), -np.sin(ang)], 0) / math.sqrt(PATCH)
    tok = np.arange(NP).reshape(NT, P).T
    inv = 1.0 / 10000.0 ** (np.arange(0, 16, 2, dtype=np.float32) / 16)
    fr = (tok[..., None].astype(np.float32) * inv).astype(np.float32)
    sin, cos = np.sin(fr), np.cos(fr)
    q, k = np.arange(P)[:, None], np.arange(P)[None, :]
    row = np.arange(P)[:, None]
    head_of_row = np.arange(4)[None, :, None] * 2 + row[:, :, None] // 64
    return {
        "c_dft": dft,
        "c_pos": 1.0 / np.sqrt((tok + 1) * 64.0),
        "c_cos": np.concatenate([cos, cos], -1),
        "c_sin": np.concatenate([-sin, sin], -1),
        "c_ident": np.eye(P),
        "c_after": np.where(k > q, NEG, 0.0),
        "c_afterT": np.where(q > k, NEG, 0.0),
        "c_upto": np.where(q <= k, 1.0, 0.0),
        "c_rank": np.broadcast_to(8.0 - np.arange(NE), (P, NE)),
        "c_headoff": np.broadcast_to(np.arange(PKH) * float(PKK * PKK), (P, PKH)),
        "c_iota": np.broadcast_to(np.arange(NPAIR), (P, NPAIR)),
        "c_ownhead": (np.arange(C)[None, None, :] // 8 == head_of_row),
        "c_valid": (tok < N_TOK),
        "c_headrow": (np.arange(P)[:, None] // TOPK == np.arange(PKH)[None, :]),
    }


def chunks(base, lo=0, hi=NP):
    out = []
    while lo < hi:
        end = min(hi, (base + lo) // 512 * 512 + 512 - base)
        out.append((lo, end))
        lo = end
    return out


class Phases:

    def __init__(self, nc):
        self.nc = nc
        self.stale = []

    def clear(self):
        for s in self.stale:
            self.nc.gpsimd.sem_clear(s)
        self.stale = []

    def close_loop(self):
        self.clear()
        self.nc.all_engine_barrier()

    @contextmanager
    def phase(self, *names):
        self.clear()
        with ExitStack() as ctx:
            sems = [ctx.enter_context(self.nc.semaphore(n)) for n in names]
            with self.nc.Block() as block:
                yield (block, *sems)
        self.stale = sems


class Steps:

    def __init__(self, eng, sem):
        self.eng, self.sem, self.n = eng, sem, 0

    def __call__(self, ins):
        self.n += 1
        ins.then_inc(self.sem, 1)
        self.eng.wait_ge(self.sem, self.n)


def build(nc, io, out, n_batch=N_BATCH):
    ctx = ExitStack()
    with ctx:
        ph = Phases(nc)

        def sb(name, shape, dt=F32):
            return ctx.enter_context(nc.sbuf_tensor(name, shape, dt))

        taken = {}

        def scratch(name, shape, dt=F32):
            taken[name] = taken.get(name, 0) + 1
            return nc.sbuf_tensor(f"{name}_{taken[name]}", shape, dt)

        psum = ctx.enter_context(nc.psum_tensor("psum", [P, 8 * 512], F32))
        A, B, D, F = 0, 3 * 512, 6 * 512, 7 * 512
        loads, zeroed = [], []

        def const(key, shape, src=None):
            t = sb("sb_" + key, shape)[:]
            loads.append((t, src if src is not None else io[key]))
            return t

        def padded(key, shape, bias=None):
            t = sb("sb_" + key, [P, *shape[1:]])
            zeroed.append(t)
            loads.append((t[0:shape[0]], io[key]))
            if bias:
                loads.append((t[C:C + 1], io[bias]))
            return t[:]

        ident = const("c_ident", [P, P])
        after = const("c_after", [P, P])
        afterT = const("c_afterT", [P, P])
        upto_q = const("c_upto", [P, P])
        pos_norm = const("c_pos", [P, NT])
        cos = const("c_cos", [P, NT, 16])
        sin = const("c_sin", [P, NT, 16])
        rank = const("c_rank", [P, NE])
        headoff = const("c_headoff", [P, PKH])
        iota = const("c_iota", [P, NPAIR])
        ownhead = const("c_ownhead", [P, 4, C])
        valid = const("c_valid", [P, NT])
        headrow = const("c_headrow", [P, PKH])
        a_w1p = padded("a_w1p", [C, P])
        a_w1h = padded("a_w1h", [C, P])
        a_b1p = const("a_b1p", [P, 1])
        a_b1h = const("a_b1h", [P, 1])
        a_b2 = const("a_b2", [1, 160])
        a_vw = padded("a_vw", [C, C], bias="a_vb")
        a_ow = padded("a_ow", [C, C], bias="a_ob")
        a_g = const("a_g", [P, C], src=io["a_g"].partition_broadcast(P))
        a_b = const("a_b", [P, C], src=io["a_b"].partition_broadcast(P))
        f_ln1 = const("f_ln1", [P, C], src=io["f_ln1"].partition_broadcast(P))
        f_ln2 = const("f_ln2", [P, C], src=io["f_ln2"].partition_broadcast(P))
        f_qkv = padded("f_qkv", [C, P])
        f_wo = padded("f_wo", [C, C])
        f_router = padded("f_router", [C, NE])
        m_in = padded("m_in", [C, 2 * P])
        m_cw = const("m_cw", [P, TAPS])
        m_cb = const("m_cb", [P, 1])
        m_xp = const("m_xp", [P, 1 + 2 * NSTATE])
        m_wdt = const("m_wdt", [P, 1])
        m_bdt = const("m_bdt", [P, 1])
        m_A = const("m_A", [P, NSTATE])
        m_D = const("m_D", [P, 1])
        m_out = const("m_out", [P, C])
        k_wqpk = padded("k_wqpk", [C, 512])
        k_wq = padded("k_wq", [C, 512])
        k_wo = const("k_wo", [P, 4, C])
        s_win = padded("s_win", [C, C], bias="s_bin")
        s_temp = const("s_temp", [P, 8], src=io["s_temp"].partition_broadcast(P))
        s_qkvw = const("s_qkvw", [C, 24])
        s_bq = const("s_bq", [8, 1])
        s_bk = const("s_bk", [8, 1])
        s_bv = const("s_bv", [1, 8])
        s_wout = padded("s_wout", [C, C], bias="s_bout")
        e_router = padded("e_router", [C, NE])
        e_w1 = padded("e_w1", [C, 512])
        e_b1 = const("e_b1", [P, 4])
        e_b2 = const("e_b2", [P, 512], src=io["e_b2"].partition_broadcast(P))
        r_ih = padded("r_ih", [C, C])
        r_hh = padded("r_hh", [C, C])
        r_b = const("r_b", [C, 2])
        g_w1 = padded("g_w1", [C, 256])
        g_b1 = const("g_b1", [P, 2])
        g_wg = const("g_wg", [P, 2, NE])
        g_bg = const("g_bg", [1, NE])
        g_wd = const("g_wd", [P, 2, 512])
        g_bd = const("g_bd", [P, 512], src=io["g_bd"].partition_broadcast(P))

        a_w2p = sb("a_w2p_sb", [P, 96])
        a_w2h = sb("a_w2h_sb", [P, 64])
        k_keys = sb("k_keys_sb", [P, 4, 256])
        s_slice = sb("s_slice_sb", [P, 512])
        e_w2 = sb("e_w2_sb", [P, 4, P])
        blocks = []
        for j in range(2):
            blocks.append((a_w2p[j * 64:(j + 1) * 64, j * 48:(j + 1) * 48], io["a_w2p"][j]))
            blocks.append((a_w2h[j * 64:(j + 1) * 64, j * 32:(j + 1) * 32], io["a_w2h"][j]))
        for c in range(4):
            for j in range(4):
                blocks.append((k_keys[32 * j:32 * j + 32, c, 64 * j:64 * j + 64], io["k_keys"][c, j]))
            for j in range(2):
                blocks.append((e_w2[64 * j:64 * j + 64, c, 64 * j:64 * j + 64], io["e_w2"][2 * c + j]))
        for h in range(8):
            blocks.append((s_slice[8 * h:8 * h + 8, 64 * h:64 * h + 64], io["s_wslice"]))
        blocks.append((s_slice[C:C + 1, :], io["s_bslice"]))

        w_tok = sb("w_tok", [P, 8, C])
        ones = sb("ones", [P, P])
        eps = sb("eps", [P, 3])
        s_rtemp = sb("s_rtemp", [P, 8])
        r_bias = sb("r_bias", [C, 1])

        h_new = sb("h_new", [P, NT, C])
        h_mid = sb("h_mid", [P, NT, C])
        h_old = sb("h_old", [P, NT, C])
        h_tok = h_new
        x_tok = sb("x_tok", [P, NT, C])
        xT = sb("xT", [P, NP])
        y_tok = sb("y_tok", [P, NT, C])
        yT = sb("yT", [P, NP])
        hidden = sb("hidden", [P, NP])
        stat = sb("stat", [P, 8, NT])
        tmp = sb("tmp", [P, NT, C])
        rt_l, rt_p, rt_k, rt_m, rt_o, rt_w = [sb(f"rt{i}", [P, NT, NE]) for i in range(6)]
        rt_s = sb("rt_s", [P, 4, NT])

        dram_w = nc.dram_tensor("dram_w", [PATCH, C, C], F32, kind="Internal").ap()

        def bc(ap, shape, axis):
            return ap.unsqueeze(axis).broadcast_to(shape)

        def flat(t):
            return t[:].rearrange("p a b -> p (a b)")

        def columns(base, rows, pairs):
            for a, b in chunks(base):
                for n, (w, d) in enumerate(pairs):
                    last = nc.tensor.matmul(psum[0:rows, base + a:base + b], w, d[:, a:b],
                                            start=(n == 0), stop=(n == len(pairs) - 1))
            return last

        def turn_tiles(base, src, rows):
            for t in range(NT):
                last = nc.tensor.transpose(psum[0:rows, base + t * P:base + (t + 1) * P],
                                           src[:, t, :], ident)
            return last

        with ph.phase("cleared", "loaded", "fold_in", "folded", "fold_out", "fold_back", "sp_blocks",
                      "dve_step") as (block, cleared, loaded, fold_in, folded, fold_out, fold_back,
                                      blocks_in, dve_step):
            with scratch("w_freq", [18, C, C]) as w_freq, \
                    scratch("dft", [18, PATCH]) as dft, \
                    scratch("w_fold", [PATCH, C * C]) as w_fold:

                @block.sync
                def _(sp):
                    sp.dma_start(w_freq[:], io["t_w"]).then_inc(fold_in, 16)
                    sp.dma_start(dft[:], io["c_dft"]).then_inc(fold_in, 16)
                    sp.wait_ge(cleared, 1)
                    for dst, src in loads:
                        sp.dma_start(dst, src).then_inc(loaded, 16)
                    for dst, src in blocks:
                        sp.dma_start(dst, src).then_inc(blocks_in, 16)
                    sp.wait_ge(fold_out, 2)
                    sp.dma_start(dram_w, w_fold[:].rearrange("t (c o) -> t c o", c=C)).then_inc(fold_back, 16)
                    sp.wait_ge(fold_back, 16)
                    for r in range(2):
                        sp.dma_start(w_tok[r * C:(r + 1) * C],
                                     dram_w.rearrange("(u r) c o -> r c u o", r=2)[r]).then_inc(fold_back, 16)
                    sp.wait_ge(fold_back, 48)
                    sp.wait_ge(loaded, 16 * len(loads))
                    sp.wait_ge(blocks_in, 16 * len(blocks))

                @block.tensor
                def _(pe):
                    pe.wait_ge(fold_in, 32)
                    wf = w_freq[:].rearrange("f c o -> f (c o)")
                    for n in range(8):
                        nc.tensor.matmul(psum[0:PATCH, n * 512:(n + 1) * 512], dft[:],
                                         wf[:, n * 512:(n + 1) * 512], start=True, stop=True).then_inc(folded, 1)

                @block.vector
                def _(dve):
                    for t in (a_w2p, a_w2h, k_keys, s_slice, xT, yT, hidden, *zeroed):
                        nc.vector.memset(t[:], 0.0)
                    nc.vector.memset(e_w2[:], 0.0).then_inc(cleared, 1)
                    dve.wait_ge(cleared, 1)
                    for t in (xT, yT):
                        nc.vector.memset(t[C:C + 1, :], 1.0)
                    nc.vector.memset(ones[:], 1.0)
                    nc.vector.memset(eps[:, 0:1], LN_EPS)
                    nc.vector.memset(eps[:, 1:2], RMS_EPS)
                    nc.vector.memset(eps[:, 2:3], math.pi / 2)
                    dve.wait_ge(folded, 8)
                    nc.vector.tensor_copy(w_fold[:], psum[0:PATCH, :]).then_inc(fold_out, 2)
                    dve.wait_ge(loaded, 16 * len(loads))
                    nc.vector.reciprocal(s_rtemp[:], s_temp)
                    nc.vector.tensor_tensor(r_bias[:], r_b[:, 0:1], r_b[:, 1:2], ALU.add)

        def layer_norm(rms_weight=None, src=None, dst=None, want_T=True):
            src = src or h_tok
            dst = dst or x_tok
            rms = rms_weight is not None
            with ph.phase("variance", "deviation", "normed", "turned", "dve_step") as (
                    block, variance, deviation, normed, turned, dve_step):
                @block.vector
                def _(dve):
                    step = Steps(dve, dve_step)
                    cen = src
                    if not rms:
                        step(nc.vector.tensor_reduce(stat[:, 0], src[:], AX.X, ALU.add))
                        step(nc.vector.tensor_scalar(stat[:, 1], stat[:, 0], 1.0 / C, None, ALU.mult))
                        step(nc.vector.tensor_tensor(dst[:], src[:], bc(stat[:, 1], [P, NT, C], 2), ALU.subtract))
                        cen = dst
                    step(nc.vector.tensor_tensor(tmp[:], cen[:], cen[:], ALU.mult))
                    nc.vector.tensor_reduce(stat[:, 2], tmp[:], AX.X, ALU.add).then_inc(variance, 1)
                    dve.wait_ge(deviation, 1)
                    step(nc.vector.reciprocal(stat[:, 4], stat[:, 3]))
                    ins = nc.vector.tensor_tensor(dst[:], cen[:], bc(stat[:, 4], [P, NT, C], 2), ALU.mult)
                    if rms:
                        step(ins)
                        ins = nc.vector.tensor_tensor(dst[:], dst[:], bc(rms_weight, [P, NT, C], 1), ALU.mult)
                    ins.then_inc(normed, 1)

                @block.scalar
                def _(act):
                    act.wait_ge(variance, 1)
                    nc.scalar.activation(stat[:, 3], stat[:, 2], ACT.Sqrt, scale=1.0 / C,
                                         bias=eps[:, 1:2] if rms else eps[:, 0:1]).then_inc(deviation, 1)
                    if want_T:
                        act.wait_ge(turned, 1)
                        nc.scalar.copy(xT[0:C, :], psum[0:C, A:A + NP])

                @block.tensor
                def _(pe):
                    pe.wait_ge(normed, 1)
                    if want_T:
                        turn_tiles(A, dst, C).then_inc(turned, 1)

        def project_add(srcT, weights, extra=None):
            with ph.phase("projected", "dve_step") as (block, projected, dve_step):
                @block.tensor
                def _(pe):
                    for t in range(NT):
                        o = psum[:, A + t * C:A + (t + 1) * C]
                        for n, (s, w) in enumerate(zip(srcT, weights)):
                            last = nc.tensor.matmul(o, s[:, t * P:(t + 1) * P], w, start=(n == 0),
                                                    stop=(n == len(srcT) - 1))
                    last.then_inc(projected, 1)

                @block.vector
                def _(dve):
                    step = Steps(dve, dve_step)
                    if extra is not None:
                        step(nc.vector.tensor_tensor(flat(h_tok), flat(h_tok), flat(extra), ALU.add))
                    dve.wait_ge(projected, 1)
                    nc.vector.tensor_tensor(flat(h_tok), flat(h_tok), psum[:, A:A + NT * C], ALU.add)

        def softmax_experts(step, logits):
            step(nc.vector.tensor_reduce(rt_s[:, 0], logits, AX.X, ALU.max))
            step(nc.vector.tensor_tensor(rt_l[:], logits, bc(rt_s[:, 0], [P, NT, NE], 2), ALU.subtract))

        def pick_best(step, probs, picked, top):
            step(nc.vector.tensor_reduce(top, probs, AX.X, ALU.max))
            step(nc.vector.tensor_tensor(rt_k[:], probs, bc(top, [P, NT, NE], 2), ALU.is_ge))
            step(nc.vector.tensor_tensor(rt_k[:], rt_k[:], bc(rank, [P, NT, NE], 1), ALU.mult))
            step(nc.vector.tensor_reduce(rt_s[:, 3], rt_k[:], AX.X, ALU.max))
            step(nc.vector.tensor_tensor(picked, rt_k[:], bc(rt_s[:, 3], [P, NT, NE], 2), ALU.is_equal))

        def route(logit_products, top2, floor_add, floor_max):
            with ph.phase("logits", "shifted", "exps", "dve_step") as (block, logits, shifted, exps, dve_step):
                @block.tensor
                def _(pe):
                    for t in range(NT):
                        last = logit_products(t, psum[:, D + t * NE:D + (t + 1) * NE])
                    last.then_inc(logits, 1)

                @block.scalar
                def _(act):
                    act.wait_ge(shifted, 1)
                    nc.scalar.activation(rt_p[:], rt_l[:], ACT.Exp).then_inc(exps, 1)

                @block.vector
                def _(dve):
                    step = Steps(dve, dve_step)
                    lg = psum[:, D:D + NT * NE].rearrange("p (t e) -> p t e", e=NE)
                    dve.wait_ge(logits, 1)
                    softmax_experts(step, lg)
                    nc.vector.tensor_copy(rt_s[:, 1], rt_s[:, 0]).then_inc(shifted, 1)
                    dve.wait_ge(exps, 1)
                    dve.wait_ge(shifted, 1)
                    step(nc.vector.tensor_reduce(rt_s[:, 1], rt_p[:], AX.X, ALU.add))
                    step(nc.vector.reciprocal(rt_s[:, 2], rt_s[:, 1]))
                    step(nc.vector.tensor_tensor(rt_p[:], rt_p[:], bc(rt_s[:, 2], [P, NT, NE], 2), ALU.mult))
                    pick_best(step, rt_p[:], rt_m[:], rt_s[:, 0])
                    if not top2:
                        step(nc.vector.tensor_tensor(rt_w[:], rt_m[:], rt_p[:], ALU.mult))
                        return
                    step(nc.vector.scalar_tensor_tensor(rt_l[:].rearrange("p a b -> p (a b)"), flat(rt_m), -4.0,
                                                        flat(rt_p), ALU.mult, ALU.add))
                    pick_best(step, rt_l[:], rt_o[:], rt_s[:, 1])
                    step(nc.vector.tensor_tensor(rt_m[:], rt_m[:], rt_o[:], ALU.add))
                    step(nc.vector.tensor_tensor(rt_w[:], rt_m[:], rt_p[:], ALU.mult))
                    step(nc.vector.tensor_reduce(rt_s[:, 1], rt_w[:], AX.X, ALU.add))
                    step(nc.vector.tensor_scalar(rt_s[:, 1], rt_s[:, 1], floor_add, floor_max, ALU.add, ALU.max))
                    step(nc.vector.reciprocal(rt_s[:, 2], rt_s[:, 1]))
                    step(nc.vector.tensor_tensor(rt_w[:], rt_w[:], bc(rt_s[:, 2], [P, NT, NE], 2), ALU.mult))

        def mix_experts(tile_products, bias, extra=None):
            with scratch("mixed", [P, 2, NE, C]) as mixed, \
                    ph.phase("tile_out", "tile_used", "weighed", "dve_step") as (
                        block, tile_out, tile_used, weighed, dve_step):
                @block.tensor
                def _(pe):
                    for t in range(NT):
                        if t >= 4:
                            pe.wait_ge(tile_used, t - 3)
                        tile_products(t, psum[:, (t % 4) * 512:(t % 4 + 1) * 512]).then_inc(tile_out, 1)

                @block.vector
                def _(dve):
                    step = Steps(dve, dve_step)
                    for t in range(NT):
                        dve.wait_ge(tile_out, t + 1)
                        if t >= 2:
                            dve.wait_ge(dve_step, t - 1)
                        o = psum[:, (t % 4) * 512:(t % 4 + 1) * 512].rearrange("p (e c) -> p e c", c=C)
                        nc.vector.tensor_tensor(mixed[:, t % 2], o, bias.rearrange("p (e c) -> p e c", c=C),
                                                ALU.add).then_inc(tile_used, 1)
                        dve.wait_ge(tile_used, t + 1)
                        nc.vector.tensor_tensor(mixed[:, t % 2], mixed[:, t % 2], bc(rt_w[:, t], [P, NE, C], 2),
                                                ALU.mult).then_inc(weighed, 1)
                        dve.wait_ge(weighed, t + 1)
                        nc.vector.tensor_reduce(tmp[:, t], mixed[:, t % 2].rearrange("p e c -> p c e"),
                                                AX.X, ALU.add).then_inc(dve_step, 1)
                    step.n = NT
                    dve.wait_ge(dve_step, NT)
                    step(nc.vector.tensor_tensor(flat(h_tok), flat(h_tok), flat(tmp), ALU.add))
                    if extra is not None:
                        step(nc.vector.tensor_tensor(flat(h_tok), flat(h_tok), flat(extra), ALU.add))

        HEAD_SEMS = ("q_turned", "k_turned", "row_cleared", "qT_out", "kT_out", "scores", "maxed", "max_turned",
                     "max_row", "scoresT", "exped", "weighed", "summed", "normed")
        w_of = [(t + 1) * P for t in range(NT)]

        def out_column(t, hd):
            per_bank = 512 // (hd + 1)
            return D + t * (hd + 1) if t < per_bank else F + (t - per_bank) * (hd + 1)

        class Head:

            def __init__(self, sems, buf, hd, k_row, scale):
                (self.q_turned, self.k_turned, self.row_cleared, self.qT_out, self.kT_out, self.scores, self.maxed,
                 self.max_turned, self.max_row, self.scoresT, self.exped, self.weighed, self.summed,
                 self.normed) = sems
                self.q_h, self.k_h, self.v_h, self.qT, self.kT, self.neg_max, self.probsT, self.r_sum = buf
                self.hd, self.k_row, self.scale = hd, k_row, scale
                self.per_bank = 512 // (hd + 1)

            def clear_row(self):
                nc.vector.memset(self.qT[self.k_row:self.k_row + 1, :], 0.0).then_inc(self.row_cleared, 1)

            def max_tiles(self, dve, tiles):
                for t in tiles:
                    r = A if t % 2 == 0 else B
                    dve.wait_ge(self.scores, t + 1)
                    nc.vector.tensor_reduce(self.neg_max[:, t:t + 1], psum[:, r:r + w_of[t]], AX.X, ALU.max,
                                            negate=True).then_inc(self.maxed, 1)

            def row_of_max(self, dve):
                dve.wait_ge(self.max_turned, 1)
                nc.vector.tensor_copy(self.qT[self.k_row:self.k_row + 1, :], psum[0:1, A:A + NP]).then_inc(self.max_row, 1)

            def normalize(self, dve, out_of):
                dve.wait_ge(self.weighed, NT)
                hd = self.hd
                parts = [(0, min(self.per_bank, NT))] + ([(self.per_bank, NT)] if NT > self.per_bank else [])
                views = []
                for a, b in parts:
                    c = out_column(a, hd)
                    views.append(psum[:, c:c + (b - a) * (hd + 1)].rearrange("p (t d) -> p t d", d=hd + 1))
                    nc.vector.reciprocal(self.r_sum[:, a:b], views[-1][:, :, hd]).then_inc(self.summed, 1)
                dve.wait_ge(self.summed, len(parts))
                for (a, b), o in zip(parts, views):
                    ins = nc.vector.tensor_tensor(out_of(a, b), o[:, :, 0:hd], bc(self.r_sum[:, a:b], [P, b - a, hd], 2),
                                                  ALU.mult)
                ins.then_inc(self.normed, 1)

            def run_scalar(self, act):
                hd = self.hd
                act.wait_ge(self.q_turned, 1)
                nc.scalar.copy(self.qT[0:hd, :], psum[0:hd, A:A + NP]).then_inc(self.qT_out, 1)
                act.wait_ge(self.k_turned, 1)
                nc.scalar.copy(self.kT[0:hd, :], psum[0:hd, B:B + NP]).then_inc(self.kT_out, 1)
                for t in range(NT):
                    r = B if t % 2 == 0 else A
                    act.wait_ge(self.scoresT, t + 1)
                    if t >= 2:
                        act.wait_ge(self.weighed, t - 1)
                    nc.scalar.activation(self.probsT[:, t % 2, t * P:NP], psum[:, r + t * P:r + NP], ACT.Exp,
                                         scale=self.scale).then_inc(self.exped, 1)

            def run_tensor(self, pe):
                hd, qT, kT = self.hd, self.qT, self.kT
                turn_tiles(A, self.q_h, hd).then_inc(self.q_turned, 1)
                turn_tiles(B, self.k_h, hd).then_inc(self.k_turned, 1)
                pe.wait_ge(self.qT_out, 1)
                pe.wait_ge(self.kT_out, 1)
                pe.wait_ge(self.row_cleared, 1)
                for t in range(NT):
                    r = A if t % 2 == 0 else B
                    if t >= 2:
                        pe.wait_ge(self.maxed, t - 1)
                    for a, b in chunks(r, 0, w_of[t]):
                        own = min(b, t * P)
                        if a < own:
                            nc.tensor.matmul(psum[:, r + a:r + own], qT[:, t * P:(t + 1) * P], kT[:, a:own],
                                             start=True, stop=True)
                        if own < b:
                            nc.tensor.matmul(psum[:, r + own:r + b], qT[:, t * P:(t + 1) * P], kT[:, own:b],
                                             start=True, stop=False)
                            last = nc.tensor.matmul(psum[:, r + own:r + b], ident, after, start=False, stop=True)
                    last.then_inc(self.scores, 1)
                pe.wait_ge(self.maxed, NT)
                for t in range(NT):
                    last = nc.tensor.transpose(psum[0:1, A + t * P:A + (t + 1) * P], self.neg_max[:, t:t + 1], ident)
                last.then_inc(self.max_turned, 1)
                pe.wait_ge(self.max_row, 1)

                def weigh(j):
                    pe.wait_ge(self.exped, j + 1)
                    for t in range(j, NT):
                        c = out_column(t, hd)
                        m = nc.tensor.matmul(psum[:, c:c + hd + 1], self.probsT[:, j % 2, t * P:(t + 1) * P],
                                             self.v_h[:, j, :], start=(j == 0 and c % 512 == 0),
                                             stop=(j == NT - 1 or (j == self.per_bank - 1 and t == j)))
                    m.then_inc(self.weighed, 1)

                for t in range(NT):
                    r = B if t % 2 == 0 else A
                    if t >= 2:
                        pe.wait_ge(self.exped, t - 1)
                    for a, b in chunks(r, t * P, (t + 1) * P):
                        nc.tensor.matmul(psum[:, r + a:r + b], kT[:, t * P:(t + 1) * P], qT[:, a:b], start=True, stop=False)
                        last = nc.tensor.matmul(psum[:, r + a:r + b], ident, afterT[:, a - t * P:b - t * P],
                                                start=False, stop=True)
                    for a, b in chunks(r, (t + 1) * P, NP):
                        last = nc.tensor.matmul(psum[:, r + a:r + b], kT[:, t * P:(t + 1) * P], qT[:, a:b],
                                                start=True, stop=True)
                    last.then_inc(self.scoresT, 1)
                    if t >= 1:
                        weigh(t - 1)
                weigh(NT - 1)

        def head_buffers(c2, hd, other=None):
            def b(name, shape):
                return c2.enter_context(scratch(name, shape))
            return [b("q_h", [P, NT, hd]), b("k_h", [P, NT, hd]), b("v_h", [P, NT, hd + 1]), b("qT", [P, NP]),
                    b("kT", [P, NP]), b("neg_max", [P, NT]),
                    other[6] if other else b("probsT", [P, 2, NP]), b("r_sum", [P, NT])]

        def init_heads(dve, step, heads):
            for (q_h, k_h, v_h, qT, kT, *_), hd, k_row in heads:
                nc.vector.memset(q_h[:, NT - 1], 0.0)
                nc.vector.memset(k_h[:, NT - 1], 0.0)
                step(nc.vector.memset(v_h[:, NT - 1], 0.0))
                nc.vector.memset(v_h[:, :, hd:hd + 1], 1.0)
                nc.vector.memset(qT[:], 0.0)
                step(nc.vector.memset(kT[:], 0.0))
                step(nc.vector.memset(kT[k_row:k_row + 1, :], 1.0))

        def tokens(b, heads):
            U = N_TIME // 2
            with scratch("series", [P, U + 4, N_VAR]) as series, \
                    scratch("edge", [P, N_VAR]) as edge, \
                    scratch("hT", [C, NP]) as hT, \
                    ph.phase("series_in", "padded", "embedded", "hT_out", "turned", "dve_step") as (
                        block, series_in, padded, embedded, hT_out, turned, dve_step):
                @block.sync
                def _(sp):
                    xb = io["x"][bass.ds(b, 1)].rearrange("a c (u r) v -> (a r) c u v", r=2)
                    for r in range(2):
                        sp.dma_start(series[r * C:(r + 1) * C, 0:U, :], xb[r]).then_inc(series_in, 16)
                        sp.dma_start(edge[r * C:(r + 1) * C, :],
                                     io["x"][bass.ds(b, 1), :, N_TIME - 1, :].rearrange("a c v -> (a c) v")
                                     ).then_inc(series_in, 16)
                    sp.dma_start(hT[:, 0:1], io["cls"]).then_inc(series_in, 16)

                @block.vector
                def _(dve):
                    nc.vector.memset(hT[:, N_TOK:NP], 0.0)
                    init_heads(dve, Steps(dve, dve_step), heads)
                    dve.wait_ge(series_in, 80)
                    nc.vector.tensor_copy(series[:, U:U + 4, :], bc(edge[:], [P, 4, N_VAR], 1)).then_inc(padded, 1)
                    dve.wait_ge(embedded, 1)
                    nc.vector.tensor_copy(hT[:, 1:N_TOK], psum[0:C, A:A + N_TOK - 1]).then_inc(hT_out, 1)
                    dve.wait_ge(turned, 1)
                    nc.vector.tensor_copy(flat(h_tok), psum[:, B:B + NT * C])

                @block.tensor
                def _(pe):
                    pe.wait_ge(padded, 1)
                    for half in range(2):
                        o = psum[0:C, A + half * 512:A + (half + 1) * 512]
                        for u in range(8):
                            rhs = series[:, u:u + 4 * (N_PATCH - 1) + 1:4, half * 32:(half + 1) * 32]
                            last = nc.tensor.matmul(o, w_tok[:, u, :], rhs.rearrange("p n v -> p v n"),
                                                    start=(u == 0), stop=(u == 7))
                    last.then_inc(embedded, 1)
                    pe.wait_ge(hT_out, 1)
                    for t in range(NT):
                        last = nc.tensor.transpose(psum[:, B + t * C:B + (t + 1) * C],
                                                   hT[:, t * P:(t + 1) * P], ident[0:C, 0:C])
                    last.then_inc(turned, 1)

        def phasor():
            layer_norm()
            with ExitStack() as c2:
                def b(name, shape):
                    return c2.enter_context(scratch(name, shape))
                hid_p, hid_h = b("hid_p", [P, NP]), b("hid_h", [P, NP])
                pre = b("pre", [P, NT, 160])
                val = b("val", [P, NT, C])
                half_sin, half_cos = b("half_sin", [P, NT, 96]), b("half_cos", [P, NT, 96])
                feat = b("feat", [P, 2, NT, P])
                featT = b("featT", [P, 2, NP])
                rad = b("rad", [P, 4, NT, 32])
                ret = b("ret", [P, NT, C])
                local = b("local", [P, 2, P])
                memory = b("memory", [P, 2, C])
                with ph.phase("hid_in", "hid_out", "pre_in", "val_in") as (block, hid_in, hid_out, pre_in, val_in):
                    @block.tensor
                    def _(pe):
                        columns(A, P, [(a_w1p, xT[:])]).then_inc(hid_in, 1)
                        columns(B, P, [(a_w1h, xT[:])]).then_inc(hid_in, 1)
                        for t in range(NT):
                            o = psum[:, D + t * C:D + (t + 1) * C]
                            last = nc.tensor.matmul(o, xT[:, t * P:(t + 1) * P], a_vw, start=True, stop=True)
                        last.then_inc(val_in, 1)
                        pe.wait_ge(hid_out, 2)
                        for t in range(NT):
                            o = A + (t // 3) * 512 + (t % 3) * 160
                            s = slice(t * P, (t + 1) * P)
                            nc.tensor.matmul(psum[:, o:o + 96], hid_p[:, s], a_w2p[:], start=True, stop=False)
                            nc.tensor.matmul(psum[:, o + 96:o + 160], hid_h[:, s], a_w2h[:], start=False, stop=False)
                            last = nc.tensor.matmul(psum[:, o:o + 160], ones[0:1, :], a_b2, start=False, stop=True)
                        last.then_inc(pre_in, 1)

                    @block.scalar
                    def _(act):
                        act.wait_ge(hid_in, 1)
                        nc.scalar.activation(hid_p[:], psum[:, A:A + NP], ACT.Gelu, bias=a_b1p).then_inc(hid_out, 1)
                        act.wait_ge(hid_in, 2)
                        nc.scalar.activation(hid_h[:], psum[:, B:B + NP], ACT.Gelu, bias=a_b1h).then_inc(hid_out, 1)
                        act.wait_ge(pre_in, 1)
                        for j in range(3):
                            o = psum[:, A + j * 512:A + j * 512 + 480].rearrange("p (t f) -> p t f", f=160)
                            nc.scalar.activation(pre[:, 3 * j:3 * j + 3, :], o, ACT.Tanh)

                    @block.vector
                    def _(dve):
                        dve.wait_ge(val_in, 1)
                        nc.vector.tensor_copy(flat(val), psum[:, D:D + NT * C])

                with ph.phase("angles", "radii2", "sines", "radii", "featured", "turned", "dve_step") as (
                        block, angles, radii2, sines, radii, featured, turned, dve_step):
                    ang = pre[:, :, 0:96]
                    pair = pre[:, :, 96:160].rearrange("p t (n c) -> p t n c", c=2)

                    @block.vector
                    def _(dve):
                        step = Steps(dve, dve_step)
                        nc.vector.scalar_tensor_tensor(half_cos[:], ang, -1.0, ang, ALU.mult, ALU.max).then_inc(angles, 1)
                        step(nc.vector.tensor_scalar(pair, pair, 0.9, None, ALU.mult))
                        step(nc.vector.tensor_tensor(rad[:, 0], pair[:, :, :, 0], pair[:, :, :, 0], ALU.mult))
                        step(nc.vector.tensor_tensor(rad[:, 1], pair[:, :, :, 1], pair[:, :, :, 1], ALU.mult))
                        step(nc.vector.tensor_tensor(rad[:, 0], rad[:, 0], rad[:, 1], ALU.add))
                        step(nc.vector.tensor_scalar(rad[:, 1], rad[:, 0], 0.0, None, ALU.is_equal))
                        nc.vector.tensor_tensor(pair[:, :, :, 0], pair[:, :, :, 0], rad[:, 1], ALU.add).then_inc(radii2, 1)
                        dve.wait_ge(radii2, 1)
                        dve.wait_ge(radii, 1)
                        step(nc.vector.tensor_tensor(rad[:, 3], rad[:, 2], rad[:, 1], ALU.add))
                        step(nc.vector.reciprocal(rad[:, 3], rad[:, 3]))
                        step(nc.vector.tensor_scalar(rad[:, 2], rad[:, 2], -1.0, 1.0, ALU.mult, ALU.add))
                        step(nc.vector.tensor_tensor(rad[:, 3], rad[:, 3], rad[:, 2], ALU.mult))
                        for kq in range(2):
                            s = slice(kq * 16, (kq + 1) * 16)
                            nc.vector.tensor_tensor(feat[:, kq, :, NPER:64], pair[:, :, s, 0], rad[:, 3, :, s], ALU.mult)
                            nc.vector.tensor_tensor(feat[:, kq, :, 64 + NPER:P], pair[:, :, s, 1], rad[:, 3, :, s], ALU.mult)
                        dve.wait_ge(sines, 1)
                        step(nc.vector.scalar_tensor_tensor(half_cos[:], half_cos[:], 2.0, half_sin[:], ALU.mult, ALU.mult))
                        step(nc.vector.tensor_tensor(half_sin[:], half_sin[:], half_sin[:], ALU.mult))
                        for kq in range(2):
                            s = slice(kq * NPER, (kq + 1) * NPER)
                            step(nc.vector.tensor_copy(feat[:, kq, :, 64:64 + NPER], half_cos[:, :, s]))
                            step(nc.vector.tensor_scalar(feat[:, kq, :, 0:NPER], half_sin[:, :, s], -2.0, 1.0,
                                                         ALU.mult, ALU.add))
                        nc.vector.tensor_copy(stat[:, 0], stat[:, 4]).then_inc(featured, 1)

                    @block.scalar
                    def _(act):
                        act.wait_ge(radii2, 1)
                        nc.scalar.activation(rad[:, 2], rad[:, 0], ACT.Sqrt).then_inc(radii, 1)
                        nc.scalar.activation(half_sin[:], ang, ACT.Sin, scale=math.pi / 2)
                        nc.scalar.activation(half_cos[:], half_cos[:], ACT.Sin, scale=-math.pi / 2,
                                             bias=eps[:, 2:3]).then_inc(sines, 1)
                        for kq in range(2):
                            act.wait_ge(turned, kq + 1)
                            r = A if kq == 0 else B
                            nc.scalar.copy(featT[:, kq, :], psum[:, r:r + NP])

                    @block.tensor
                    def _(pe):
                        pe.wait_ge(featured, 1)
                        turn_tiles(A, feat[:, 0], P).then_inc(turned, 1)
                        turn_tiles(B, feat[:, 1], P).then_inc(turned, 1)

                with ph.phase("scored", "masked", "grown", "kept", "read", "read_out", "dve_step") as (
                        block, scored, masked, grown, kept, read, read_out, dve_step):
                    @block.tensor
                    def _(pe):
                        def score(t):
                            s = slice(t * P, (t + 1) * P)
                            if t >= 2:
                                pe.wait_ge(masked, t - 1)
                            nc.tensor.matmul(psum[:, A + (t % 2) * 512:A + (t % 2) * 512 + P], featT[:, 0, s],
                                             featT[:, 1, s], start=True, stop=True).then_inc(scored, 1)

                        score(0)
                        for t in range(NT):
                            if t + 1 < NT:
                                score(t + 1)
                            if t >= 2:
                                pe.wait_ge(kept, t - 1)
                            g = B + (t % 2) * 512
                            nc.tensor.matmul(psum[:, g:g + C], feat[:, 0, t, :], val[:, t, :],
                                             start=True, stop=True).then_inc(grown, 1)
                            pe.wait_ge(masked, t + 1)
                            if t >= 2:
                                pe.wait_ge(read_out, t - 1)
                            o = psum[:, D + (t % 2) * 512:D + (t % 2) * 512 + C]
                            m = nc.tensor.matmul(o, local[:, t % 2, :], val[:, t, :], start=True, stop=(t == 0))
                            if t >= 1:
                                pe.wait_ge(kept, t)
                                m = nc.tensor.matmul(o, featT[:, 1, t * P:(t + 1) * P], memory[:, (t - 1) % 2, :],
                                                     start=False, stop=True)
                            m.then_inc(read, 1)

                    @block.vector
                    def _(dve):
                        def read_tile(t):
                            dve.wait_ge(read, t + 1)
                            nc.vector.tensor_scalar(ret[:, t, :], psum[:, D + (t % 2) * 512:D + (t % 2) * 512 + C],
                                                    pos_norm[:, t:t + 1], None, ALU.mult).then_inc(read_out, 1)

                        for t in range(NT):
                            dve.wait_ge(scored, t + 1)
                            if t >= 2:
                                dve.wait_ge(read, t - 1)
                            nc.vector.tensor_tensor(local[:, t % 2, :], psum[:, A + (t % 2) * 512:A + (t % 2) * 512 + P],
                                                    upto_q, ALU.mult).then_inc(masked, 1)
                            dve.wait_ge(grown, t + 1)
                            g = B + (t % 2) * 512
                            if t == 0:
                                nc.vector.tensor_copy(memory[:, 0, :], psum[:, g:g + C]).then_inc(kept, 1)
                            else:
                                read_tile(t - 1)
                                dve.wait_ge(kept, t)
                                nc.vector.tensor_tensor(memory[:, t % 2, :], memory[:, (t - 1) % 2, :], psum[:, g:g + C],
                                                        ALU.add).then_inc(kept, 1)
                        read_tile(NT - 1)
                layer_norm(src=ret, dst=y_tok, want_T=False)
                with ph.phase("scaled", "turned", "dve_step") as (block, scaled, turned, dve_step):
                    @block.vector
                    def _(dve):
                        step = Steps(dve, dve_step)
                        step(nc.vector.tensor_tensor(y_tok[:], y_tok[:], bc(a_g, [P, NT, C], 1), ALU.mult))
                        nc.vector.tensor_tensor(y_tok[:], y_tok[:], bc(a_b, [P, NT, C], 1), ALU.add).then_inc(scaled, 1)

                    @block.tensor
                    def _(pe):
                        pe.wait_ge(scaled, 1)
                        turn_tiles(A, y_tok, C).then_inc(turned, 1)

                    @block.scalar
                    def _(act):
                        act.wait_ge(turned, 1)
                        nc.scalar.copy(yT[0:C, :], psum[0:C, A:A + NP])
            project_add([yT], [a_ow], extra=x_tok)

        def rotary_queries(q_all, k_all, v_all):
            layer_norm()
            layer_norm(rms_weight=f_ln1, src=x_tok, dst=y_tok)
            with scratch("qkv", [P, NT, P]) as qkv, scratch("rot", [P, NT, 6, 16]) as rot:
                with ph.phase("qkv_in", "dve_step") as (block, qkv_in, dve_step):
                    @block.tensor
                    def _(pe):
                        for t in range(NT):
                            last = nc.tensor.matmul(psum[:, A + t * P:A + (t + 1) * P], xT[:, t * P:(t + 1) * P], f_qkv,
                                                    start=True, stop=True)
                        last.then_inc(qkv_in, 1)

                    @block.vector
                    def _(dve):
                        step = Steps(dve, dve_step)
                        dve.wait_ge(qkv_in, 1)
                        step(nc.vector.tensor_copy(flat(qkv), psum[:, A:A + NP]))
                        qk = qkv[:, :, 0:96].rearrange("p t (h d) -> p t h d", d=16)
                        step(nc.vector.tensor_tensor(rot[:, :, :, 0:8], qk[:, :, :, 8:16],
                                                     bc(sin[:, :, 0:8], [P, NT, 6, 8], 2), ALU.mult))
                        step(nc.vector.tensor_tensor(rot[:, :, :, 8:16], qk[:, :, :, 0:8],
                                                     bc(sin[:, :, 8:16], [P, NT, 6, 8], 2), ALU.mult))
                        step(nc.vector.tensor_tensor(qk, qk, bc(cos, [P, NT, 6, 16], 2), ALU.mult))
                        r6 = rot[:].rearrange("p t h d -> p t (h d)")
                        nc.vector.tensor_tensor(q_all[:], qkv[:, :, 0:64], r6[:, :, 0:64], ALU.add)
                        for h in range(4):
                            g = h // 2
                            nc.vector.tensor_tensor(k_all[:, :, h * 16:h * 16 + 16], qkv[:, :, 64 + g * 16:80 + g * 16],
                                                    r6[:, :, 64 + g * 16:80 + g * 16], ALU.add)
                            nc.vector.tensor_copy(v_all[:, :, h * 16:h * 16 + 16], qkv[:, :, 96 + g * 16:112 + g * 16])

        def rotary_out():
            with ph.phase("turned", "turned_out", "projected") as (block, turned, turned_out, projected):
                @block.tensor
                def _(pe):
                    turn_tiles(A, y_tok, C).then_inc(turned, 1)
                    pe.wait_ge(turned_out, 1)
                    for t in range(NT):
                        last = nc.tensor.matmul(psum[:, D + t * C:D + (t + 1) * C], yT[:, t * P:(t + 1) * P], f_wo,
                                                start=True, stop=True)
                    last.then_inc(projected, 1)

                @block.scalar
                def _(act):
                    act.wait_ge(turned, 1)
                    nc.scalar.copy(yT[0:C, :], psum[0:C, A:A + NP]).then_inc(turned_out, 1)

                @block.vector
                def _(dve):
                    dve.wait_ge(projected, 1)
                    nc.vector.tensor_tensor(flat(x_tok), flat(x_tok), psum[:, D:D + NT * C], ALU.add)
            layer_norm(rms_weight=f_ln2, src=x_tok, dst=y_tok)
            route(lambda t, o: nc.tensor.matmul(o, xT[:, t * P:(t + 1) * P], f_router, start=True, stop=True),
                  True, 1e-9, 0.0)

        EXPERT_SEMS = ("weights_in", "gate_in", "up_in", "gated", "hid_out", "expert_out", "e_weighed", "e_added")

        class Experts:

            def __init__(self, sems, buf):
                (self.weights_in, self.gate_in, self.up_in, self.gated, self.hid_out, self.expert_out, self.weighed,
                 self.added) = sems
                self.w1, self.w3, self.w2, self.gate, self.hid, self.part = buf

            def load(self, sp, first):
                for dst, src in ((self.w1, "f_w1"), (self.w3, "f_w3")):
                    sp.dma_start(dst[0:C], io[src][:, bass.ds(first * HID0, 2 * HID0)]).then_inc(self.weights_in, 16)
                sp.dma_start(self.w2[:], io["f_w2"][:, bass.ds(first * 2, 4)]).then_inc(self.weights_in, 16)

            def run_tensor(self, pe):
                pe.wait_ge(self.weights_in, 48)
                for i in range(4):
                    w = slice(i * HB, (i + 1) * HB)
                    if i >= 1:
                        pe.wait_ge(self.gated, i)
                    columns(A, HB, [(self.w1[:, w], xT[:])]).then_inc(self.gate_in, 1)
                    if i >= 1:
                        pe.wait_ge(self.hid_out, i)
                    columns(B, HB, [(self.w3[:, w], xT[:])]).then_inc(self.up_in, 1)
                    if i % 2 == 1:
                        pe.wait_ge(self.hid_out, i + 1)
                        if i == 3:
                            pe.wait_ge(self.weighed, 1)
                        for t in range(NT):
                            o = psum[:, D + t * C:D + (t + 1) * C]
                            for j in range(2):
                                last = nc.tensor.matmul(o, self.hid[:, j, t * P:(t + 1) * P], self.w2[:, i - 1 + j, :],
                                                        start=(j == 0), stop=(j == 1))
                        last.then_inc(self.expert_out, 1)

            def run_scalar(self, act):
                for i in range(4):
                    act.wait_ge(self.gate_in, i + 1)
                    if i >= 1:
                        act.wait_ge(self.hid_out, i)
                    nc.scalar.activation(self.gate[:], psum[0:HB, A:A + NP], ACT.Silu).then_inc(self.gated, 1)

            def hidden(self, dve, i):
                dve.wait_ge(self.gated, i + 1)
                dve.wait_ge(self.up_in, i + 1)
                if i >= 2:
                    dve.wait_ge(self.expert_out, i // 2)
                nc.vector.tensor_tensor(self.hid[:, i % 2, :], self.gate[:], psum[0:HB, B:B + NP],
                                        ALU.mult).then_inc(self.hid_out, 1)

            def output(self, dve, n, expert):
                dve.wait_ge(self.expert_out, n + 1)
                if n:
                    dve.wait_ge(self.added, n)
                o = psum[:, D:D + NT * C].rearrange("p (t c) -> p t c", c=C)
                nc.vector.tensor_tensor(self.part[:], o, rt_w[:, :, bass.ds(expert, 1)].broadcast_to([P, NT, C]),
                                        ALU.mult).then_inc(self.weighed, 1)
                dve.wait_ge(self.weighed, n + 1)
                nc.vector.tensor_tensor(flat(x_tok), flat(x_tok), flat(self.part), ALU.add).then_inc(self.added, 1)

        def state_space():
            layer_norm()
            with ExitStack() as c2:
                def b(name, shape):
                    return c2.enter_context(scratch(name, shape))
                xin = b("xin", [P, TAPS - 1 + NP])
                w_rep = b("w_rep", [P, 1 + 2 * NSTATE, P])
                gz, u, dt, dtu, ys = b("gz", [P, NP]), b("u", [P, NP]), b("dt", [P, NP]), b("dtu", [P, NP]), b("ys", [P, NP])
                decay, drive, state, part = b("decay", [P, 2, NP]), b("drive", [P, 2, NP]), b("state", [P, 2, NP]), b("part", [P, 2, NP])
                with ph.phase("xz_in", "gate_out", "repeated", "u_out", "dt_in", "pre_out", "e_out", "l_out",
                              "dve_step") as (block, xz_in, gate_out, repeated, u_out, dt_in, pre_out, e_out, l_out,
                                              dve_step):
                    @block.gpsimd
                    def _(pool):
                        for n0, n1 in ((0, 1), (1, 1 + 2 * NSTATE)):
                            nc.gpsimd.tensor_copy(w_rep[:, n0:n1], bc(m_xp[:, n0:n1], [P, n1 - n0, P], 2)).then_inc(repeated, 1)

                    @block.tensor
                    def _(pe):
                        columns(A, P, [(m_in[:, 0:P], xT[:])]).then_inc(xz_in, 1)
                        columns(B, P, [(m_in[:, P:2 * P], xT[:])]).then_inc(xz_in, 1)
                        pe.wait_ge(u_out, 1)
                        pe.wait_ge(repeated, 1)
                        columns(A, P, [(w_rep[:, 0, :], u[:])]).then_inc(dt_in, 1)

                    @block.scalar
                    def _(act):
                        act.wait_ge(xz_in, 2)
                        nc.scalar.activation(gz[:], psum[:, B:B + NP], ACT.Sigmoid).then_inc(gate_out, 1)
                        act.wait_ge(pre_out, 1)
                        nc.scalar.activation(gz[:], gz[:], ACT.Exp, scale=-1.0).then_inc(e_out, 1)
                        act.wait_ge(e_out, 1)
                        nc.scalar.activation(gz[:], gz[:], ACT.Ln, bias=ones[:, 0:1]).then_inc(l_out, 1)

                    @block.vector
                    def _(dve):
                        step = Steps(dve, dve_step)
                        nc.vector.memset(xin[:, 0:TAPS - 1], 0.0)
                        dve.wait_ge(xz_in, 1)
                        step(nc.vector.tensor_copy(xin[:, TAPS - 1:], psum[:, A:A + NP]))
                        step(nc.vector.tensor_scalar(u[:], xin[:, 0:NP], m_cw[:, 0:1], m_cb[:, 0:1], ALU.mult, ALU.add))
                        for k in range(1, TAPS):
                            step(nc.vector.scalar_tensor_tensor(u[:], xin[:, k:k + NP], m_cw[:, k:k + 1], u[:],
                                                                ALU.mult, ALU.add))
                        dve.wait_ge(gate_out, 1)
                        nc.vector.tensor_tensor(u[:], u[:], gz[:], ALU.mult).then_inc(u_out, 1)
                        dve.wait_ge(dt_in, 1)
                        step(nc.vector.tensor_scalar(dtu[:], psum[:, A:A + NP], m_wdt[:, 0:1], m_bdt[:, 0:1],
                                                     ALU.mult, ALU.add))
                        nc.vector.scalar_tensor_tensor(gz[:], dtu[:], -1.0, dtu[:], ALU.mult, ALU.max).then_inc(pre_out, 1)
                        dve.wait_ge(l_out, 1)
                        step(nc.vector.scalar_tensor_tensor(dt[:], dtu[:], 0.0, gz[:], ALU.max, ALU.add))
                        nc.vector.tensor_tensor(dtu[:], dt[:], u[:], ALU.mult)
                        nc.vector.tensor_scalar(ys[:], u[:], m_D[:, 0:1], None, ALU.mult)

                with ph.phase("decayed", "b_in", "c_in", "driven", "scanned", "shown", "summed") as (
                        block, decayed, b_in, c_in, driven, scanned, shown, summed):
                    @block.tensor
                    def _(pe):
                        for n in range(NSTATE):
                            if n >= 1:
                                pe.wait_ge(driven, n)
                            columns(A, P, [(w_rep[:, 1 + n, :], u[:])]).then_inc(b_in, 1)
                            if n >= 1:
                                pe.wait_ge(shown, n)
                            columns(B, P, [(w_rep[:, 1 + NSTATE + n, :], u[:])]).then_inc(c_in, 1)

                    @block.scalar
                    def _(act):
                        for n in range(NSTATE):
                            if n >= 2:
                                act.wait_ge(scanned, n - 1)
                            nc.scalar.activation(decay[:, n % 2, :], dt[:], ACT.Exp, scale=m_A[:, n:n + 1]).then_inc(decayed, 1)

                    @block.vector
                    def _(dve):
                        for n in range(NSTATE):
                            s = n % 2
                            dve.wait_ge(b_in, n + 1)
                            if n >= 2:
                                dve.wait_ge(scanned, n - 1)
                            nc.vector.tensor_tensor(drive[:, s, :], dtu[:], psum[:, A:A + NP], ALU.mult).then_inc(driven, 1)
                            dve.wait_ge(driven, n + 1)
                            dve.wait_ge(decayed, n + 1)
                            if n >= 2:
                                dve.wait_ge(shown, n - 1)
                            nc.vector.tensor_tensor_scan(state[:, s, :], decay[:, s, :], drive[:, s, :], 0.0,
                                                         ALU.mult, ALU.add).then_inc(scanned, 1)
                            dve.wait_ge(scanned, n + 1)
                            dve.wait_ge(c_in, n + 1)
                            if n >= 2:
                                dve.wait_ge(summed, n - 1)
                            nc.vector.tensor_tensor(part[:, s, :], state[:, s, :], psum[:, B:B + NP], ALU.mult).then_inc(shown, 1)

                    @block.gpsimd
                    def _(pool):
                        for n in range(NSTATE):
                            pool.wait_ge(shown, n + 1)
                            if n >= 1:
                                pool.wait_ge(summed, n)
                            nc.gpsimd.tensor_tensor(ys[:], ys[:], part[:, n % 2, :], ALU.add).then_inc(summed, 1)
                project_add([ys], [m_out])

        dram_kv = nc.dram_tensor("dram_kv", [N_BATCH, P + N_TOK, PKH, P], F32, kind="Internal").ap()
        dram_q = nc.dram_tensor("dram_q", [N_BATCH, N_TOK, 512], F32, kind="Internal").ap()
        FULL = (NT - 1) * P

        dram_qpk = nc.dram_tensor("dram_qpk", [N_BATCH, NT, P, 4, P], F32, kind="Internal").ap()
        dram_y = nc.dram_tensor("dram_y", [N_BATCH, NT, P, 512], F32, kind="Internal").ap()

        def key_queries(b):
            layer_norm()
            with scratch("q_all", [P, NT, 512]) as q_all, scratch("qpkT", [P, 4, NP]) as qpkT, \
                    ph.phase("q_in", "q_out", "q_stored") as (block, q_in, q_out, q_stored):
                @block.tensor
                def _(pe):
                    for t in range(NT):
                        if t >= 2:
                            pe.wait_ge(q_out, t - 1)
                        nc.tensor.matmul(psum[:, D + (t % 2) * 512:D + (t % 2 + 1) * 512], xT[:, t * P:(t + 1) * P],
                                         k_wq, start=True, stop=True).then_inc(q_in, 1)
                    for c in range(4):
                        if c >= 2:
                            pe.wait_ge(q_out, NT + c - 1)
                        columns(A if c % 2 == 0 else B, P, [(k_wqpk[:, c * P:(c + 1) * P], xT[:])]).then_inc(q_in, 1)

                @block.scalar
                def _(act):
                    for t in range(NT):
                        act.wait_ge(q_in, t + 1)
                        nc.scalar.mul(q_all[:, t, :], psum[:, D + (t % 2) * 512:D + (t % 2 + 1) * 512],
                                      C ** -0.5).then_inc(q_out, 1)
                    for c in range(4):
                        r = A if c % 2 == 0 else B
                        act.wait_ge(q_in, NT + c + 1)
                        nc.scalar.copy(qpkT[:, c, :], psum[:, r:r + NP]).then_inc(q_out, 1)

                @block.sync
                def _(sp):
                    sp.wait_ge(q_out, NT)
                    qb = dram_q[bass.ds(b, 1)].rearrange("a n c -> (a n) c")
                    sp.dma_start(qb[0:FULL].rearrange("(t p) c -> p t c", p=P), q_all[:, 0:NT - 1, :]).then_inc(q_stored, 16)
                    sp.dma_start(qb[FULL:N_TOK], q_all[0:N_TOK - FULL, NT - 1, :]).then_inc(q_stored, 16)
                    for c in range(4):
                        sp.wait_ge(q_out, NT + c + 1)
                        sp.dma_start(dram_qpk[bass.ds(b, 1), :, :, c, :].rearrange("a t p n -> p (a t) n"),
                                     qpkT[:, c, :].rearrange("p (t n) -> p t n", n=P)).then_inc(q_stored, 16)
                    sp.wait_ge(q_stored, 96)

        SEARCH_SEMS = ("tile_in", "half_in", "sims", "s_shifted", "exps", "found", "search_step")

        class Search:

            def __init__(self, sems, buf):
                self.tile_in, self.half_in, self.sims, self.shifted, self.exps, self.found, self.step_sem = sems
                (self.qt, self.sim, self.sim2, self.best, self.bidx, self.bidf, self.cand, self.cand2,
                 self.cidx, self.fin, self.fpos, self.fposf, self.wgt, self.wsum, self.hot, self.gidf) = buf

            def load(self, sp, b, tile):
                sp.dma_start(self.qt[:], dram_qpk[bass.ds(b, 1), bass.ds(tile, 1)].rearrange("a t p c n -> (a t p) c n")
                             ).then_inc(self.tile_in, 16)

            def fetch(self, act):
                for half in range(2):
                    act.wait_ge(self.half_in, half + 1)
                    nc.scalar.copy(self.sim[:, half * 512:(half + 1) * 512], psum[:, F:F + 512]).then_inc(self.sims, 1)

            def exponentials(self, act):
                act.wait_ge(self.shifted, 1)
                nc.scalar.activation(self.wgt[:], self.wgt[:], ACT.Exp).then_inc(self.exps, 1)

            def run_tensor(self, pe):
                pe.wait_ge(self.tile_in, 16)
                for half in range(2):
                    if half:
                        pe.wait_ge(self.sims, half)
                    for j in range(2):
                        last = nc.tensor.matmul(psum[:, F + j * 256:F + (j + 1) * 256], self.qt[:, 2 * half + j, :],
                                                k_keys[:, 2 * half + j, :], start=True, stop=True)
                    last.then_inc(self.half_in, 1)

            def begin(self, dve):
                self.step = Steps(dve, self.step_sem)
                self.dve = dve

            def half(self, half):
                self.dve.wait_ge(self.sims, half + 1)
                sim = self.sim[:].rearrange("p (g k) -> p g k", k=PKK)
                best, bidx, sim2 = self.best, self.bidx, self.sim2
                G = range(half * PKH, (half + 1) * PKH)
                for g in G:
                    ins = nc.vector.max(best[:, g, 0:8], sim[:, g, :])
                self.step(ins)
                for g in G:
                    nc.vector.max_index(bidx[:, g, 0:8], best[:, g, 0:8], sim[:, g, :])
                    ins = nc.vector.match_replace(sim2[:, g, :], best[:, g, 0:8], sim[:, g, :], LOWEST)
                self.step(ins)
                for g in G:
                    ins = nc.vector.max(best[:, g, 8:16], sim2[:, g, :])
                self.step(ins)
                for g in G:
                    ins = nc.vector.max_index(bidx[:, g, 8:16], best[:, g, 8:16], sim2[:, g, :])
                self.step(ins)

            def pairs(self):
                step, best, bidf = self.step, self.best, self.bidf
                step(nc.vector.tensor_copy(flat(bidf), flat(self.bidx)))
                step(nc.vector.tensor_scalar(bidf[:, PKH:, :], bidf[:, PKH:, :], float(PKK), None, ALU.mult))
                step(nc.vector.tensor_tensor(bidf[:, 0:PKH, :], bidf[:, 0:PKH, :],
                                             bc(headoff, [P, PKH, TOPK], 2), ALU.add))
                for dst, src in ((self.cand, best), (self.cidx, bidf)):
                    for o, i0, i1, nj in PAIRS:
                        ni = i1 - i0
                        d = dst[:, :, o:o + ni * nj].rearrange("p h (i j) -> p h i j", j=nj)
                        ins = nc.vector.tensor_tensor(d, bc(src[:, 0:PKH, i0:i1], [P, PKH, ni, nj], 3),
                                                      bc(src[:, PKH:, 0:nj], [P, PKH, ni, nj], 2), ALU.add)
                step(ins)

            def top_pairs(self):
                step, fin, fpos, cand, cand2 = self.step, self.fin, self.fpos, self.cand, self.cand2
                for h in range(PKH):
                    ins = nc.vector.max(fin[:, h, 0:8], cand[:, h, :])
                step(ins)
                for h in range(PKH):
                    nc.vector.max_index(fpos[:, h, 0:8], fin[:, h, 0:8], cand[:, h, :])
                    ins = nc.vector.match_replace(cand2[:, h, :], fin[:, h, 0:8], cand[:, h, :], LOWEST)
                step(ins)
                for h in range(PKH):
                    ins = nc.vector.max(fin[:, h, 8:16], cand2[:, h, :])
                step(ins)
                nc.vector.tensor_tensor(self.wgt[:], fin[:], fin[:, :, 0:1].broadcast_to([P, PKH, TOPK]),
                                        ALU.subtract).then_inc(self.shifted, 1)
                for h in range(PKH):
                    ins = nc.vector.max_index(fpos[:, h, 8:16], fin[:, h, 8:16], cand2[:, h, :])
                step(ins)
                step(nc.vector.tensor_copy(flat(self.fposf), flat(fpos)))

            def rows_of(self, heads):
                for h in heads:
                    s = self.hot[:]
                    self.step(nc.vector.tensor_tensor(s, bc(self.fposf[:, h, :], [P, TOPK, NPAIR], 2),
                                                      bc(iota, [P, TOPK, NPAIR], 1), ALU.is_equal))
                    self.step(nc.vector.tensor_tensor(s, s, bc(self.cidx[:, h, :], [P, TOPK, NPAIR], 1), ALU.mult))
                    self.step(nc.vector.tensor_reduce(self.gidf[:, h, :], s, AX.X, ALU.add))

            def weights(self):
                self.dve.wait_ge(self.exps, 1)
                self.step(nc.vector.tensor_reduce(self.wsum[:, 0], self.wgt[:], AX.X, ALU.add))
                self.step(nc.vector.reciprocal(self.wsum[:, 1], self.wsum[:, 0]))
                self.step(nc.vector.tensor_tensor(self.wgt[:], self.wgt[:], bc(self.wsum[:, 1], [P, PKH, TOPK], 2), ALU.mult))

        search_buf = [sb("qt", [P, 4, P]), sb("sim", [P, 16 * PKK]), sb("sim2", [P, 16, PKK]), sb("best", [P, 16, TOPK]),
                      sb("bidx", [P, 16, TOPK], U32), sb("bidf", [P, 16, TOPK]), sb("cand", [P, PKH, NPAIR]),
                      sb("cand2", [P, PKH, NPAIR]), sb("cidx", [P, PKH, NPAIR]), sb("fin", [P, PKH, TOPK]),
                      sb("fpos", [P, PKH, TOPK], U32), sb("fposf", [P, PKH, TOPK]), sb("wgt", [P, PKH, TOPK]),
                      sb("wsum", [P, 2, PKH]), sb("hot", [P, TOPK, NPAIR]), sb("gidf", [P, PKH, TOPK])]
        gidx, wnow, wlast = sb("gidx", [P, PKH, TOPK], U32), sb("wnow", [P, PKH, TOPK]), sb("wlast", [P, TOPK])
        rows, acc = sb("rows", [P, 2, TOPK, P]), sb("acc", [P, 2, P])
        kv_tile, kv_last = sb("kv_tile", [P, PKH, P]), sb("kv_last", [P, P])
        lastcol, lastw, lastix = sb("lastcol", [P, 1]), sb("lastw", [P, PKH]), sb("lastix", [P, 1], U32)

        class Rows:

            def __init__(self, b):
                self.b = b
                self.gidx, self.wnow, self.wlast, self.rows, self.acc = gidx, wnow, wlast, rows, acc
                self.kv_tile, self.kv_last, self.lastcol, self.lastw, self.lastix = kv_tile, kv_last, lastcol, lastw, lastix

            def sum_rows(self, dve, i, rows, weights, out, acc_even, acc_odd, rows_used):
                for k in range(TOPK):
                    s, sem = k % 2, (acc_even, acc_odd)[k % 2]
                    if k >= 2 or i:
                        dve.wait_ge(sem, (TOPK // 2) * i + k // 2)
                    if k == 0 and i:
                        dve.wait_ge(rows_used, i)
                    if k < 2:
                        ins = nc.vector.tensor_scalar(self.acc[:, s], rows[:, k, :], weights[:, k:k + 1], None, ALU.mult)
                    else:
                        ins = nc.vector.scalar_tensor_tensor(self.acc[:, s], rows[:, k, :], weights[:, k:k + 1],
                                                             self.acc[:, s], ALU.mult, ALU.add)
                    ins.then_inc(sem, 1)
                for sem in (acc_even, acc_odd):
                    dve.wait_ge(sem, (TOPK // 2) * (i + 1))
                nc.vector.tensor_tensor(out, self.acc[:, 0], self.acc[:, 1], ALU.add).then_inc(rows_used, 1)

        def first_search(b):
            with ph.phase(*SEARCH_SEMS) as (block, *sems):
                first = Search(sems, search_buf)

                @block.sync
                def _(sp):
                    first.load(sp, b, 0)

                @block.scalar
                def _(act):
                    first.fetch(act)
                    first.exponentials(act)

                @block.tensor
                def _(pe):
                    first.run_tensor(pe)

                @block.vector
                def _(dve):
                    first.begin(dve)
                    first.half(0)
                    first.half(1)
                    first.pairs()
                    first.top_pairs()
                    first.rows_of(range(PKH))
                    first.weights()

        def rounds(t_first, rw, b_heads, hbuf, rotary=None, experts=None):
            with nc.Fori(t_first, t_first + 4) as t:
                own = ("head_in", "r_head_in", "rows_named", "rows_even", "rows_odd", "rows_used", "acc_even", "acc_odd",
                       "tile_stored")
                layer_0_sems = ["r_" + n for n in HEAD_SEMS] if rotary else EXPERT_SEMS if experts else ()
                with ph.phase(*own, *(HEAD_SEMS if b_heads is not None else ()), *(SEARCH_SEMS if rw else ()),
                              *layer_0_sems) as (block, *sems):
                    (head_in, r_head_in, rows_named, rows_even, rows_odd, rows_used, acc_even, acc_odd,
                     tile_stored), sems = sems[:len(own)], sems[len(own):]
                    head = y_h = search = None
                    if b_heads is not None:
                        head, y_h = Head(sems[:len(HEAD_SEMS)], hbuf[:-1], C, C, 1.0), hbuf[-1]
                        sems = sems[len(HEAD_SEMS):]
                    if rw:
                        search, sems = Search(sems[:len(SEARCH_SEMS)], search_buf), sems[len(SEARCH_SEMS):]
                    if rotary:
                        q_all, k_all, v_all, rbuf = rotary
                        rhead = Head(sems, rbuf, 16, 32, 0.25)
                        of_head = bass.ds((t - t_first) * 16, 16)
                    if experts:
                        pair = Experts(sems, experts)
                        e_first = (t - t_first) * 2

                    @block.sync
                    def _(sp):
                        if rw:
                            search.load(sp, rw.b, t + 1)
                            sp.wait_ge(rows_used, 1)
                            sp.dma_start(dram_kv[bass.ds(rw.b, 1), bass.ds(t * P, P), PKH - 1].rearrange("a n d -> (a n) d"),
                                         rw.kv_last[:]).then_inc(tile_stored, 16)
                        if head:
                            kv = dram_kv[bass.ds(b_heads, 1), P:P + N_TOK, bass.ds(t, 1), :].rearrange("a n h d -> (a n) (h d)")
                            qb = dram_q[bass.ds(b_heads, 1), :, bass.ds(t * C, C)].rearrange("a n c -> (a n) c")
                            for dst, src in ((head.q_h, qb), (head.k_h, kv[:, 0:C]), (head.v_h, kv[:, C:P])):
                                sp.dma_start(dst[:, 0:NT - 1, 0:C], src[0:FULL].rearrange("(t p) c -> p t c", p=P)
                                             ).then_inc(head_in, 16)
                                sp.dma_start(dst[0:N_TOK - FULL, NT - 1, 0:C], src[FULL:N_TOK]).then_inc(head_in, 16)
                        if experts:
                            pair.load(sp, e_first)
                        if head:
                            sp.wait_ge(head.normed, 1)
                            sp.dma_start(dram_y[bass.ds(b_heads, 1), :, :, bass.ds(t * C, C)].rearrange("a t p c -> p (a t) c"),
                                         y_h[:]).then_inc(tile_stored, 16)
                        if rw:
                            sp.wait_ge(rows_used, PKH)
                            sp.dma_start(dram_kv[bass.ds(rw.b, 1), bass.ds((t + 1) * P, P), 0:PKH - 1
                                                 ].rearrange("a n h d -> (a n) (h d)"),
                                         rw.kv_tile[:, 0:PKH - 1].rearrange("p h d -> p (h d)")).then_inc(tile_stored, 16)
                        if head or rw:
                            sp.wait_ge(tile_stored, 16 * ((1 if head else 0) + (2 if rw else 0)))

                    @block.scalar
                    def _(act):
                        if rw:
                            search.fetch(act)
                        if head:
                            head.run_scalar(act)
                        if rotary:
                            rhead.run_scalar(act)
                        if experts:
                            pair.run_scalar(act)
                        if rw:
                            search.exponentials(act)

                    @block.tensor
                    def _(pe):
                        if rw:
                            search.run_tensor(pe)
                            pe.wait_ge(search.sims, 2)
                        if head:
                            pe.wait_ge(head_in, 96)
                            head.run_tensor(pe)
                            if rotary or experts:
                                pe.wait_ge(head.normed, 1)
                        if rotary:
                            pe.wait_ge(r_head_in, 3)
                            rhead.run_tensor(pe)
                        if experts:
                            pair.run_tensor(pe)

                    @block.gpsimd
                    def _(pool):
                        if not rw:
                            return
                        pool.wait_ge(rows_named, 1)
                        for h in range(PKH):
                            if h:
                                pool.wait_ge(rows_used, h)
                            for k in range(TOPK):
                                nc.gpsimd.indirect_dma_start(
                                    out=rw.rows[:, h % 2, k, :], out_offset=None, in_=io["k_table"],
                                    in_offset=bass.IndirectOffsetOnAxis(ap=rw.gidx[:, h, k:k + 1], axis=0),
                                ).then_inc(rows_even if h % 2 == 0 else rows_odd, 16)
                        for s in (rows_even, rows_odd):
                            pool.wait_ge(s, 16 * TOPK * PKH // 2)
                        nc.gpsimd.dma_reset()

                    @block.vector
                    def _(dve):
                        def sum_rows(i, *what):
                            rw.sum_rows(dve, i, *what, acc_even, acc_odd, rows_used)

                        if rw:
                            nc.vector.tensor_copy(flat(rw.gidx), flat(search.gidf)).then_inc(rows_named, 1)
                            nc.vector.tensor_copy(rw.wlast[:], rw.wnow[:, PKH - 1, :]).then_inc(rows_named, 1)
                            dve.wait_ge(rows_named, 2)
                            nc.vector.tensor_copy(flat(rw.wnow), flat(search.wgt)).then_inc(rows_named, 1)
                            dve.wait_ge(rows_named, 3)
                            search.begin(dve)
                            sum_rows(0, rw.rows[:, 1], rw.wlast, rw.kv_last[:])
                        if head:
                            head.clear_row()
                        if rotary:
                            rhead.clear_row()
                            nc.vector.tensor_copy(rhead.q_h[:], q_all[:, :, of_head]).then_inc(r_head_in, 1)
                            nc.vector.tensor_copy(rhead.k_h[:], k_all[:, :, of_head]).then_inc(r_head_in, 1)
                            nc.vector.tensor_copy(rhead.v_h[:, :, 0:16], v_all[:, :, of_head]).then_inc(r_head_in, 1)
                        for h in range(PKH):
                            if rw and h in (0, 2):
                                search.half(h // 2)
                            if head:
                                if h < 2:
                                    head.max_tiles(dve, range(3) if h == 0 else range(3, NT))
                                if h == 1:
                                    head.row_of_max(dve)
                                if h == 3:
                                    head.normalize(dve, lambda t0, t1: y_h[:, t0:t1, :])
                            if rotary:
                                if h in (3, 4):
                                    rhead.max_tiles(dve, range(5) if h == 3 else range(5, NT))
                                if h == 4:
                                    rhead.row_of_max(dve)
                                if h == 6:
                                    rhead.normalize(dve, lambda t0, t1: y_tok[:, t0:t1, of_head])
                            if experts and h in (4, 6):
                                pair.hidden(dve, h - 4)
                            if rw and h == 4:
                                search.pairs()
                            if rw and h == 6:
                                search.rows_of((2,))
                            if experts and h in (4, 6):
                                pair.hidden(dve, h - 3)
                            if rw and h == 5:
                                search.top_pairs()
                            if experts and h in (5, 7):
                                pair.output(dve, (h - 5) // 2, e_first + (h - 5) // 2)
                            if rw:
                                if h >= 5:
                                    search.rows_of(((0, 1), (3,), (4, 5, 6, 7))[h - 5])
                                if h == 7:
                                    search.weights()
                                else:
                                    dve.wait_ge(rows_even if h % 2 == 0 else rows_odd, 16 * TOPK * (h // 2 + 1))
                                    sum_rows(h + 1, rw.rows[:, h % 2], rw.wnow[:, h], rw.kv_tile[:, h, :])
                ph.close_loop()

        def last_row(rw):
            with ph.phase("stood", "last_ix", "last_rows", "last_in", "last_out", "dve_step", "acc_even", "acc_odd",
                          "rows_used", "tile_stored") as (
                    block, stood, last_ix, last_rows, last_in, last_out, dve_step, acc_even, acc_odd,
                    rows_used, tile_stored):
                found = Search([None] * 7, search_buf)
                came = rw.rows[:, 0, 0, :]

                @block.tensor
                def _(pe):
                    nc.tensor.transpose(psum[:, B:B + 1], found.gidf[0:1].rearrange("p h k -> p (h k)"), ident[0:1, 0:1])
                    nc.tensor.transpose(psum[:, B + 1:B + 2], found.wgt[0:1].rearrange("p h k -> p (h k)"),
                                        ident[0:1, 0:1]).then_inc(stood, 1)
                    pe.wait_ge(last_ix, 2)
                    pe.wait_ge(last_rows, 16)
                    for h in range(PKH):
                        m = nc.tensor.matmul(psum[0:1, D + h * P:D + (h + 1) * P], rw.lastw[:, h:h + 1], came,
                                             start=True, stop=True)
                    m.then_inc(last_in, 1)

                @block.gpsimd
                def _(pool):
                    pool.wait_ge(last_ix, 1)
                    nc.gpsimd.indirect_dma_start(out=came, out_offset=None, in_=io["k_table"],
                                                 in_offset=bass.IndirectOffsetOnAxis(ap=rw.lastix[:, 0:1], axis=0),
                                                 ).then_inc(last_rows, 16)
                    pool.wait_ge(last_rows, 16)
                    nc.gpsimd.dma_reset()

                @block.vector
                def _(dve):
                    step = Steps(dve, dve_step)
                    dve.wait_ge(stood, 1)
                    nc.vector.tensor_copy(rw.lastix[:], psum[:, B:B + 1]).then_inc(last_ix, 1)
                    step(nc.vector.tensor_copy(rw.lastcol[:], psum[:, B + 1:B + 2]))
                    nc.vector.tensor_scalar(rw.lastw[:], headrow, rw.lastcol[:], None, ALU.mult).then_inc(last_ix, 1)
                    rw.sum_rows(dve, 0, rw.rows[:, 1], rw.wnow[:, PKH - 1], rw.kv_last[:], acc_even, acc_odd, rows_used)
                    dve.wait_ge(last_in, 1)
                    nc.vector.tensor_copy(rw.kv_tile[0:1].rearrange("p h d -> p (h d)"),
                                          psum[0:1, D:D + PKH * P]).then_inc(last_out, 1)

                @block.sync
                def _(sp):
                    sp.wait_ge(rows_used, 1)
                    sp.dma_start(dram_kv[bass.ds(rw.b, 1), FULL:P + FULL, PKH - 1].rearrange("a n d -> (a n) d"),
                                 rw.kv_last[:]).then_inc(tile_stored, 16)
                    sp.wait_ge(last_out, 1)
                    sp.dma_start(dram_kv[bass.ds(rw.b, 1), P + FULL:P + N_TOK].rearrange("a n h d -> (a n) (h d)"),
                                 rw.kv_tile[0:1].rearrange("p h d -> p (h d)")).then_inc(last_out, 16)
                    sp.wait_ge(last_out, 17)
                    sp.wait_ge(tile_stored, 16)

        def heads_out(b):
            with scratch("y_all", [P, NT, 512]) as y_all, scratch("yaT", [P, 4, NP]) as yaT:
                with ph.phase("y_in", "turned", "turned_out") as (block, y_in, turned, turned_out):
                    @block.sync
                    def _(sp):
                        sp.dma_start(y_all[:], dram_y[bass.ds(b, 1)].rearrange("a t p c -> p (a t) c")).then_inc(y_in, 16)

                    @block.tensor
                    def _(pe):
                        pe.wait_ge(y_in, 16)
                        for c in range(4):
                            if c >= 2:
                                pe.wait_ge(turned_out, c - 1)
                            turn_tiles(A if c % 2 == 0 else B, y_all[:, :, c * P:(c + 1) * P], P).then_inc(turned, 1)

                    @block.scalar
                    def _(act):
                        for c in range(4):
                            r = A if c % 2 == 0 else B
                            act.wait_ge(turned, c + 1)
                            nc.scalar.copy(yaT[:, c, :], psum[:, r:r + NP]).then_inc(turned_out, 1)
                project_add([yaT[:, c] for c in range(4)], [k_wo[:, c] for c in range(4)])

        def slices(b_search=None):
            layer_norm()
            with ExitStack() as c2:
                def b(name, shape):
                    return c2.enter_context(scratch(name, shape))
                t_tok = b("t_tok", [P, NT, C + 1])
                sw = b("sw", [P, NT, 8, C])
                swT = b("swT", [P, 4, NP])
                red = b("red", [P, NT, 2, 8])
                tokn = b("tokn", [P, 4, C])
                nrm = b("nrm", [P, 2, 4])
                tokT = b("tokT", [C, 512])
                qs, ks = b("qs", [8, 512]), b("ks", [8, 512])
                vs = b("vs", [C, 8, 8])
                att = b("att", [C, 8, C])
                attT = b("attT", [C, 8, C])
                ared = b("ared", [C, 2, 8])
                obd = b("obd", [P, 4, C])
                with ph.phase("t_in", "t_out", "logit", "scaled", "swept", "exped", "sw_out", "dve_step", "pool_step") as (
                        block, t_in, t_out, logit, scaled, swept, exped, sw_out, dve_step, pool_step):
                    @block.tensor
                    def _(pe):
                        columns(A, C, [(s_win, xT[:])]).then_inc(t_in, 1)
                        pe.wait_ge(t_out, 1)
                        for t in range(NT):
                            if t == 2:
                                for n in range(NT):
                                    o = psum[:, D + n * C:D + (n + 1) * C]
                                    last = nc.tensor.matmul(o, xT[:, n * P:(n + 1) * P], s_win, start=True, stop=True)
                                last.then_inc(t_in, 1)
                            if t >= 2:
                                pe.wait_ge(scaled, t - 1)
                            o = psum[:, B + (t % 2) * 512:B + (t % 2 + 1) * 512]
                            nc.tensor.matmul(o, yT[:, t * P:(t + 1) * P], s_slice[:], start=True, stop=True
                                             ).then_inc(logit, 1)

                    @block.scalar
                    def _(act):
                        act.wait_ge(t_in, 1)
                        nc.scalar.copy(yT[0:C, :], psum[0:C, A:A + NP]).then_inc(t_out, 1)
                        for t in range(NT):
                            act.wait_ge(swept, t + 1)
                            nc.scalar.activation(sw[:, t], sw[:, t], ACT.Exp).then_inc(exped, 1)

                    @block.vector
                    def _(dve):
                        step = Steps(dve, dve_step)

                        def finish(t):
                            dve.wait_ge(exped, t + 1)
                            step(nc.vector.tensor_reduce(red[:, t, 1], sw[:, t], AX.X, ALU.add))
                            nc.vector.reciprocal(red[:, t, 1], red[:, t, 1]).then_inc(sw_out, 1)
                        for t in range(NT):
                            dve.wait_ge(logit, t + 1)
                            o = psum[:, B + (t % 2) * 512:B + (t % 2 + 1) * 512].rearrange("p (h g) -> p h g", g=C)
                            nc.vector.tensor_tensor(sw[:, t], o, bc(s_rtemp[:], [P, 8, C], 2), ALU.mult).then_inc(scaled, 1)
                            dve.wait_ge(scaled, t + 1)
                            step(nc.vector.tensor_reduce(red[:, t, 0], sw[:, t], AX.X, ALU.max))
                            nc.vector.tensor_tensor(sw[:, t], sw[:, t], bc(red[:, t, 0], [P, 8, C], 2),
                                                    ALU.subtract).then_inc(swept, 1)
                            if t >= 1:
                                finish(t - 1)
                        finish(NT - 1)
                        dve.wait_ge(t_in, 2)
                        o = psum[:, D:D + NT * C].rearrange("p (t c) -> p t c", c=C)
                        nc.vector.tensor_tensor(t_tok[:, :, 0:C], o, bc(valid, [P, NT, C], 2), ALU.mult)
                        nc.vector.tensor_copy(t_tok[:, :, C], valid)

                    @block.gpsimd
                    def _(pool):
                        for t in range(NT):
                            pool.wait_ge(sw_out, t + 1)
                            nc.gpsimd.tensor_tensor(sw[:, t], sw[:, t], bc(red[:, t, 1], [P, 8, C], 2),
                                                    ALU.mult).then_inc(pool_step, 1)

                with ph.phase("sliced", "normed", "turned", "tokT_out", "qkv_in", "qkv_out", "sim", "shifted", "exped",
                              "att_out", "att_turned", "attT_out", "mixed", "cleared", "obd_out", "sw_turned",
                              "swT_out", "dve_step", *(SEARCH_SEMS if b_search is not None else ())) as (
                        block, sliced, normed, turned, tokT_out, qkv_in, qkv_out, sim, shifted, exped, att_out,
                        att_turned, attT_out, mixed, cleared, obd_out, sw_turned, swT_out, dve_step, *sems):
                    search = Search(sems, search_buf) if sems else None

                    def turn_weights(base, c):
                        turn_tiles(base, sw[:, :, 2 * c:2 * c + 2, :].rearrange("p t h g -> p t (h g)"), P
                                   ).then_inc(sw_turned, 1)

                    if search:
                        @block.sync
                        def _(sp):
                            search.load(sp, b_search, 0)

                    @block.tensor
                    def _(pe):
                        if search:
                            search.run_tensor(pe)
                        for c in range(4):
                            o = psum[:, A + c * 512:A + c * 512 + C + 1]
                            for t in range(NT):
                                last = nc.tensor.matmul(o, sw[:, t, 2 * c:2 * c + 2, :].rearrange("p h g -> p (h g)"),
                                                        t_tok[:, t, :], start=(t == 0), stop=(t == NT - 1))
                        last.then_inc(sliced, 1)
                        pe.wait_ge(normed, 1)
                        for c in range(4):
                            last = nc.tensor.transpose(psum[0:C, D + c * P:D + (c + 1) * P], tokn[:, c, :], ident)
                        last.then_inc(turned, 1)
                        pe.wait_ge(tokT_out, 1)
                        nc.tensor.matmul(psum[0:8, A:A + 512], s_qkvw[:, 0:8], tokT[:], start=True, stop=True)
                        nc.tensor.matmul(psum[0:8, A + 512:A + 1024], s_qkvw[:, 8:16], tokT[:], start=True, stop=True)
                        for h in range(8):
                            o = psum[0:C, A + 1024 + 8 * h:A + 1024 + 8 * h + 8]
                            nc.tensor.matmul(o, tokT[:, h * C:(h + 1) * C], s_qkvw[:, 16:24], start=True, stop=False)
                            last = nc.tensor.matmul(o, ones[0:1, 0:C], s_bv, start=False, stop=True)
                        last.then_inc(qkv_in, 1)
                        turn_weights(B, 0)
                        pe.wait_ge(qkv_out, 2)
                        if search:
                            pe.wait_ge(search.sims, 2)
                        for h in range(8):
                            last = nc.tensor.matmul(psum[0:C, F + h * C:F + (h + 1) * C], qs[:, h * C:(h + 1) * C],
                                                    ks[:, h * C:(h + 1) * C], start=True, stop=True)
                        last.then_inc(sim, 1)
                        turn_weights(A, 1)
                        pe.wait_ge(att_out, 1)
                        for h in range(8):
                            last = nc.tensor.transpose(psum[0:C, D + h * C:D + (h + 1) * C], att[:, h, :],
                                                       ident[0:C, 0:C])
                        last.then_inc(att_turned, 1)
                        pe.wait_ge(swT_out, 1)
                        turn_weights(B, 2)
                        pe.wait_ge(attT_out, 1)
                        for h in range(8):
                            last = nc.tensor.matmul(psum[0:C, F + 8 * h:F + 8 * h + 8], attT[:, h, :],
                                                    vs[:, h, :], start=True, stop=True)
                        last.then_inc(mixed, 1)
                        pe.wait_ge(swT_out, 2)
                        turn_weights(A, 3)
                        pe.wait_ge(swT_out, 4)
                        pe.wait_ge(obd_out, 1)
                        columns(B, C, [(obd[:, c, :], swT[:, c, :]) for c in range(4)]).then_inc(sw_turned, 1)

                    @block.scalar
                    def _(act):
                        def weights_out(c):
                            act.wait_ge(sw_turned, c + 1)
                            base = B if c % 2 == 0 else A
                            nc.scalar.copy(swT[:, c, :], psum[:, base:base + NP]).then_inc(swT_out, 1)

                        if search:
                            search.fetch(act)
                        act.wait_ge(turned, 1)
                        nc.scalar.copy(tokT[:], psum[0:C, D:D + 512]).then_inc(tokT_out, 1)
                        act.wait_ge(qkv_in, 1)
                        nc.scalar.activation(qs[:], psum[0:8, A:A + 512], ACT.Identity, bias=s_bq)
                        nc.scalar.activation(ks[:], psum[0:8, A + 512:A + 1024], ACT.Identity, bias=s_bk).then_inc(qkv_out, 1)
                        weights_out(0)
                        act.wait_ge(shifted, 1)
                        nc.scalar.activation(att[:], att[:], ACT.Exp, scale=8 ** -0.5).then_inc(exped, 1)
                        if search:
                            search.exponentials(act)
                        weights_out(1)
                        act.wait_ge(att_turned, 1)
                        nc.scalar.copy(attT[:].rearrange("p h g -> p (h g)"), psum[0:C, D:D + 512]).then_inc(attT_out, 1)
                        weights_out(2)
                        weights_out(3)
                        act.wait_ge(sw_turned, 5)
                        nc.scalar.copy(yT[0:C, :], psum[0:C, B:B + NP])

                    @block.vector
                    def _(dve):
                        step = Steps(dve, dve_step)
                        nc.vector.memset(obd[:], 0.0).then_inc(cleared, 1)
                        if search:
                            search.begin(dve)
                            search.half(0)
                            search.half(1)
                            search.pairs()
                        dve.wait_ge(sliced, 1)
                        sl = psum[:, A:A + 4 * 512].rearrange("p (c f) -> p c f", f=512)
                        step(nc.vector.tensor_scalar(nrm[:, 0], sl[:, :, C], 1e-5, None, ALU.add))
                        step(nc.vector.reciprocal(nrm[:, 1], nrm[:, 0]))
                        step(nc.vector.tensor_tensor(tokn[:], sl[:, :, 0:C], bc(nrm[:, 1], [P, 4, C], 2), ALU.mult))
                        nc.vector.tensor_tensor(tokn[:], tokn[:], ownhead, ALU.mult).then_inc(normed, 1)
                        if search:
                            search.top_pairs()
                            search.rows_of((0,))
                        dve.wait_ge(qkv_in, 1)
                        nc.vector.tensor_copy(vs[:].rearrange("p h d -> p (h d)"),
                                              psum[0:C, A + 1024:A + 1024 + 64]).then_inc(qkv_out, 1)
                        dve.wait_ge(sim, 1)
                        s = psum[0:C, F:F + 512].rearrange("p (h g) -> p h g", g=C)
                        step(nc.vector.tensor_reduce(ared[:, 0], s, AX.X, ALU.max))
                        nc.vector.tensor_tensor(att[:], s, bc(ared[:, 0], [C, 8, C], 2), ALU.subtract).then_inc(shifted, 1)
                        if search:
                            search.rows_of((1,))
                        dve.wait_ge(exped, 1)
                        step(nc.vector.tensor_reduce(ared[:, 0], att[:], AX.X, ALU.add))
                        step(nc.vector.reciprocal(ared[:, 1], ared[:, 0]))
                        nc.vector.tensor_tensor(att[:], att[:], bc(ared[:, 1], [C, 8, C], 2), ALU.mult).then_inc(att_out, 1)
                        if search:
                            search.rows_of((2, 3))
                        dve.wait_ge(mixed, 1)
                        dve.wait_ge(cleared, 1)
                        for h in range(8):
                            ins = nc.vector.tensor_copy(obd[64 * (h % 2):64 * (h % 2) + 64, h // 2, 8 * h:8 * h + 8],
                                                        psum[0:C, F + 8 * h:F + 8 * h + 8])
                        ins.then_inc(obd_out, 1)
                        if search:
                            search.rows_of((4, 5, 6, 7))
                            search.weights()
                project_add([yT], [s_wout])

        def moe():
            layer_norm()
            route(lambda t, o: nc.tensor.matmul(o, xT[:, t * P:(t + 1) * P], e_router, start=True, stop=True),
                  True, 0.0, 1e-12)
            with scratch("ehid", [P, 4, NP]) as ehid:
                with ph.phase("hid_in", "hid_out") as (block, hid_in, hid_out):
                    @block.tensor
                    def _(pe):
                        for c in range(4):
                            if c >= 2:
                                pe.wait_ge(hid_out, c - 1)
                            columns(A if c % 2 == 0 else B, P, [(e_w1[:, c * P:(c + 1) * P], xT[:])]).then_inc(hid_in, 1)

                    @block.scalar
                    def _(act):
                        for c in range(4):
                            r = A if c % 2 == 0 else B
                            act.wait_ge(hid_in, c + 1)
                            nc.scalar.activation(ehid[:, c, :], psum[:, r:r + NP], ACT.Gelu, bias=e_b1[:, c:c + 1]).then_inc(hid_out, 1)

                def products(t, o):
                    for c in range(4):
                        m = nc.tensor.matmul(o[:, c * P:(c + 1) * P], ehid[:, c, t * P:(t + 1) * P], e_w2[:, c, :],
                                             start=True, stop=True)
                    return m
                mix_experts(products, e_b2, extra=x_tok)

        def recurrence():
            layer_norm()
            with ph.phase("sum_in", "stepped", "turned") as (block, sum_in, stepped, turned):
                @block.tensor
                def _(pe):
                    columns(A, C, [(r_ih, xT[:]), (r_hh, hidden[:])]).then_inc(sum_in, 1)
                    pe.wait_ge(stepped, 1)
                    for t in range(NT):
                        last = nc.tensor.transpose(psum[:, B + t * C:B + (t + 1) * C], hidden[0:C, t * P:(t + 1) * P],
                                                   ident[0:C, 0:C])
                    last.then_inc(turned, 1)

                @block.scalar
                def _(act):
                    act.wait_ge(sum_in, 1)
                    nc.scalar.activation(hidden[0:C, :], psum[0:C, A:A + NP], ACT.Tanh, bias=r_bias[:]).then_inc(stepped, 1)

                @block.vector
                def _(dve):
                    dve.wait_ge(turned, 1)
                    nc.vector.tensor_tensor(flat(h_tok), flat(h_tok), psum[:, B:B + NT * C], ALU.add)

        def gated():
            layer_norm()
            with scratch("ghid", [P, 2, NP]) as ghid:
                with ph.phase("hid_in") as (block, hid_in):
                    @block.tensor
                    def _(pe):
                        for c in range(2):
                            columns(A if c == 0 else B, P, [(g_w1[:, c * P:(c + 1) * P], xT[:])]).then_inc(hid_in, 1)

                    @block.scalar
                    def _(act):
                        for c in range(2):
                            r = A if c == 0 else B
                            act.wait_ge(hid_in, c + 1)
                            nc.scalar.activation(ghid[:, c, :], psum[:, r:r + NP], ACT.Gelu, bias=g_b1[:, c:c + 1])

                def logit(t, o):
                    for c in range(2):
                        nc.tensor.matmul(o, ghid[:, c, t * P:(t + 1) * P], g_wg[:, c, :], start=(c == 0), stop=False)
                    return nc.tensor.matmul(o, ones[0:1, :], g_bg, start=False, stop=True)
                route(logit, False, 0.0, 0.0)

                def products(t, o):
                    for c in range(2):
                        m = nc.tensor.matmul(o, ghid[:, c, t * P:(t + 1) * P], g_wd[:, c, :], start=(c == 0), stop=(c == 1))
                    return m
                mix_experts(products, g_bd)

        def store(b):
            with ph.phase("stored") as (block, stored):
                @block.sync
                def _(sp):
                    ob = out[bass.ds(b, 1)].rearrange("a n c -> (a n) c")
                    sp.dma_start(ob[0:(NT - 1) * P].rearrange("(t p) c -> p t c", p=P), h_tok[:, 0:NT - 1, :]).then_inc(stored, 16)
                    sp.dma_start(ob[(NT - 1) * P:N_TOK], h_tok[0:N_TOK - (NT - 1) * P, NT - 1, :]).then_inc(stored, 16)
                    sp.wait_ge(stored, 32)

        def stage(front, middle, back):
            nonlocal h_tok
            with ExitStack() as c2:
                rw = Rows(middle) if middle is not None else None
                hbuf, heads = None, []
                if back is not None:
                    hbuf = head_buffers(c2, C) + [c2.enter_context(scratch("y_h", [P, NT, C]))]
                    heads = [(hbuf, C, C)]
                with ExitStack() as c3:
                    rotary = None
                    if front is not None:
                        r_buf = head_buffers(c3, 16, other=hbuf)
                        tokens(front, heads + [(r_buf, 16, 32)])
                        phasor()
                        rotary = [c3.enter_context(scratch(n, [P, NT, C])) for n in ("q_all", "k_all", "v_all")]
                        rotary_queries(*rotary)
                        rotary.append(r_buf)
                    elif heads:
                        with ph.phase("dve_step") as (block, dve_step):
                            @block.vector
                            def _(dve):
                                init_heads(dve, Steps(dve, dve_step), heads)
                    rounds(0, rw, back, hbuf, rotary=rotary)
                with ExitStack() as c3:
                    experts = None
                    if front is not None:
                        rotary_out()
                        experts = [c3.enter_context(scratch(n, shape)) for n, shape in (
                            ("w1", [P, 2 * HID0]), ("w3", [P, 2 * HID0]), ("w2", [HB, 4, C]), ("gate", [HB, NP]),
                            ("hid", [HB, 2, NP]), ("part", [P, NT, C]))]
                        with ph.phase("zeroed") as (block, zeroed):
                            @block.vector
                            def _(dve):
                                for w in experts[0:2]:
                                    nc.vector.memset(w[:], 0.0).then_inc(zeroed, 1)
                    rounds(4, rw, back, hbuf, experts=experts)
                if rw:
                    last_row(rw)
            if front is not None:
                with ph.phase("added") as (block, added):
                    @block.vector
                    def _(dve):
                        nc.vector.tensor_tensor(flat(h_tok), flat(h_tok), flat(x_tok), ALU.add).then_inc(added, 1)
                state_space()
                key_queries(front)
                if back is None:
                    first_search(front)
            if back is not None:
                h_tok = h_old
                heads_out(back)
                slices(front)
                moe()
                recurrence()
                gated()
                store(back)
                h_tok = h_new
            with ph.phase("moved") as (block, moved):
                @block.vector
                def _(dve):
                    if middle is not None:
                        nc.vector.tensor_copy(flat(h_old), flat(h_mid)).then_inc(moved, 1)
                        dve.wait_ge(moved, 1)
                    if front is not None:
                        nc.vector.tensor_copy(flat(h_mid), flat(h_new)).then_inc(moved, 1)

        n = n_batch
        with ph.phase("zeroed") as (block, zeroed):
            @block.vector
            def _(dve):
                nc.vector.memset(rows[:, 1], 0.0).then_inc(zeroed, 1)
                nc.vector.memset(wnow[:, PKH - 1, :], 0.0).then_inc(zeroed, 1)
        stage(0, None, None)
        stage(1, 0, None)
        if n > 2:
            with nc.Fori(2, n) as b:
                stage(b, b - 1, b - 2)
                ph.close_loop()
        stage(None, n - 1, n - 2)
        stage(None, None, n - 1)


def layouts(i):
    cat, T = np.concatenate, np.transpose
    col = lambda a: np.reshape(a, (-1, 1))
    row = lambda a: np.reshape(a, (1, -1))
    w = {k: np.asarray(v) for k, v in i.items()}
    g = lambda k: w[k]
    d = {
        "x": g("x"), "cls": col(g("cls_tok")),
        "t_w": T(g("L0_tok_W").reshape(C, 18, C), (1, 2, 0)),
        "a_w1p": cat([g("L0_attn_kp_w1").T, g("L0_attn_qp_w1").T], 1),
        "a_w1h": cat([g("L0_attn_kh_w1").T, g("L0_attn_qh_w1").T], 1),
        "a_b1p": col(cat([g("L0_attn_kp_b1"), g("L0_attn_qp_b1")])),
        "a_b1h": col(cat([g("L0_attn_kh_b1"), g("L0_attn_qh_b1")])),
        "a_b2": row(cat([g("L0_attn_kp_b2"), g("L0_attn_qp_b2"), g("L0_attn_kh_b2"), g("L0_attn_qh_b2")])),
        "a_w2p": np.stack([g("L0_attn_kp_w2").T, g("L0_attn_qp_w2").T]),
        "a_w2h": np.stack([g("L0_attn_kh_w2").T, g("L0_attn_qh_w2").T]),
        "a_vw": g("L0_attn_v_w").T, "a_vb": row(g("L0_attn_v_b")),
        "a_ow": g("L0_attn_out_w").T, "a_ob": row(g("L0_attn_out_b")),
        "a_g": g("L0_attn_ln_g"), "a_b": g("L0_attn_ln_b"),
        "f_ln1": g("L0_ffn_ln1_w"), "f_ln2": g("L0_ffn_ln2_w"),
        "f_qkv": cat([g("L0_ffn_wq").T, g("L0_ffn_wk").T, g("L0_ffn_wv").T], 1),
        "f_wo": g("L0_ffn_wo").T, "f_router": g("L0_ffn_router_w").T,
        "f_w1": T(g("L0_ffn_w1"), (2, 0, 1)).reshape(C, -1),
        "f_w3": T(g("L0_ffn_w3"), (2, 0, 1)).reshape(C, -1),
        "f_w2": T(T(g("L0_ffn_w2"), (0, 2, 1)).reshape(2 * NE, HB, C), (1, 0, 2)),
        "m_in": g("L1_attn_W_in"), "m_cw": g("L1_attn_conv_w").reshape(P, TAPS), "m_cb": col(g("L1_attn_conv_b")),
        "m_xp": g("L1_attn_W_xproj"), "m_wdt": col(g("L1_attn_w_dt")), "m_bdt": col(g("L1_attn_b_dt")),
        "m_A": g("L1_attn_A"), "m_D": col(g("L1_attn_D")), "m_out": g("L1_attn_W_out"),
        "k_wqpk": g("L1_ffn_Wq_pk"), "k_wq": g("L1_ffn_Wq"),
        "k_keys": T(g("L1_ffn_pk_keys"), (0, 2, 3, 1)).reshape(4, 4, 32, PKK),
        "k_table": cat([g("L1_ffn_keys_table"), g("L1_ffn_values_table")], 1),
        "k_wo": T(g("L1_ffn_Wo").reshape(4, P, C), (1, 0, 2)),
        "s_win": g("L2_attn_W_in"), "s_bin": row(g("L2_attn_b_in")),
        "s_wslice": g("L2_attn_W_slice"), "s_bslice": row(np.tile(g("L2_attn_b_slice"), 8)),
        "s_temp": g("L2_attn_temperature").reshape(8),
        "s_qkvw": np.tile(cat([g("L2_attn_W_q"), g("L2_attn_W_k"), g("L2_attn_W_v")], 1), (8, 1)),
        "s_bq": col(g("L2_attn_b_q")), "s_bk": col(g("L2_attn_b_k")), "s_bv": row(g("L2_attn_b_v")),
        "s_wout": g("L2_attn_W_out"), "s_bout": row(g("L2_attn_b_out")),
        "e_router": g("L2_ffn_router_w").T, "e_w1": T(g("L2_ffn_w1"), (1, 0, 2)).reshape(C, 512),
        "e_b1": T(g("L2_ffn_b1").reshape(4, P)), "e_w2": g("L2_ffn_w2"), "e_b2": g("L2_ffn_b2").reshape(-1),
        "r_ih": g("L3_attn_W_ih").T, "r_hh": g("L3_attn_W_hh").T,
        "r_b": np.stack([g("L3_attn_b_ih"), g("L3_attn_b_hh")], 1),
        "g_w1": g("L3_ffn_W1"), "g_b1": T(g("L3_ffn_b1").reshape(2, P)),
        "g_wg": T(g("L3_ffn_Wg").reshape(2, P, NE), (1, 0, 2)), "g_bg": row(g("L3_ffn_bg")),
        "g_wd": T(T(g("L3_ffn_Wd"), (1, 0, 2)).reshape(2, P, 512), (1, 0, 2)), "g_bd": g("L3_ffn_bd").reshape(-1),
    }
    d = {k: np.ascontiguousarray(v) for k, v in d.items()}
    for k, v in constants().items():
        d[k] = np.ascontiguousarray(v, dtype=np.float32)
    return d


def kernel(**inputs):
    import concourse.bacc as bacc
    from concourse.bass_utils import run_bass_kernel_spmd

    nc = bacc.Bacc("TRN2", target_bir_lowering=False, num_devices=1)
    arrays, io = {}, {}
    for name, a in layouts(inputs).items():
        arrays["in_" + name] = a
        io[name] = nc.dram_tensor("in_" + name, a.shape, mybir.dt.from_np(a.dtype), kind="ExternalInput").ap()
    out = nc.dram_tensor("out_0", (N_BATCH, N_TOK, C), F32, kind="ExternalOutput").ap()
    build(nc, io, out)
    r = run_bass_kernel_spmd(nc, [arrays], core_ids=[0])
    return r.results[0]["out_0"]
```
